# Optimizing a Trainium2 kernel written in Bass

```python
import numpy as np
import jax
import jax.numpy as jnp

def _softmax(x, axis=-1):
    return jax.nn.softmax(x, axis=axis)

def _gelu(x):
    return jax.nn.gelu(x, approximate=True)

def _silu(x):
    return jax.nn.silu(x)

def _sigmoid(x):
    return jax.nn.sigmoid(x)

def _layernorm(x, axis=-1, eps=1e-05):
    m = jnp.mean(x, axis=axis, keepdims=True)
    v = jnp.var(x, axis=axis, keepdims=True)
    return (x - m) / jnp.sqrt(v + eps)

def _scatter_add(tgt, idx, src, axis=0):
    return tgt.at[idx].add(src)

def _segment_sum(src, seg, n):
    return jax.ops.segment_sum(src, seg, n)
kernel_name = 'mk_gnn_resnorm_d2_gnn_r8_5201cb'

def setup_inputs(seed: int=0):
    np.random.seed(seed)
    _w = jnp.asarray

    def _rec_inputs():
        import jax
        import jax.numpy as jnp
        _gk = jax.random.key(seed)
        x = -0.0009044 + 1 * jax.random.normal(jax.random.fold_in(_gk, 1), (12500, 32), jnp.float32)
        src = jax.random.randint(jax.random.fold_in(_gk, 2), (200000,), 0, 12500, jnp.int32)
        dst = jnp.minimum((12500 * jax.random.uniform(jax.random.fold_in(_gk, 3), (200000,)) ** 2.0).astype(jnp.int32), 99999)
        _o = jnp.argsort(dst, stable=True)
        src = src[_o]
        dst = dst[_o]
        edge_attr_10 = jax.random.uniform(jax.random.fold_in(_gk, 12), (200000, 10), jnp.float32, 0.0, 1)
        edge_attr_3 = 0.00109039 + 0.999626 * jax.random.normal(jax.random.fold_in(_gk, 13), (200000, 3), jnp.float32)
        edge_weight = jax.random.uniform(jax.random.fold_in(_gk, 14), (200000,), jnp.float32, 0.0, 0.999997)
        return (x, src, dst, edge_attr_10, edge_attr_3, edge_weight)
    x, src, dst, edge_attr_10, edge_attr_3, edge_weight = _rec_inputs()

    def _L0_gnn_setup():
        import jax, jax.numpy as jnp
        import numpy as np
        MUL = 16
        MOUT = 8
        TANH_GAIN = 1.593
        INV_SQRT3 = 0.5773502691896258
        PW_S = 0.17677669529663687
        PW_V = 0.25

        def _w3j_121():
            s2, s6 = (2 ** 0.5, 6 ** 0.5)
            M = np.zeros((5, 3, 3))
            M[0, 0, 1] = M[0, 1, 0] = 1 / s2
            M[1, 1, 2] = M[1, 2, 1] = 1 / s2
            M[2] = np.diag([-1.0, -1.0, 2.0]) / s6
            M[3, 0, 2] = M[3, 2, 0] = 1 / s2
            M[4] = np.diag([1.0, -1.0, 0.0]) / s2
            return jnp.asarray(np.transpose(M, (1, 0, 2)) / 5 ** 0.5, jnp.float32)
        W3J121 = _w3j_121()

        def _sph(edge_vec):
            n = edge_vec / jnp.linalg.norm(edge_vec, axis=1, keepdims=True)
            x, y, z = (n[:, 0], n[:, 1], n[:, 2])
            y1 = 3.0 ** 0.5 * n
            s15 = 15.0 ** 0.5
            y2 = jnp.stack([s15 * x * y, s15 * y * z, 5.0 ** 0.5 / 2 * (3 * z * z - 1), s15 * x * z, s15 / 2 * (x * x - y * y)], axis=1)
            return (y1, y2)

        def _forward(x, edge_src, edge_dst, edge_vec, emb, norm, W1, W2):
            N, E = (x.shape[0], edge_src.shape[0])
            xs = jnp.concatenate([x[edge_src, :8], x[edge_dst, :8]], axis=1)
            xv = jnp.concatenate([x[edge_src, 8:].reshape(E, 8, 3), x[edge_dst, 8:].reshape(E, 8, 3)], axis=1)
            y1, y2 = _sph(edge_vec)
            h = 2.0 ** 0.5 * jax.nn.relu(emb @ W1 / 10.0 ** 0.5)
            w = (h @ W2 / 16.0 ** 0.5).reshape(E, 7, MUL, MOUT)
            wa_s, wb_s, wa_g, wb_g, wc, wd, we = [w[:, i] for i in range(7)]
            s_out = PW_S * (jnp.einsum('eu,euw->ew', xs, wa_s) + INV_SQRT3 * jnp.einsum('eui,ei,euw->ew', xv, y1, wb_s))
            g_out = PW_S * (jnp.einsum('eu,euw->ew', xs, wa_g) + INV_SQRT3 * jnp.einsum('eui,ei,euw->ew', xv, y1, wb_g))
            v_out = PW_V * (INV_SQRT3 * jnp.einsum('eu,ek,euw->ewk', xs, y1, wc) + INV_SQRT3 * jnp.einsum('eui,euw->ewi', xv, wd) + jnp.einsum('eui,ea,iak,euw->ewk', xv, y2, W3J121, we))
            s_act = TANH_GAIN * jnp.tanh(s_out)
            gates = TANH_GAIN * jnp.tanh(g_out)
            edge_ftr = jnp.concatenate([s_act, (gates[:, :, None] * v_out).reshape(E, 24)], axis=1) * norm[:, None]
            return jax.ops.segment_sum(edge_ftr, edge_dst, num_segments=N)
        key = jax.random.key(seed)
        ks = jax.random.split(key, 8)
        N, E = (6250, 37500)
        return {'x': jax.random.normal(ks[0], (N, 32), jnp.float32), 'edge_src': jax.random.randint(ks[1], (E,), 0, N), 'edge_dst': jax.random.randint(ks[2], (E,), 0, N), 'edge_vec': jax.random.normal(ks[3], (E, 3), jnp.float32), 'emb': jax.random.uniform(ks[4], (E, 10), jnp.float32), 'norm': jax.random.uniform(ks[5], (E,), jnp.float32), 'W1': jax.random.normal(ks[6], (10, 16), jnp.float32), 'W2': jax.random.normal(ks[7], (16, 896), jnp.float32)}
    _L0_gnn_all = _L0_gnn_setup()
    _L0_gnn_in = {k: v for k, v in _L0_gnn_all.items() if k in ('W1', 'W2')}
    del _L0_gnn_all

    def _L1_gnn_setup():
        import jax, jax.numpy as jnp
        import numpy as np
        N_NODES = 12500
        N_EDGES = 200000
        DIM1 = 32
        LEAKY_SLOPE = 0.01
        key = jax.random.key(seed)
        k1, k2, k3, k4 = jax.random.split(key, 4)
        h = jax.random.normal(k1, (N_NODES, DIM1), dtype=jnp.float32)
        attn_w = jax.random.normal(k2, (2 * DIM1,), dtype=jnp.float32) * (1.0 / np.sqrt(2 * DIM1))
        src = jax.random.randint(k3, (N_EDGES,), 0, N_NODES, dtype=jnp.int32)
        dst = jax.random.randint(k4, (N_EDGES,), 0, N_NODES, dtype=jnp.int32)
        return {'h': h, 'attn_w': attn_w, 'src': src, 'dst': dst}
    _L1_gnn_all = _L1_gnn_setup()
    _L1_gnn_in = {k: v for k, v in _L1_gnn_all.items() if k in ('attn_w',)}
    del _L1_gnn_all
    return {'x': x, 'src': src, 'dst': dst, 'edge_attr_10': edge_attr_10, 'edge_attr_3': edge_attr_3, 'edge_weight': edge_weight, 'L0_gnn_W1': _L0_gnn_in['W1'], 'L0_gnn_W2': _L0_gnn_in['W2'], 'L1_gnn_attn_w': _L1_gnn_in['attn_w']}

def reference(x, src, dst, edge_attr_10, edge_attr_3, edge_weight, L0_gnn_W1, L0_gnn_W2, L1_gnn_attn_w):
    import jax
    import jax.numpy as jnp

    def _L0_gnn_ref(x, edge_src, edge_dst, edge_vec, emb, norm, W1, W2):
        import jax, jax.numpy as jnp
        import numpy as np
        MUL = 16
        MOUT = 8
        TANH_GAIN = 1.593
        INV_SQRT3 = 0.5773502691896258
        PW_S = 0.17677669529663687
        PW_V = 0.25

        def _w3j_121():
            s2, s6 = (2 ** 0.5, 6 ** 0.5)
            M = np.zeros((5, 3, 3))
            M[0, 0, 1] = M[0, 1, 0] = 1 / s2
            M[1, 1, 2] = M[1, 2, 1] = 1 / s2
            M[2] = np.diag([-1.0, -1.0, 2.0]) / s6
            M[3, 0, 2] = M[3, 2, 0] = 1 / s2
            M[4] = np.diag([1.0, -1.0, 0.0]) / s2
            return jnp.asarray(np.transpose(M, (1, 0, 2)) / 5 ** 0.5, jnp.float32)
        W3J121 = _w3j_121()

        def _sph(edge_vec):
            n = edge_vec / jnp.linalg.norm(edge_vec, axis=1, keepdims=True)
            x, y, z = (n[:, 0], n[:, 1], n[:, 2])
            y1 = 3.0 ** 0.5 * n
            s15 = 15.0 ** 0.5
            y2 = jnp.stack([s15 * x * y, s15 * y * z, 5.0 ** 0.5 / 2 * (3 * z * z - 1), s15 * x * z, s15 / 2 * (x * x - y * y)], axis=1)
            return (y1, y2)

        def _forward(x, edge_src, edge_dst, edge_vec, emb, norm, W1, W2):
            N, E = (x.shape[0], edge_src.shape[0])
            xs = jnp.concatenate([x[edge_src, :8], x[edge_dst, :8]], axis=1)
            xv = jnp.concatenate([x[edge_src, 8:].reshape(E, 8, 3), x[edge_dst, 8:].reshape(E, 8, 3)], axis=1)
            y1, y2 = _sph(edge_vec)
            h = 2.0 ** 0.5 * jax.nn.relu(emb @ W1 / 10.0 ** 0.5)
            w = (h @ W2 / 16.0 ** 0.5).reshape(E, 7, MUL, MOUT)
            wa_s, wb_s, wa_g, wb_g, wc, wd, we = [w[:, i] for i in range(7)]
            s_out = PW_S * (jnp.einsum('eu,euw->ew', xs, wa_s) + INV_SQRT3 * jnp.einsum('eui,ei,euw->ew', xv, y1, wb_s))
            g_out = PW_S * (jnp.einsum('eu,euw->ew', xs, wa_g) + INV_SQRT3 * jnp.einsum('eui,ei,euw->ew', xv, y1, wb_g))
            v_out = PW_V * (INV_SQRT3 * jnp.einsum('eu,ek,euw->ewk', xs, y1, wc) + INV_SQRT3 * jnp.einsum('eui,euw->ewi', xv, wd) + jnp.einsum('eui,ea,iak,euw->ewk', xv, y2, W3J121, we))
            s_act = TANH_GAIN * jnp.tanh(s_out)
            gates = TANH_GAIN * jnp.tanh(g_out)
            edge_ftr = jnp.concatenate([s_act, (gates[:, :, None] * v_out).reshape(E, 24)], axis=1) * norm[:, None]
            return jax.ops.segment_sum(edge_ftr, edge_dst, num_segments=N)
        return _forward(x, edge_src, edge_dst, edge_vec, emb, norm, W1, W2)

    def _L1_gnn_ref(h, attn_w, src, dst):
        import jax, jax.numpy as jnp
        import numpy as np
        N_NODES = 12500
        N_EDGES = 200000
        DIM1 = 32
        LEAKY_SLOPE = 0.01
        N, d = h.shape
        s_src = h @ attn_w[:d]
        s_dst = h @ attn_w[d:]
        e = s_src[src] + s_dst[dst]
        e = jnp.where(e >= 0, e, LEAKY_SLOPE * e)
        m = jax.ops.segment_max(e, dst, num_segments=N)
        ex = jnp.exp(e - m[dst])
        denom = jax.ops.segment_sum(ex, dst, num_segments=N)
        alpha = ex / denom[dst]
        out = jax.ops.segment_sum(h[src] * alpha[:, None], dst, num_segments=N)
        return out
    x = _layernorm(x + _L0_gnn_ref(x, src, dst, edge_attr_3, edge_attr_10, edge_weight, L0_gnn_W1, L0_gnn_W2), axis=-1)
    x = _layernorm(x + _L1_gnn_ref(x, L1_gnn_attn_w, src, dst), axis=-1)
    return x

_drawn_inputs = setup_inputs


def setup_inputs(seed=0):
    import zlib

    import numpy as np

    out = dict(_drawn_inputs(seed))
    spreads = {}
    factors = {}
    for name, (base, spread) in spreads.items():
        noise = np.random.default_rng([zlib.crc32(name.encode()), seed]).standard_normal(out[name].shape)
        drawn = base * np.exp(spread * noise) if base else spread * noise
        out[name] = jnp.asarray(drawn.astype(out[name].dtype))
    for name, factor in factors.items():
        out[name] = (out[name] * factor).astype(out[name].dtype)
    return out
```

```python
import concourse.bass as bass
from concourse import mybir
from contextlib import ExitStack


def gnn_resnorm_kernel(nc, x, src, dst, emb, vec, weight, W1, W2, attn, out):
    f32 = mybir.dt.float32
    i32 = mybir.dt.int32
    ALU = mybir.AluOpType
    ACT = mybir.ActivationFunctionType
    AX = mybir.AxisListType

    N, DIM = x.shape
    E = src.shape[0]
    NEMB, HID = W1.shape
    P = 125
    EP = E // P
    NP = N // P
    assert P * EP == E and P * NP == N
    C = 40
    PAIRS = EP // (2 * C)
    GT = 4
    GW = GT * P
    GC = C // GT
    G2 = 2 * GC
    MO = 8
    NBLK = 6
    QF = 80
    FW = QF + NEMB
    OW = NBLK * MO
    SB = 500
    NSB = E // SB
    ZROW = E + 200
    PAD = 256
    R1 = DIM + 2
    BIG = 3.0e38
    EPS = 1e-5
    TG = 1.593
    PW_S, PW_V, INV3 = 0.17677669529663687, 0.25, 0.5773502691896258
    KS = PW_S / HID ** 0.5
    KV = PW_V / HID ** 0.5
    C121 = 1.5 ** 0.5

    def edges(ap, width):
        return ap.rearrange("(p c) f -> p c f", c=EP) if width > 1 else ap.rearrange("(p c) -> p c", c=EP)

    ctx = ExitStack()
    with ctx:
        def sb(name, shape, dt=f32):
            return ctx.enter_context(nc.sbuf_tensor(name, shape, dt))

        def sem(name):
            return ctx.enter_context(nc.semaphore(name))

        def dram(name, shape, dt=f32):
            return nc.dram_tensor(name, shape, dt, kind="Internal").ap()

        dstf_d = dram("dstf_d", (NSB, SB))
        samp_d = dram("samp_d", (NSB,))
        end_d = dram("end_d", (N + 1, 1))
        xd_d = dram("xd_d", (E, DIM))
        sd_d = dram("sd_d", (E, 1))
        dir_d = dram("dir_d", (E, 3))
        keep_d = dram("keep_d", (E,))
        y0_d = dram("y0_d", (E + PAD, DIM))
        y1_d = dram("y1_d", (E + PAD, R1))
        tab_d = dram("tab_d", (N, DIM + 1))
        sdt_d = dram("sdt_d", (N, 1))

        ident = sb("ident", [128, 128])
        ones = sb("ones", [128, 128])
        zeros = sb("zeros", [P, 3200])
        wh = sb("wh", [FW, 128])
        wst = sb("wst", [FW, NBLK * 128])
        red = sb("red", [128, NBLK * OW])
        attn_b = sb("attn_b", [P, 2 * DIM])

        xn = sb("xn", [P, NP * DIM])
        endf = sb("endf", [P, NP])
        startf = sb("startf", [P, NP])
        empty = sb("empty", [P, NP])
        first_i = sb("first_i", [P, NP], i32)
        last_i = sb("last_i", [P, NP], i32)
        head_i = sb("head_i", [P, 1], i32)
        fix_i = sb("fix_i", [P, 1], i32)
        headf = sb("headf", [P, 1])
        tailf = sb("tailf", [P, 1])
        hx_keep = sb("hx_keep", [P, DIM])
        tail1 = sb("tail1", [P, R1])
        hsd = sb("hsd", [P, 1])
        link = sb("link", [P, P])
        linkT = sb("linkT", [P, P])

        banks = [ctx.enter_context(nc.psum_tensor(f"bank{i}", [128, 512], f32)) for i in range(8)]
        T_ps = banks[0:2]
        H_ps = banks[2]
        G_ps = banks[3:6]
        R_ps = banks[6]
        Y_ps = banks[7]

        all_sems = {}

        def S(name):
            if name not in all_sems:
                all_sems[name] = sem(name)
            return all_sems[name]

        with ExitStack() as st:
            def sbt(name, shape, dt=f32):
                return st.enter_context(nc.sbuf_tensor(name, shape, dt))

            dst_i = sbt("dst_i", [P, EP], i32)
            dstf = sbt("dstf", [P, EP + 1])
            prev_i = sbt("prev_i", [P, 1], i32)
            keep = sbt("keep", [P, EP])
            dirv = sbt("dirv", [P, EP * 3])
            sq = sbt("sq", [P, EP * 3])
            s2 = sbt("s2", [P, EP])
            rn = sbt("rn", [P, EP])
            samp_b = sbt("samp_b", [P, NSB])
            node_i = sbt("node_i", [P, NP], i32)
            nodef = sbt("nodef", [P, NP])
            NF = 4
            junk = sbt("junk", [P, NF * SB], mybir.dt.bfloat16)
            cnt = sbt("cnt", [P, NP])
            blk_i = sbt("blk_i", [P, NP], i32)
            fine = sbt("fine", [P, NP])
            blkbuf = sbt("blkbuf", [P, NF * SB])
            w2s = sbt("w2s", [HID, 7 * 128])
            w2x = sbt("w2x", [HID, NBLK * MO * FW])
            wr = sbt("wr", [HID, 128])
            head_row = sbt("head_row", [P, P])
            diag = sbt("diag", [P, P])
            part_i = sbt("part_i", [P, 1], i32)
            partf = sbt("partf", [P, 1])
            endh = sbt("endh", [P, 1])
            idx1 = sbt("idx1", [P, 1], i32)
            t1 = sbt("t1", [P, 4])
            tn = sbt("tn", [P, 4 * NP])

            with nc.Block() as block:
                @block.sync
                def _(sp):
                    sp.dma_start(dst_i[:, :], edges(dst, 1)).then_inc(S("a_dst"), 16)
                    sp.wait_ge(S("a_prev0"), 1)
                    sp.dma_start(prev_i[1:P, :], dst.rearrange("(p c) -> p c", c=EP)[0:P - 1, EP - 1:EP], allow_slow_non_contiguous=True).then_inc(S("a_prev"), 16)
                    sp.dma_start(dirv[:, :], vec.rearrange("(p c) f -> p (c f)", c=EP)).then_inc(S("a_vec"), 16)
                    sp.dma_start(xn[:, :], x.rearrange("(p k) f -> p (k f)", k=NP)).then_inc(S("a_x"), 16)
                    sp.dma_start(w2s[:, :], W2).then_inc(S("a_w"), 16)
                    sp.dma_start(attn_b[:, :], attn.rearrange("(a f) -> a f", a=1).broadcast_to([P, 2 * DIM])).then_inc(S("a_w"), 16)
                    sp.wait_ge(S("a_wh0"), 1)
                    for w in range(MO):
                        sp.dma_start(wh[QF:FW, w * HID:(w + 1) * HID], W1).then_inc(S("a_w1"), 16)
                    sp.wait_ge(S("a_dstf"), 1)
                    sp.dma_start(dstf_d.rearrange("a b -> (a b)").rearrange("(p c) -> p c", c=EP), dstf[:, 1:]).then_inc(S("a_dstd"), 16)
                    sp.wait_ge(S("a_dstd"), 16)
                    sp.dma_start(samp_d.rearrange("(a b) -> a b", b=1), dstf_d[:, 0:1], allow_slow_non_contiguous=True).then_inc(S("a_samp"), 16)
                    sp.wait_ge(S("a_samp"), 16)
                    sp.dma_start(samp_b[:, :], samp_d.rearrange("(a b) -> a b", a=1).broadcast_to([P, NSB])).then_inc(S("a_sampb"), 16)
                    sp.wait_ge(S("a_zero"), 1)
                    for i in range(EP * DIM // 3200):
                        sp.dma_start(xd_d.rearrange("(p c) f -> p (c f)", c=EP)[:, i * 3200:(i + 1) * 3200], zeros[:, :]).then_inc(S("a_xd0"), 16)
                    sp.dma_start(sd_d.rearrange("(p c) a -> p (c a)", c=EP), zeros[:, 0:EP]).then_inc(S("a_xd0"), 16)
                    sp.dma_start(y0_d[E:E + PAD, :].rearrange("(a b) f -> a (b f)", a=64), zeros[0:64, 0:4 * DIM]).then_inc(S("a_pad"), 16)
                    sp.dma_start(y1_d[E:E + PAD, :].rearrange("(a b) f -> a (b f)", a=64), zeros[0:64, 0:4 * R1]).then_inc(S("a_pad"), 16)
                    sp.dma_start(end_d[0:1, :], zeros[0:1, 0:1]).then_inc(S("a_end"), 16)
                    sp.wait_ge(S("a_endf"), 1)
                    sp.dma_start(end_d[1:N + 1, :].rearrange("(p k) a -> p (k a)", k=NP), endf[:, :]).then_inc(S("a_end"), 16)
                    sp.wait_ge(S("a_end"), 32)
                    sp.dma_start(startf[:, :], end_d[0:N, :].rearrange("(p k) a -> p (k a)", k=NP)).then_inc(S("a_start"), 16)
                    sp.wait_ge(S("a_keep"), 1)
                    sp.dma_start(keep_d.rearrange("(p c) -> p c", c=EP), keep[:, :]).then_inc(S("a_out"), 16)
                    sp.wait_ge(S("a_dir"), 1)
                    sp.dma_start(dir_d.rearrange("(p c) f -> p (c f)", c=EP), dirv[:, :]).then_inc(S("a_out"), 16)
                    sp.wait_ge(S("a_out"), 32)
                    sp.wait_ge(S("a_pad"), 32)

                @block.gpsimd
                def _(pool):
                    nc.gpsimd.memset(prev_i[:, :], -1).then_inc(S("a_prev0"), 1)
                    nc.gpsimd.memset(ones[:, :], 1.0).then_inc(S("a_ones"), 1)
                    nc.gpsimd.memset(ident[:, :], 0.0).then_inc(S("a_id"), 1)
                    pool.wait_ge(S("a_id"), 1)
                    nc.gpsimd.affine_select(out=ident[:, :], in_=ident[:, :], compare_op=ALU.not_equal, fill=1.0, base=0,
                                            pattern=[[-1, 128]], channel_multiplier=1).then_inc(S("a_id"), 1)
                    nc.gpsimd.iota(node_i[:, :], [[1, NP]], base=0, channel_multiplier=NP).then_inc(S("a_iota"), 1)
                    nc.gpsimd.iota(part_i[:, :], [[0, 1]], base=0, channel_multiplier=1).then_inc(S("a_iota"), 1)
                    nc.gpsimd.memset(red[:, :], 0.0).then_inc(S("a_red"), 1)
                    pool.wait_ge(S("a_red"), 1)
                    nc.gpsimd.memset(wh[:, :], 0.0).then_inc(S("a_wh0"), 1)
                    for b in range(NBLK):
                        blk = red[:, b * OW + b * MO:b * OW + (b + 1) * MO]
                        nc.gpsimd.memset(blk, 1.0).then_inc(S("a_red"), 1)
                        pool.wait_ge(S("a_red"), 3 * b + 2)
                        nc.gpsimd.affine_select(out=blk, in_=blk, compare_op=ALU.is_ge, fill=0.0, base=0,
                                                pattern=[[-HID, MO]], channel_multiplier=1).then_inc(S("a_red"), 1)
                        pool.wait_ge(S("a_red"), 3 * b + 3)
                        nc.gpsimd.affine_select(out=blk, in_=blk, compare_op=ALU.is_ge, fill=0.0, base=HID - 1,
                                                pattern=[[HID, MO]], channel_multiplier=-1).then_inc(S("a_red"), 1)
                    pool.wait_ge(S("a_head"), 1)
                    pool.wait_ge(S("a_blk"), 1)
                    for k in range(NP):
                        if k >= NF:
                            pool.wait_ge(S("a_fine"), k - NF + 1)
                        nc.gpsimd.indirect_dma_start(out=blkbuf[:, (k % NF) * SB:(k % NF + 1) * SB], out_offset=None, in_=dstf_d,
                                                     in_offset=bass.IndirectOffsetOnAxis(blk_i[:, k:k + 1], 0)).then_inc(S(f"a_fg{k % NF}"), 16)
                    pool.wait_ge(S("a_idx"), 1)
                    pool.wait_ge(S("a_x"), 16)
                    pool.wait_ge(S("a_xd0"), 16 * (EP * DIM // 3200 + 1))
                    for k in range(NP):
                        nc.gpsimd.indirect_dma_start(out=xd_d, out_offset=bass.IndirectOffsetOnAxis(first_i[:, k:k + 1], 0),
                                                     in_=xn[:, k * DIM:(k + 1) * DIM], in_offset=None,
                                                     bounds_check=E - 1, oob_is_err=False).then_inc(S("a_xd"), 16)
                    pool.wait_ge(S("a_idx1"), 1)
                    nc.gpsimd.indirect_dma_start(out=endh[:, :], out_offset=None, in_=end_d,
                                                 in_offset=bass.IndirectOffsetOnAxis(idx1[:, :], 0)).then_inc(S("a_endh"), 16)
                    nc.gpsimd.indirect_dma_start(out=hx_keep[:, :], out_offset=None, in_=x,
                                                 in_offset=bass.IndirectOffsetOnAxis(head_i[:, :], 0)).then_inc(S("a_hx"), 16)
                    pool.wait_ge(S("a_xd"), 16 * NP)
                    pool.wait_ge(S("a_hx"), 16)
                    pool.wait_ge(S("a_link0"), 2)
                    nc.gpsimd.affine_select(out=link[:, :], in_=link[:, :], compare_op=ALU.is_gt, fill=0.0, base=0,
                                            pattern=[[1, P]], channel_multiplier=-1).then_inc(S("a_link"), 1)
                    pool.wait_ge(S("a_link"), 1)

                @block.vector
                def _(dve):
                    n = [0]

                    def step(ins):
                        n[0] += 1
                        ins.then_inc(S("a_dve"), 1)
                        dve.wait_ge(S("a_dve"), n[0])

                    V = nc.vector
                    V.memset(zeros[:, :], 0.0).then_inc(S("a_zero"), 1)
                    dve.wait_ge(S("a_dst"), 16)
                    V.tensor_copy(dstf[:, 1:], dst_i[:, :]).then_inc(S("a_dstf"), 1)
                    dve.wait_ge(S("a_prev"), 16)
                    step(V.tensor_copy(dstf[:, 0:1], prev_i[:, :]))
                    dve.wait_ge(S("a_dstf"), 1)
                    V.tensor_tensor(keep[:, :], dstf[:, 1:], dstf[:, 0:EP], ALU.is_equal).then_inc(S("a_keep"), 1)
                    V.tensor_copy(headf[:, :], dstf[:, 1:2])
                    V.tensor_copy(tailf[:, :], dstf[:, EP:EP + 1])
                    V.tensor_copy(head_i[:, :], dst_i[:, 0:1])
                    step(V.tensor_scalar(idx1[:, :], dstf[:, 1:2], 1.0, None, ALU.add))
                    V.memset(w2x[:, :], 0.0).then_inc(S("a_head"), 1)
                    dve.wait_ge(S("a_iota"), 2)
                    V.tensor_copy(partf[:, :], part_i[:, :])
                    step(V.tensor_copy(nodef[:, :], node_i[:, :]))
                    dve.wait_ge(S("a_sampb"), 16)
                    for k in range(NP):
                        if k >= NF:
                            dve.wait_ge(S("a_coarse"), k - NF + 1)
                        V.tensor_scalar(junk[:, (k % NF) * SB:(k % NF) * SB + NSB], samp_b[:, :], nodef[:, k:k + 1], None, ALU.is_le, ALU.add,
                                        accum_out=cnt[:, k:k + 1]).then_inc(S("a_coarse"), 1)
                    dve.wait_ge(S("a_coarse"), NP)
                    step(V.tensor_scalar(tn[:, 0:NP], cnt[:, :], -1.0, 0.0, ALU.add, ALU.max))
                    V.tensor_copy(blk_i[:, :], tn[:, 0:NP]).then_inc(S("a_blk"), 1)
                    for k in range(NP):
                        dve.wait_ge(S(f"a_fg{k % NF}"), 16 * (k // NF + 1))
                        if k >= NF:
                            dve.wait_ge(S("a_fine"), k - NF + 1)
                        V.tensor_scalar(junk[:, (k % NF) * SB:(k % NF + 1) * SB], blkbuf[:, (k % NF) * SB:(k % NF + 1) * SB], nodef[:, k:k + 1], None,
                                        ALU.is_le, ALU.add, accum_out=fine[:, k:k + 1]).then_inc(S("a_fine"), 1)
                    dve.wait_ge(S("a_fine"), NP)
                    V.scalar_tensor_tensor(endf[:, :], tn[:, 0:NP], float(SB), fine[:, :], ALU.mult, ALU.add).then_inc(S("a_endf"), 1)
                    dve.wait_ge(S("a_endf"), 1)
                    dve.wait_ge(S("a_start"), 16)
                    step(V.tensor_tensor(empty[:, :], endf[:, :], startf[:, :], ALU.is_equal))
                    V.scalar_tensor_tensor(first_i[:, :], empty[:, :], float(E), startf[:, :], ALU.mult, ALU.add).then_inc(S("a_idx"), 1)
                    step(V.tensor_scalar(tn[:, 0:NP], endf[:, :], -1.0, float(ZROW + 1), ALU.mult, ALU.add))
                    step(V.tensor_tensor(tn[:, NP:2 * NP], tn[:, 0:NP], empty[:, :], ALU.mult))
                    step(V.scalar_tensor_tensor(last_i[:, :], endf[:, :], -1.0, tn[:, NP:2 * NP], ALU.add, ALU.add))
                    V.tensor_scalar(t1[:, 3:4], headf[:, :], 0.0, None, ALU.add).then_inc(S("a_idx1"), 1)

                    dve.wait_ge(S("a_w"), 32)
                    dve.wait_ge(S("a_head"), 1)
                    w2v = w2s[:, :].rearrange("j (i u w) -> j i w u", i=7, w=MO)
                    w2o = w2x[:, :].rearrange("j (b w f) -> j b w f", b=NBLK, f=FW)
                    wrv = wr[:, :].rearrange("j (w u) -> j w u", w=MO)
                    step(V.tensor_scalar(wrv, w2v[:, 6], -KV * C121 / 3.0, None, ALU.mult))
                    step(V.scalar_tensor_tensor(wrv, w2v[:, 5], KV * INV3, wrv, ALU.mult, ALU.add))
                    for b, f0, i, k in ((0, 0, 0, KS), (0, 16, 1, KS * INV3 * 3.0 ** 0.5), (1, 0, 2, KS),
                                        (1, 16, 3, KS * INV3 * 3.0 ** 0.5), (2, 0, 4, KV * INV3 * 3.0 ** 0.5), (2, 16, 6, KV * C121)):
                        V.tensor_scalar(w2o[:, b, :, f0:f0 + 16], w2v[:, i], k, None, ALU.mult).then_inc(S("a_w2x"), 1)
                    for a in range(3):
                        V.tensor_copy(w2o[:, 3 + a, :, 32 + 16 * a:48 + 16 * a], wrv).then_inc(S("a_w2x"), 1)
                    dve.wait_ge(S("a_vec"), 16)
                    step(V.tensor_tensor(sq[:, :], dirv[:, :], dirv[:, :], ALU.mult))
                    V.tensor_reduce(s2[:, :], sq[:, :].rearrange("p (c a) -> p c a", a=3), AX.X, ALU.add).then_inc(S("a_s2"), 1)
                    dve.wait_ge(S("a_sqrt"), 1)
                    step(V.reciprocal(rn[:, :], s2[:, :]))
                    V.tensor_tensor(dirv[:, :].rearrange("p (c a) -> p c a", a=3), dirv[:, :].rearrange("p (c a) -> p c a", a=3),
                                    rn[:, :].rearrange("p (c a) -> p c a", a=1).broadcast_to([P, EP, 3]), ALU.mult).then_inc(S("a_dir"), 1)
                    for b in range(NBLK):
                        dve.wait_ge(S("a_wt"), b + 1)
                        V.tensor_copy(wst[:, b * 128:(b + 1) * 128], banks[b][0:FW, 0:128])
                    step(V.tensor_scalar(diag[:, :], ident[0:P, 0:P], headf[:, :], None, ALU.mult))
                    V.memset(t1[:, 0:1], 0.0).then_inc(S("a_diag"), 1)
                    dve.wait_ge(S("a_hrow"), 1)
                    V.tensor_scalar(link[:, :], banks[6][0:P, 0:P], tailf[:, :], None, ALU.is_equal).then_inc(S("a_link0"), 2)
                    dve.wait_ge(S("a_linkT"), 1)
                    V.tensor_copy(linkT[:, :], banks[7][0:P, 0:P])
                    dve.wait_ge(S("a_endh"), 16)
                    step(V.tensor_scalar(t1[:, 0:1], partf[:, :], float(EP), float(EP), ALU.mult, ALU.add))
                    step(V.tensor_tensor(t1[:, 1:2], endh[:, :], t1[:, 0:1], ALU.is_le))
                    step(V.tensor_scalar(t1[:, 2:3], partf[:, :], float(E + 1), None, ALU.add))
                    step(V.tensor_tensor(t1[:, 0:1], endh[:, :], t1[:, 2:3], ALU.subtract))
                    step(V.tensor_tensor(t1[:, 0:1], t1[:, 0:1], t1[:, 1:2], ALU.mult))
                    step(V.scalar_tensor_tensor(fix_i[:, :], t1[:, 2:3], -1.0, t1[:, 0:1], ALU.add, ALU.add))

                @block.scalar
                def _(act):
                    act.wait_ge(S("a_s2"), 1)
                    nc.scalar.activation(s2[:, :], s2[:, :], ACT.Sqrt).then_inc(S("a_sqrt"), 1)

                @block.tensor
                def _(pe):
                    pe.wait_ge(S("a_id"), 2)
                    pe.wait_ge(S("a_w2x"), 9)
                    w2o = w2x[:, :].rearrange("j (b w f) -> j b w f", b=NBLK, f=FW)
                    for b in range(NBLK):
                        for w in range(MO):
                            last = nc.tensor.transpose(banks[b][0:FW, w * HID:(w + 1) * HID], w2o[:, b, w, :], ident[0:HID, 0:HID])
                        last.then_inc(S("a_wt"), 1)
                    pe.wait_ge(S("a_ones"), 1)
                    pe.wait_ge(S("a_w1"), 16 * MO)
                    pe.wait_ge(S("a_diag"), 1)
                    nc.tensor.matmul(banks[6][0:P, 0:P], ones[0:P, 0:P], diag[:, :], start=True, stop=True).then_inc(S("a_hrow"), 1)
                    pe.wait_ge(S("a_link"), 1)
                    nc.tensor.transpose(banks[7][0:P, 0:P], link[:, :], ident[0:P, 0:P]).then_inc(S("a_linkT"), 1)

        with ExitStack() as st:
            def sbt(name, shape, dt=f32):
                return st.enter_context(nc.sbuf_tensor(name, shape, dt))

            def two(name, w, dt=f32):
                return [sbt(f"{name}_{h}", [P, w], dt) for h in range(2)]

            idx = two("idx", C, i32)
            gx = two("gx", C * DIM)
            xv = two("xv", C * DIM)
            em = two("em", C * NEMB)
            dr = two("dr", C * 3)
            kp = two("kp", C)
            nm = two("nm", C)
            F = two("F", C * FW)
            O = two("O", C * DIM)
            Z = two("Z", C * DIM)
            tmp = sbt("tmp", [P, C * 48])
            FT = [sbt(f"FT{h}", [FW, GW]) for h in range(2)]
            hid = [sbt(f"hid{h}", [128, GW]) for h in range(2)]
            prod = [[sbt(f"prod{h}_{b}", [128, GW]) for b in range(NBLK)] for h in range(2)]
            rt = [sbt(f"rt{h}", [OW, GW]) for h in range(2)]
            th = sbt("th", [P, 2 * GT * 16])
            pa = sbt("pa", [P, 2 * GT * 24])
            pb = sbt("pb", [P, 2 * GT * 24])
            pg = sbt("pg", [P, 2 * GT * MO])

            Fv = [f[:, :].rearrange("p (c f) -> p c f", f=FW) for f in F]

            def col(f):
                if f < 8:
                    return 8 + f
                u, a = divmod(f - 8, 3)
                return 32 + 16 * a + 8 + u

            LD = 5

            with nc.Block() as block:
                @block.sync
                def _(sp):
                    def load(ch, h, t):
                        sp.wait_ge(S(f"b_gx{h}"), t * 16 * C)
                        sp.sem_inc(S("go_sp"), 1)
                        sp.wait_ge(S(f"b_fa{h}"), t * 3)
                        sp.sem_inc(S("go_sp"), 1)
                        sp.dma_start(idx[h][:, :], edges(src, 1)[:, bass.ds(ch * C, C)]).then_inc(S(f"b_idx{h}"), 16)
                        sp.wait_ge(S(f"b_st{h}"), t * 16)
                        sp.sem_inc(S("go_sp"), 1)
                        sp.wait_ge(S(f"b_post{h}"), t)
                        sp.sem_inc(S("go_sp"), 1)
                        sp.dma_start(em[h][:, :], emb.rearrange("(p c) f -> p (c f)", c=EP)[:, bass.ds(ch * C * NEMB, C * NEMB)]).then_inc(S(f"b_ld{h}"), 16)
                        sp.dma_start(xv[h][:, :], xd_d.rearrange("(p c) f -> p (c f)", c=EP)[:, bass.ds(ch * C * DIM, C * DIM)]).then_inc(S(f"b_ld{h}"), 16)
                        sp.dma_start(dr[h][:, :], dir_d.rearrange("(p c) f -> p (c f)", c=EP)[:, bass.ds(ch * C * 3, C * 3)]).then_inc(S(f"b_ld{h}"), 16)
                        sp.dma_start(kp[h][:, :], edges(keep_d, 1)[:, bass.ds(ch * C, C)]).then_inc(S(f"b_ld{h}"), 16)
                        sp.dma_start(nm[h][:, :], edges(weight, 1)[:, bass.ds(ch * C, C)]).then_inc(S(f"b_ld{h}"), 16)

                    def store(ch, h, t):
                        sp.wait_ge(S(f"b_z{h}"), t + 1)
                        sp.dma_start(y0_d[0:E, :].rearrange("(p c) f -> p (c f)", c=EP)[:, bass.ds(ch * C * DIM, C * DIM)], Z[h][:, :]).then_inc(S(f"b_st{h}"), 16)

                    load(0, 0, 0)
                    load(1, 1, 0)
                    with sp.Fori(0, PAIRS - 1) as t:
                        for h in range(2):
                            store(t * 2 + h, h, t)
                            load(t * 2 + h + 2, h, t + 1)
                    for h in range(2):
                        store(2 * PAIRS - 2 + h, h, PAIRS - 1)
                    for h in range(2):
                        sp.wait_ge(S(f"b_st{h}"), 16 * PAIRS)

                @block.gpsimd
                def _(pool):
                    with pool.Fori(0, PAIRS) as t:
                        for h in range(2):
                            pool.wait_ge(S(f"b_idx{h}"), t * 16 + 16)
                            pool.sem_inc(S("go_pool"), 1)
                            for c in range(C):
                                nc.gpsimd.indirect_dma_start(out=gx[h][:, c * DIM:(c + 1) * DIM], out_offset=None, in_=x,
                                                             in_offset=bass.IndirectOffsetOnAxis(idx[h][:, c:c + 1], 0)).then_inc(S(f"b_gx{h}"), 16)

                @block.scalar
                def _(act):
                    A = nc.scalar

                    def features(h, t):
                        act.wait_ge(S(f"b_gx{h}"), t * 16 * C + 16 * C)
                        act.wait_ge(S(f"b_ld{h}"), t * 16 * LD + 16 * LD)
                        act.wait_ge(S("b_T"), (t * G2 + (h + 1) * GC) - G2 if not isinstance(t, int) or t > 0 else 0)
                        g = gx[h][:, :].rearrange("p (c f) -> p c f", f=DIM)
                        A.activation(Fv[h][:, :, 0:8], g[:, :, 0:8], ACT.Copy).then_inc(S(f"b_fa{h}"), 1)
                        A.activation(Fv[h][:, :, 32:80].rearrange("p c (a u) -> p c a u", a=3)[:, :, :, 0:8],
                                     g[:, :, 8:32].rearrange("p c (u a) -> p c a u", a=3), ACT.Copy).then_inc(S(f"b_fa{h}"), 1)
                        A.activation(Fv[h][:, :, QF:FW], em[h][:, :].rearrange("p (c f) -> p c f", f=NEMB), ACT.Copy).then_inc(S(f"b_fa{h}"), 1)

                    def turn(t, first=False, last=False):
                        for g in range(G2):
                            n = t * G2 + g
                            k = g % 2
                            if not (last and g == G2 - 1):
                                act.wait_ge(S("b_T"), n + 2)
                                if not (first and g == 0):
                                    act.wait_ge(S("b_H"), n)
                                    act.wait_ge(S("b_G"), n * NBLK)
                                A.activation(FT[1 - k][:, :], T_ps[1 - k][0:FW, 0:GW], ACT.Copy).then_inc(S("b_FT"), 1)
                                act.wait_ge(S("b_H"), n + 2)
                                if not (first and g == 0):
                                    act.wait_ge(S("b_prod"), n * NBLK)
                                A.activation(hid[1 - k][:, :], H_ps[:, 0:GW], ACT.Relu, scale=(2.0 / NEMB) ** 0.5).then_inc(S("b_hid"), 1)
                            if not (first and g == 0):
                                act.wait_ge(S("b_R"), n)
                                if not (first and g <= 2):
                                    act.wait_ge(S("b_Y"), n - 2)
                                A.activation(rt[1 - k][:, :], R_ps[0:OW, 0:GW], ACT.Copy).then_inc(S("b_rt"), 1)
                            if k == 1 and not (first and g < 3):
                                tanh(n - 3)
                            if g == GC - 4 and not last or g == GC - 4:
                                features(1, t)
                            if g == G2 - 4 and not last:
                                features(0, t + 1)

                    def tanh(n0):
                        act.wait_ge(S("b_Y"), n0 + 2)
                        if not isinstance(n0, int) or n0 > 0:
                            act.wait_ge(S("b_gs"), n0)
                        A.activation(th[:, :].rearrange("p (c f) -> p c f", f=16),
                                     Y_ps[0:P, 0:2 * GT * OW].rearrange("p (c f) -> p c f", f=OW)[:, :, 0:16], ACT.Tanh).then_inc(S("b_th"), 1)

                    features(0, 0)
                    act.wait_ge(S("b_T"), 1)
                    A.activation(FT[0][:, :], T_ps[0][0:FW, 0:GW], ACT.Copy).then_inc(S("b_FT"), 1)
                    act.wait_ge(S("b_H"), 1)
                    A.activation(hid[0][:, :], H_ps[:, 0:GW], ACT.Relu, scale=(2.0 / NEMB) ** 0.5).then_inc(S("b_hid"), 1)
                    turn(0, first=True)
                    with act.Fori(1, PAIRS - 1) as t:
                        turn(t)
                    turn(PAIRS - 1, last=True)
                    NG = PAIRS * G2
                    act.wait_ge(S("b_R"), NG)
                    act.wait_ge(S("b_Y"), NG - 2)
                    A.activation(rt[1][:, :], R_ps[0:OW, 0:GW], ACT.Copy).then_inc(S("b_rt"), 1)
                    tanh(NG - 2)

                @block.tensor
                def _(pe):
                    Tn = nc.tensor

                    def transposes(n, h, g):
                        for c in range(GT):
                            last = Tn.transpose(T_ps[g % 2][0:FW, c * P:(c + 1) * P], Fv[h][:, g * GT + c, :], ident[0:P, 0:P])
                        last.then_inc(S("b_T"), 1)

                    def hidden(n, k):
                        pe.wait_ge(S("b_FT"), n + 1)
                        if not isinstance(n, int) or n > 0:
                            pe.wait_ge(S("b_hid"), n)
                        Tn.matmul(H_ps[:, 0:GW], wh[:, :], FT[k][:, :], start=True, stop=True).then_inc(S("b_H"), 1)

                    def product(n, k, b):
                        if not isinstance(n, int) or NBLK * n + b >= 3:
                            pe.wait_ge(S("b_prod"), n * NBLK + b - 2)
                        Tn.matmul(G_ps[b % 3][:, 0:GW], wst[:, b * 128:(b + 1) * 128], FT[k][:, :], start=True, stop=True).then_inc(S("b_G"), 1)

                    def reduce(n, k, b):
                        pe.wait_ge(S("b_prod"), n * NBLK + b + 1)
                        if b == 0 and (not isinstance(n, int) or n > 0):
                            pe.wait_ge(S("b_rt"), n)
                        last = Tn.matmul(R_ps[0:OW, 0:GW], red[:, b * OW:(b + 1) * OW], prod[k][b][:, :], start=(b == 0), stop=(b == NBLK - 1))
                        if b == NBLK - 1:
                            last.then_inc(S("b_R"), 1)

                    def back(n, k):
                        pe.wait_ge(S("b_rt"), n + 1)
                        if k == 0 and (not isinstance(n, int) or n > 0):
                            pe.wait_ge(S("b_yr"), n)
                            pe.wait_ge(S("b_th"), n // 2 if isinstance(n, int) else half(n))
                        pe.sem_inc(S("go_pe"), 1)
                        for c in range(GT):
                            last = Tn.transpose(Y_ps[0:P, (k * GT + c) * OW:(k * GT + c + 1) * OW], rt[k][:, c * P:(c + 1) * P], ident[0:OW, 0:OW])
                        last.then_inc(S("b_Y"), 1)

                    half_of = {}

                    def half(n):
                        return half_of["n"]

                    def turn(t, first=False, last=False):
                        for g in range(G2):
                            n = t * G2 + g
                            k = g % 2
                            if not (last and g == G2 - 1):
                                g1 = (g + 1) % G2
                                h1 = g1 // GC
                                if g1 % GC == 0:
                                    tt = t + 1 if g1 == 0 else t
                                    pe.wait_ge(S(f"b_fd{h1}"), tt + 1)
                                    pe.wait_ge(S(f"b_fa{h1}"), tt * 3 + 3)
                                if not (first and g == 0):
                                    pe.wait_ge(S("b_FT"), n)
                                transposes(n + 1, h1, g1 % GC)
                            for b in range(NBLK):
                                product(n, k, b)
                                if not (first and g == 0):
                                    reduce(n - 1, 1 - k, b)
                                if b == 2 and not (first and g < 2):
                                    half_of["n"] = t * (G2 // 2) + (g - 2) // 2
                                    back(n - 2, k)
                                if b == 3 and not (last and g == G2 - 1):
                                    hidden(n + 1, 1 - k)

                    pe.wait_ge(S("b_fd0"), 1)
                    pe.wait_ge(S("b_fa0"), 3)
                    transposes(0, 0, 0)
                    hidden(0, 0)
                    turn(0, first=True)
                    with pe.Fori(1, PAIRS - 1) as t:
                        turn(t)
                    turn(PAIRS - 1, last=True)
                    NG = PAIRS * G2
                    for b in range(NBLK):
                        reduce(NG - 1, 1, b)
                    back(NG - 2, 0)
                    back(NG - 1, 1)

                @block.vector
                def _(dve):
                    V = nc.vector

                    def features(h, t):
                        dve.wait_ge(S(f"b_ld{h}"), t * 16 * LD + 16 * LD)
                        if not isinstance(t, int) or t > 0:
                            dve.wait_ge(S("b_T"), t * G2 + (h + 1) * GC - G2)
                        dve.wait_ge(S(f"b_fc{1 - h}"), t + h)
                        xvv = xv[h][:, :].rearrange("p (c f) -> p c f", f=DIM)
                        for f in range(DIM):
                            last = V.tensor_tensor_scan(out=Fv[h][:, :, col(f)], data0=kp[h][:, :], data1=xvv[:, :, f],
                                                        initial=Fv[1 - h][:, C - 1, col(f):col(f) + 1], op0=ALU.mult, op1=ALU.add)
                        last.then_inc(S(f"b_fc{h}"), 1)
                        dve.wait_ge(S(f"b_fc{h}"), t + 1)
                        dve.wait_ge(S(f"b_fa{h}"), t * 3 + 3)
                        tv = tmp[:, :].rearrange("p (c a u) -> p c a u", a=3, u=16)
                        V.tensor_tensor(tv, Fv[h][:, :, 32:80].rearrange("p c (a u) -> p c a u", a=3),
                                        dr[h][:, :].rearrange("p (c a u) -> p c a u", a=3, u=1).broadcast_to([P, C, 3, 16]), ALU.mult).then_inc(S("b_d"), 1)
                        dve.wait_ge(S("b_d"), t * 4 + 2 * h + 1)
                        V.tensor_tensor(Fv[h][:, :, 16:32], tv[:, :, 0], tv[:, :, 1], ALU.add).then_inc(S("b_d"), 1)
                        dve.wait_ge(S("b_d"), t * 4 + 2 * h + 2)
                        V.tensor_tensor(Fv[h][:, :, 16:32], Fv[h][:, :, 16:32], tv[:, :, 2], ALU.add).then_inc(S(f"b_fd{h}"), 1)

                    def products(n, k, first):
                        dve.wait_ge(S("b_hid"), n + 1)
                        for b in range(NBLK):
                            dve.wait_ge(S("b_G"), n * NBLK + b + 1)
                            if b == 0 and not first:
                                dve.wait_ge(S("b_R"), n - 1)
                            V.tensor_tensor(prod[k][b][:, :], G_ps[b % 3][:, 0:GW], hid[k][:, :], ALU.mult).then_inc(S("b_prod"), 1)

                    def post(n0, m, h, q, t):
                        W2G = 2 * GT
                        yv = Y_ps[0:P, 0:W2G * OW].rearrange("p (c f) -> p c f", f=OW)
                        thv = th[:, :].rearrange("p (c f) -> p c f", f=16)
                        c0 = q * W2G
                        nrm = nm[h][:, c0:c0 + W2G].rearrange("p (c w) -> p c w", w=1).broadcast_to([P, W2G, MO])
                        ov = O[h][:, :].rearrange("p (c f) -> p c f", f=DIM)[:, c0:c0 + W2G, :]
                        dve.wait_ge(S("b_Y"), n0 + 2)
                        dve.wait_ge(S("b_th"), m + 1)
                        if not isinstance(m, int) or m > 0:
                            dve.wait_ge(S("b_o"), m)
                        pav = pa[:, :].rearrange("p (c w a) -> p c w a", w=MO, a=3)
                        pbv = pb[:, :].rearrange("p (c w a) -> p c w a", w=MO, a=3)
                        pgv = pg[:, :].rearrange("p (c w) -> p c w", w=MO)
                        V.tensor_tensor(pav, yv[:, :, 16:24].rearrange("p c (w a) -> p c w a", a=1).broadcast_to([P, W2G, MO, 3]),
                                        dr[h][:, c0 * 3:(c0 + W2G) * 3].rearrange("p (c w a) -> p c w a", w=1, a=3).broadcast_to([P, W2G, MO, 3]),
                                        ALU.mult).then_inc(S("b_pa"), 1)
                        V.scalar_tensor_tensor(pgv, thv[:, :, 8:16], TG, nrm, ALU.mult, ALU.mult).then_inc(S("b_gs"), 1)
                        V.scalar_tensor_tensor(ov[:, :, 0:8], thv[:, :, 0:8], TG, nrm, ALU.mult, ALU.mult).then_inc(S("b_gs"), 1)
                        dve.wait_ge(S("b_pa"), m + 1)
                        V.tensor_tensor(pbv, pav, yv[:, :, 24:48].rearrange("p c (a w) -> p c w a", a=3), ALU.add).then_inc(S("b_yr"), 2)
                        dve.wait_ge(S("b_yr"), n0 + 2)
                        dve.wait_ge(S("b_gs"), n0 + 2)
                        V.tensor_tensor(ov[:, :, 8:32].rearrange("p c (w a) -> p c w a", a=3), pbv,
                                        pgv.rearrange("p c (w a) -> p c w a", a=1).broadcast_to([P, W2G, MO, 3]), ALU.mult).then_inc(S("b_o"), 1)

                    def sums(h, t, m):
                        dve.wait_ge(S("b_o"), m + 1)
                        dve.wait_ge(S(f"b_z{1 - h}"), t + h)
                        for f in range(DIM):
                            ov = O[h][:, :].rearrange("p (c f) -> p c f", f=DIM)[:, :, f]
                            zv = Z[h][:, :].rearrange("p (c f) -> p c f", f=DIM)[:, :, f]
                            last = V.tensor_tensor_scan(out=zv, data0=kp[h][:, :], data1=ov,
                                                        initial=Z[1 - h][:, (C - 1) * DIM + f:(C - 1) * DIM + f + 1], op0=ALU.mult, op1=ALU.add)
                        last.then_inc(S(f"b_z{h}"), 1)
                        dve.wait_ge(S(f"b_z{h}"), t + 1)
                        V.tensor_copy(th2[:, :], kp[h][:, 0:1]).then_inc(S(f"b_post{h}"), 1)

                    th2 = sbt("th2", [P, 1])
                    QP = GC // 2

                    def turn(t, first=False, last=False):
                        for g in range(G2):
                            products(t * G2 + g, g % 2, first and g < 2)
                            if g % 2 == 1 and not (first and g < 3):
                                n0 = t * G2 + g - 3
                                m = t * (G2 // 2) + (g - 3) // 2
                                q = (g - 3) // 2 % (G2 // 2)
                                post(n0, m, q // QP, q % QP, t)
                                if q % QP == QP - 1:
                                    h = q // QP
                                    sums(h, t - 1 if g < 3 else t, m)
                            if g == GC - 4:
                                features(1, t)
                            if g == G2 - 4 and not last:
                                features(0, t + 1)

                    hv = hx_keep[:, :]
                    V.tensor_copy(Fv[1][:, C - 1, 8:16], hv[:, 0:8])
                    V.tensor_copy(Fv[1][:, C - 1, 32:80].rearrange("p (a u) -> p a u", a=3)[:, :, 8:16],
                                  hv[:, 8:32].rearrange("p (u a) -> p a u", a=3)).then_inc(S("b_init"), 1)
                    V.memset(Z[1][:, :], 0.0).then_inc(S("b_init"), 1)
                    dve.wait_ge(S("b_init"), 2)
                    features(0, 0)
                    turn(0, first=True)
                    with dve.Fori(1, PAIRS - 1) as t:
                        turn(t)
                    turn(PAIRS - 1, last=True)
                    m = PAIRS * G2 // 2 - 1
                    post(PAIRS * G2 - 2, m, 1, QP - 1, PAIRS - 1)
                    sums(1, PAIRS - 1, m)
                    V.tensor_copy(hx_keep[:, :], Z[1][:, (C - 1) * DIM:C * DIM]).then_inc(S("b_tail"), 1)
                    dve.wait_ge(S("b_tail"), 1)

        def layer_norm(dve, step, v, out_v, sq_t, st, key):
            V = nc.vector
            vv = v.rearrange("p (k f) -> p k f", f=DIM)
            mean, var, rs = st[:, 0:NP], st[:, NP:2 * NP], st[:, 2 * NP:3 * NP]
            bc = lambda a: a.rearrange("p (k f) -> p k f", f=1).broadcast_to([P, NP, DIM])
            step(V.tensor_reduce(mean, vv, AX.X, ALU.add))
            step(V.tensor_scalar(mean, mean, 1.0 / DIM, None, ALU.mult))
            step(V.tensor_tensor(vv, vv, bc(mean), ALU.subtract))
            step(V.tensor_tensor(sq_t, v, v, ALU.mult))
            step(V.tensor_reduce(var, sq_t.rearrange("p (k f) -> p k f", f=DIM), AX.X, ALU.add))
            V.tensor_scalar(var, var, 1.0 / DIM, EPS, ALU.mult, ALU.add).then_inc(S(key + "_var"), 1)
            dve.wait_ge(S(key + "_std"), 1)
            step(V.reciprocal(rs, rs))
            step(V.tensor_tensor(out_v, vv, bc(rs), ALU.mult))

        with ExitStack() as st:
            def sbt(name, shape, dt=f32):
                return st.enter_context(nc.sbuf_tensor(name, shape, dt))

            fixr = sbt("fixr", [P, DIM])
            ng = sbt("ng", [P, NP * DIM])
            sqb = sbt("sqb", [P, NP * DIM])
            stt = sbt("stt", [P, 3 * NP])
            x1e = sbt("x1e", [P, NP * (DIM + 1)])
            sd = sbt("sd", [P, NP])

            with nc.Block() as block:
                @block.tensor
                def _(pe):
                    nc.tensor.matmul(banks[0][0:P, 0:DIM], link[:, :], hx_keep[:, :], start=True, stop=True).then_inc(S("c_carry"), 1)

                @block.gpsimd
                def _(pool):
                    nc.gpsimd.indirect_dma_start(out=fixr[:, :], out_offset=None, in_=y0_d,
                                                 in_offset=bass.IndirectOffsetOnAxis(fix_i[:, :], 0)).then_inc(S("c_fixr"), 16)
                    pool.wait_ge(S("c_fix"), 1)
                    nc.gpsimd.indirect_dma_start(out=y0_d, out_offset=bass.IndirectOffsetOnAxis(fix_i[:, :], 0),
                                                 in_=fixr[:, :], in_offset=None).then_inc(S("c_fixw"), 16)
                    pool.wait_ge(S("c_fixw"), 16)
                    for k in range(NP):
                        nc.gpsimd.indirect_dma_start(out=ng[:, k * DIM:(k + 1) * DIM], out_offset=None, in_=y0_d,
                                                     in_offset=bass.IndirectOffsetOnAxis(last_i[:, k:k + 1], 0)).then_inc(S("c_ng"), 16)
                    pool.wait_ge(S("c_sd"), 1)
                    for k in range(NP):
                        nc.gpsimd.indirect_dma_start(out=sd_d, out_offset=bass.IndirectOffsetOnAxis(first_i[:, k:k + 1], 0),
                                                     in_=sd[:, k:k + 1], in_offset=None,
                                                     bounds_check=E - 1, oob_is_err=False).then_inc(S("c_sdw"), 16)
                    pool.wait_ge(S("c_sdt"), 16)
                    nc.gpsimd.indirect_dma_start(out=hsd[:, :], out_offset=None, in_=sdt_d,
                                                 in_offset=bass.IndirectOffsetOnAxis(head_i[:, :], 0)).then_inc(S("c_hsd"), 16)
                    pool.wait_ge(S("c_sdw"), 16 * NP)
                    pool.wait_ge(S("c_hsd"), 16)

                @block.vector
                def _(dve):
                    n = [0]

                    def step(ins):
                        n[0] += 1
                        ins.then_inc(S("c_dve"), 1)
                        dve.wait_ge(S("c_dve"), n[0])

                    V = nc.vector
                    dve.wait_ge(S("c_carry"), 1)
                    dve.wait_ge(S("c_fixr"), 16)
                    V.tensor_tensor(fixr[:, :], banks[0][0:P, 0:DIM], fixr[:, :], ALU.add).then_inc(S("c_fix"), 1)
                    dve.wait_ge(S("c_ng"), 16 * NP)
                    step(V.tensor_tensor(ng[:, :], ng[:, :], xn[:, :], ALU.add))
                    layer_norm(dve, step, ng[:, :], xn[:, :].rearrange("p (k f) -> p k f", f=DIM), sqb[:, :], stt, "c")
                    xv3 = xn[:, :].rearrange("p (k f) -> p k f", f=DIM)
                    x1v = x1e[:, :].rearrange("p (k f) -> p k f", f=DIM + 1)
                    V.tensor_copy(x1v[:, :, 0:DIM], xv3)
                    bc = lambda a: a.rearrange("p (k f) -> p k f", k=1).broadcast_to([P, NP, DIM])
                    sq3 = sqb[:, :].rearrange("p (k f) -> p k f", f=DIM)
                    step(V.tensor_tensor(sq3, xv3, bc(attn_b[:, DIM:2 * DIM]), ALU.mult))
                    V.tensor_reduce(sd[:, :], sq3, AX.X, ALU.add).then_inc(S("c_sd"), 1)
                    dve.wait_ge(S("c_sd"), 1)
                    step(V.tensor_tensor(sq3, xv3, bc(attn_b[:, 0:DIM]), ALU.mult))
                    V.tensor_reduce(x1v[:, :, DIM:DIM + 1], sq3, AX.X, ALU.add).then_inc(S("c_x1e"), 1)

                @block.scalar
                def _(act):
                    act.wait_ge(S("c_var"), 1)
                    nc.scalar.activation(stt[:, 2 * NP:3 * NP], stt[:, NP:2 * NP], ACT.Sqrt).then_inc(S("c_std"), 1)

                @block.sync
                def _(sp):
                    sp.wait_ge(S("c_sd"), 1)
                    sp.dma_start(sdt_d.rearrange("(p k) a -> p (k a)", k=NP), sd[:, :]).then_inc(S("c_sdt"), 16)
                    sp.wait_ge(S("c_x1e"), 1)
                    sp.dma_start(tab_d.rearrange("(p k) f -> p (k f)", k=NP), x1e[:, :]).then_inc(S("c_tab"), 16)
                    sp.wait_ge(S("c_tab"), 16)
                    sp.wait_ge(S("c_sdt"), 16)

        with ExitStack() as st:
            def sbt(name, shape, dt=f32):
                return st.enter_context(nc.sbuf_tensor(name, shape, dt))

            def two(name, w, dt=f32):
                return [sbt(f"{name}_{h}", [P, w], dt) for h in range(2)]

            T1 = DIM + 1
            idx = two("idxb", C, i32)
            gx = two("gxb", C * T1)
            sdr = two("sdr", C)
            kp = two("kpb", C)
            rst = sbt("rst", [P, C])
            sdf = two("sdf", C)
            ee = sbt("ee", [P, C])
            lk = sbt("lk", [P, C])
            mx = two("mx", C + 1)
            ex = sbt("ex", [P, 2 * C])
            dec = sbt("dec", [P, C])
            wx = sbt("wx", [P, C * DIM])
            Z = two("Zb", C * R1)

            with nc.Block() as block:
                @block.sync
                def _(sp):
                    def load(ch, h, t):
                        sp.wait_ge(S(f"d_gx{h}"), t * 16 * C)
                        sp.sem_inc(S("go_sp"), 1)
                        sp.wait_ge(S(f"d_wx{h}"), t)
                        sp.sem_inc(S("go_sp"), 1)
                        sp.dma_start(idx[h][:, :], edges(src, 1)[:, bass.ds(ch * C, C)]).then_inc(S(f"d_idx{h}"), 16)
                        sp.wait_ge(S(f"d_z{h}"), t)
                        sp.sem_inc(S("go_sp"), 1)
                        sp.wait_ge(S(f"d_st{h}"), t * 16)
                        sp.sem_inc(S("go_sp"), 1)
                        sp.dma_start(sdr[h][:, :], sd_d.rearrange("(p c) a -> p (c a)", c=EP)[:, bass.ds(ch * C, C)]).then_inc(S(f"d_ld{h}"), 16)
                        sp.dma_start(kp[h][:, :], edges(keep_d, 1)[:, bass.ds(ch * C, C)]).then_inc(S(f"d_ld{h}"), 16)

                    def store(ch, h, t):
                        sp.wait_ge(S(f"d_z{h}"), t + 1)
                        sp.wait_ge(S(f"d_zm{h}"), t + 1)
                        sp.dma_start(y1_d[0:E, :].rearrange("(p c) f -> p (c f)", c=EP)[:, bass.ds(ch * C * R1, C * R1)], Z[h][:, :]).then_inc(S(f"d_st{h}"), 16)

                    load(0, 0, 0)
                    load(1, 1, 0)
                    with sp.Fori(0, PAIRS - 1) as t:
                        for h in range(2):
                            store(t * 2 + h, h, t)
                            load(t * 2 + h + 2, h, t + 1)
                    for h in range(2):
                        store(2 * PAIRS - 2 + h, h, PAIRS - 1)
                    for h in range(2):
                        sp.wait_ge(S(f"d_st{h}"), 16 * PAIRS)

                @block.gpsimd
                def _(pool):
                    with pool.Fori(0, PAIRS) as t:
                        for h in range(2):
                            pool.wait_ge(S(f"d_idx{h}"), t * 16 + 16)
                            pool.sem_inc(S("go_pool"), 1)
                            for c in range(C):
                                nc.gpsimd.indirect_dma_start(out=gx[h][:, c * T1:(c + 1) * T1], out_offset=None, in_=tab_d,
                                                             in_offset=bass.IndirectOffsetOnAxis(idx[h][:, c:c + 1], 0)).then_inc(S(f"d_gx{h}"), 16)

                @block.scalar
                def _(act):
                    def chunk(h, t):
                        act.wait_ge(S("d_pre"), t * 2 + h + 1)
                        nc.scalar.activation(ex[:, :], ex[:, :], ACT.Exp).then_inc(S("d_exp"), 1)
                        nc.scalar.activation(Z[h][:, :].rearrange("p (c f) -> p c f", f=R1)[:, :, DIM + 1],
                                             mx[h][:, 1:C + 1], ACT.Copy).then_inc(S(f"d_zm{h}"), 1)

                    with act.Fori(0, PAIRS) as t:
                        for h in range(2):
                            chunk(h, t)

                @block.vector
                def _(dve):
                    V = nc.vector
                    STEPS = 6

                    def chunk(h, t):
                        n = [0]

                        def step(ins):
                            n[0] += 1
                            ins.then_inc(S("d_dve"), 1)
                            dve.wait_ge(S("d_dve"), t * 2 * STEPS + h * STEPS + n[0])

                        g = gx[h][:, :].rearrange("p (c f) -> p c f", f=T1)
                        dve.wait_ge(S(f"d_ld{h}"), t * 32 + 32)
                        V.tensor_scalar(rst[:, :], kp[h][:, :], -1.0, BIG, ALU.add, ALU.mult)
                        V.tensor_copy(mx[h][:, 0:1], mx[1 - h][:, C:C + 1])
                        step(V.tensor_tensor_scan(out=sdf[h][:, :], data0=kp[h][:, :], data1=sdr[h][:, :],
                                                  initial=sdf[1 - h][:, C - 1:C], op0=ALU.mult, op1=ALU.add))
                        dve.wait_ge(S(f"d_gx{h}"), t * 16 * C + 16 * C)
                        step(V.tensor_tensor(lk[:, :], sdf[h][:, :], g[:, :, DIM], ALU.add))
                        step(V.scalar_tensor_tensor(ee[:, :], lk[:, :], 0.01, lk[:, :], ALU.mult, ALU.max))
                        step(V.tensor_tensor_scan(out=mx[h][:, 1:C + 1], data0=rst[:, :], data1=ee[:, :],
                                                  initial=mx[1 - h][:, C:C + 1], op0=ALU.add, op1=ALU.max))
                        V.tensor_tensor(ex[:, 0:C], ee[:, :], mx[h][:, 1:C + 1], ALU.subtract)
                        step(V.tensor_tensor(ex[:, C:2 * C], mx[h][:, 0:C], mx[h][:, 1:C + 1], ALU.subtract))
                        V.memset(one[:, :], 0.0).then_inc(S("d_pre"), 1)
                        dve.wait_ge(S("d_exp"), t * 2 + h + 1)
                        V.scalar_tensor_tensor(dec[:, :], ex[:, C:2 * C], 1.0, kp[h][:, :], ALU.min, ALU.mult)
                        step(V.tensor_tensor(wx[:, :].rearrange("p (c f) -> p c f", f=DIM), g[:, :, 0:DIM],
                                             ex[:, 0:C].rearrange("p (c f) -> p c f", f=1).broadcast_to([P, C, DIM]), ALU.mult))
                        V.memset(one[:, :], 0.0).then_inc(S(f"d_wx{h}"), 1)
                        assert n[0] == STEPS
                        zv = Z[h][:, :].rearrange("p (c f) -> p c f", f=R1)
                        zp = Z[1 - h][:, :].rearrange("p (c f) -> p c f", f=R1)
                        V.tensor_tensor_scan(out=zv[:, :, DIM], data0=dec[:, :], data1=ex[:, 0:C], initial=zp[:, C - 1, DIM:DIM + 1],
                                             op0=ALU.mult, op1=ALU.add)
                        for f in range(DIM):
                            last = V.tensor_tensor_scan(out=zv[:, :, f], data0=dec[:, :],
                                                        data1=wx[:, :].rearrange("p (c f) -> p c f", f=DIM)[:, :, f],
                                                        initial=zp[:, C - 1, f:f + 1], op0=ALU.mult, op1=ALU.add)
                        last.then_inc(S(f"d_z{h}"), 1)
                        dve.wait_ge(S(f"d_z{h}"), t + 1)

                    one = sbt("one_d", [P, 1])
                    V.tensor_copy(sdf[1][:, C - 1:C], hsd[:, :]).then_inc(S("d_init"), 1)
                    V.memset(mx[1][:, C:C + 1], -BIG).then_inc(S("d_init"), 1)
                    V.memset(Z[1][:, :], 0.0).then_inc(S("d_init"), 1)
                    dve.wait_ge(S("d_init"), 3)
                    with dve.Fori(0, PAIRS) as t:
                        for h in range(2):
                            chunk(h, t)
                    dve.wait_ge(S("d_zm1"), PAIRS)
                    V.tensor_copy(tail1[:, :], Z[1][:, (C - 1) * R1:C * R1]).then_inc(S("d_tail"), 1)
                    dve.wait_ge(S("d_tail"), 1)

        with ExitStack() as st:
            def sbt(name, shape, dt=f32):
                return st.enter_context(nc.sbuf_tensor(name, shape, dt))

            fixr = sbt("fixr1", [P, R1])
            dm = sbt("dm", [P, P])
            am = sbt("am", [P, P])
            cw = sbt("cw", [P, P])
            sm = sbt("sm", [P, 8])
            ng = sbt("ng1", [P, NP * R1])
            hh = sbt("hh", [P, NP * DIM])
            sqb = sbt("sqb1", [P, NP * DIM])
            stt = sbt("stt1", [P, 3 * NP])

            with nc.Block() as block:
                @block.tensor
                def _(pe):
                    pe.wait_ge(S("e_dm"), 1)
                    nc.tensor.matmul(banks[0][0:P, 0:P], ones[0:P, 0:P], dm[:, :], start=True, stop=True).then_inc(S("e_mrow"), 1)
                    pe.wait_ge(S("e_dm"), 2)
                    nc.tensor.matmul(banks[1][0:P, 0:P], ones[0:P, 0:P], dm[:, :], start=True, stop=True).then_inc(S("e_mrow"), 1)
                    pe.wait_ge(S("e_cw"), 1)
                    nc.tensor.matmul(banks[2][0:P, 0:DIM + 1], cw[:, :], tail1[:, 0:DIM + 1], start=True, stop=True).then_inc(S("e_carry"), 1)

                @block.gpsimd
                def _(pool):
                    nc.gpsimd.indirect_dma_start(out=fixr[:, :], out_offset=None, in_=y1_d,
                                                 in_offset=bass.IndirectOffsetOnAxis(fix_i[:, :], 0)).then_inc(S("e_fixr"), 16)
                    pool.wait_ge(S("e_fix"), 1)
                    nc.gpsimd.indirect_dma_start(out=y1_d, out_offset=bass.IndirectOffsetOnAxis(fix_i[:, :], 0),
                                                 in_=fixr[:, :], in_offset=None).then_inc(S("e_fixw"), 16)
                    pool.wait_ge(S("e_fixw"), 16)
                    for k in range(NP):
                        nc.gpsimd.indirect_dma_start(out=ng[:, k * R1:(k + 1) * R1], out_offset=None, in_=y1_d,
                                                     in_offset=bass.IndirectOffsetOnAxis(last_i[:, k:k + 1], 0)).then_inc(S("e_ng"), 16)

                @block.vector
                def _(dve):
                    n = [0]

                    def step(ins):
                        n[0] += 1
                        ins.then_inc(S("e_dve"), 1)
                        dve.wait_ge(S("e_dve"), n[0])

                    V = nc.vector
                    mt = tail1[:, DIM + 1:DIM + 2]
                    V.tensor_scalar(dm[:, :], ident[0:P, 0:P], mt, None, ALU.mult).then_inc(S("e_dm"), 1)
                    step(V.tensor_scalar(am[:, :], linkT[:, :], -1.0, BIG, ALU.add, ALU.mult))
                    dve.wait_ge(S("e_mrow"), 1)
                    step(V.tensor_tensor(cw[:, :], banks[0][0:P, 0:P], linkT[:, :], ALU.mult))
                    step(V.tensor_tensor(cw[:, :], cw[:, :], am[:, :], ALU.add))
                    step(V.tensor_reduce(sm[:, 0:1], cw[:, :], AX.X, ALU.max))
                    dve.wait_ge(S("e_fixr"), 16)
                    step(V.tensor_tensor(sm[:, 1:2], sm[:, 0:1], fixr[:, DIM + 1:DIM + 2], ALU.max))
                    V.tensor_scalar(dm[:, :], ident[0:P, 0:P], sm[:, 1:2], None, ALU.mult).then_inc(S("e_dm"), 1)
                    dve.wait_ge(S("e_mrow"), 2)
                    step(V.tensor_scalar(am[:, :], banks[1][0:P, 0:P], mt, 0.0, ALU.subtract, ALU.max))
                    V.tensor_tensor(sm[:, 2:3], fixr[:, DIM + 1:DIM + 2], sm[:, 1:2], ALU.subtract).then_inc(S("e_am"), 1)
                    dve.wait_ge(S("e_exp"), 2)
                    V.tensor_tensor(cw[:, :], am[:, :], link[:, :], ALU.mult).then_inc(S("e_cw"), 1)
                    dve.wait_ge(S("e_carry"), 1)
                    V.scalar_tensor_tensor(fixr[:, 0:DIM + 1], fixr[:, 0:DIM + 1], sm[:, 3:4], banks[2][0:P, 0:DIM + 1],
                                           ALU.mult, ALU.add).then_inc(S("e_fix"), 1)
                    dve.wait_ge(S("e_ng"), 16 * NP)
                    ngv = ng[:, :].rearrange("p (k f) -> p k f", f=R1)
                    hv = hh[:, :].rearrange("p (k f) -> p k f", f=DIM)
                    step(V.tensor_tensor(stt[:, 0:NP].rearrange("p (k f) -> p k f", f=1), ngv[:, :, DIM:DIM + 1],
                                         empty[:, :].rearrange("p (k f) -> p k f", f=1), ALU.add))
                    step(V.reciprocal(stt[:, NP:2 * NP], stt[:, 0:NP]))
                    step(V.tensor_tensor(hv, ngv[:, :, 0:DIM], stt[:, NP:2 * NP].rearrange("p (k f) -> p k f", f=1).broadcast_to([P, NP, DIM]), ALU.mult))
                    step(V.tensor_tensor(hh[:, :], hh[:, :], xn[:, :], ALU.add))
                    layer_norm(dve, step, hh[:, :], xn[:, :].rearrange("p (k f) -> p k f", f=DIM), sqb[:, :], stt, "e")
                    V.memset(sm[:, 4:5], 0.0).then_inc(S("e_done"), 1)

                @block.scalar
                def _(act):
                    act.wait_ge(S("e_am"), 1)
                    nc.scalar.activation(am[:, :], am[:, :], ACT.Exp, scale=-1.0).then_inc(S("e_exp"), 1)
                    nc.scalar.activation(sm[:, 3:4], sm[:, 2:3], ACT.Exp).then_inc(S("e_exp"), 1)
                    act.wait_ge(S("e_var"), 1)
                    nc.scalar.activation(stt[:, 2 * NP:3 * NP], stt[:, NP:2 * NP], ACT.Sqrt).then_inc(S("e_std"), 1)

                @block.sync
                def _(sp):
                    sp.wait_ge(S("e_done"), 1)
                    sp.dma_start(out.rearrange("(p k) f -> p (k f)", k=NP), xn[:, :]).then_inc(S("e_out"), 16)
                    sp.wait_ge(S("e_out"), 16)


_INS = ["x", "src", "dst", "edge_attr_10", "edge_attr_3", "edge_weight", "L0_gnn_W1", "L0_gnn_W2", "L1_gnn_attn_w"]


def kernel(**inputs):
    import numpy as _np
    import concourse.bacc as _bacc
    from concourse import mybir as _mybir
    from concourse.bass_utils import run_bass_kernel_spmd as _run

    nc = _bacc.Bacc("TRN2", target_bir_lowering=False, num_devices=1)
    arrays, args = {}, []
    for name in _INS:
        a = _np.ascontiguousarray(inputs[name])
        arrays[f"in_{name}"] = a
        args.append(nc.dram_tensor(f"in_{name}", a.shape, _mybir.dt.from_np(a.dtype), kind="ExternalInput").ap())
    shape = inputs["x"].shape
    args.append(nc.dram_tensor("out_0", shape, _mybir.dt.float32, kind="ExternalOutput").ap())
    gnn_resnorm_kernel(nc, *args)
    r = _run(nc, [arrays], core_ids=[0])
    return r.results[0]["out_0"]
```

```python
import concourse.bass as bass
from concourse import mybir
from contextlib import ExitStack


def gnn_resnorm_kernel(nc, x, src, dst, emb, vec, weight, W1, W2, attn, out):
    f32 = mybir.dt.float32
    f32r = mybir.dt.float32r
    i32 = mybir.dt.int32
    ALU = mybir.AluOpType
    ACT = mybir.ActivationFunctionType
    AX = mybir.AxisListType

    N, DIM = x.shape
    E = src.shape[0]
    NEMB, HID = W1.shape
    P = 125
    EP = E // P
    NP = N // P
    assert P * EP == E and P * NP == N
    C = 40
    PAIRS = EP // (2 * C)
    GT = 4
    GW = GT * P
    GC = C // GT
    G2 = 2 * GC
    MO = 8
    NOUT = 6 * MO
    KF = 32
    NT = 3
    QF = 80
    FD = QF + NEMB
    FW = NT * KF
    HJ = HID // 2
    SB = 500
    NSB = E // SB
    ZROW = E + 200
    PAD = 256
    R1 = DIM + 2
    BIG = 3.0e38
    EPS = 1e-5
    TG = 1.593
    PW_S, PW_V, INV3 = 0.17677669529663687, 0.25, 0.5773502691896258
    KS = PW_S / HID ** 0.5
    KV = PW_V / HID ** 0.5
    C121 = 1.5 ** 0.5

    def edges(ap, width):
        return ap.rearrange("(p c) f -> p c f", c=EP) if width > 1 else ap.rearrange("(p c) -> p c", c=EP)

    ctx = ExitStack()
    with ctx:
        def sb(name, shape, dt=f32):
            return ctx.enter_context(nc.sbuf_tensor(name, shape, dt))

        def sem(name):
            return ctx.enter_context(nc.semaphore(name))

        def dram(name, shape, dt=f32):
            return nc.dram_tensor(name, shape, dt, kind="Internal").ap()

        dstf_d = dram("dstf_d", (NSB, SB))
        samp_d = dram("samp_d", (NSB,))
        end_d = dram("end_d", (N + 1, 1))
        xd_d = dram("xd_d", (E, DIM))
        sd_d = dram("sd_d", (E, 1))
        dir_d = dram("dir_d", (E, 3))
        keep_d = dram("keep_d", (E,))
        y0_d = dram("y0_d", (E + PAD, DIM))
        y1_d = dram("y1_d", (E + PAD, R1))
        tab_d = dram("tab_d", (N, DIM + 1))
        sdt_d = dram("sdt_d", (N, 1))

        ident = sb("ident", [128, 128])
        ones = sb("ones", [128, 128])
        wst = sb("wst", [128, 6 * 128], f32r)
        wh = sb("wh", [128, 3 * 128], f32r)
        red = sb("red", [128, 4 * NOUT])
        attn_b = sb("attn_b", [P, 2 * DIM])

        xn = sb("xn", [P, NP * DIM])
        endf = sb("endf", [P, NP])
        startf = sb("startf", [P, NP])
        empty = sb("empty", [P, NP])
        first_i = sb("first_i", [P, NP], i32)
        last_i = sb("last_i", [P, NP], i32)
        head_i = sb("head_i", [P, 1], i32)
        fix_i = sb("fix_i", [P, 1], i32)
        headf = sb("headf", [P, 1])
        tailf = sb("tailf", [P, 1])
        hx_keep = sb("hx_keep", [P, DIM])
        tail1 = sb("tail1", [P, R1])
        hsd = sb("hsd", [P, 1])
        link = sb("link", [P, P])
        linkT = sb("linkT", [P, P])

        G_ps = [ctx.enter_context(nc.psum_tensor(f"G_ps{i}", [128, 1024], f32)) for i in range(2)]
        T_ps = ctx.enter_context(nc.psum_tensor("T_ps", [128, 512], f32))
        H_ps = ctx.enter_context(nc.psum_tensor("H_ps", [128, 512], f32))
        R_ps = ctx.enter_context(nc.psum_tensor("R_ps", [128, 512], f32))
        Y_ps = ctx.enter_context(nc.psum_tensor("Y_ps", [128, 512], f32))

        all_sems = {}

        def S(name):
            if name not in all_sems:
                all_sems[name] = sem(name)
            return all_sems[name]

        with ExitStack() as st:
            def sbt(name, shape, dt=f32):
                return st.enter_context(nc.sbuf_tensor(name, shape, dt))

            dst_i = sbt("dst_i", [P, EP], i32)
            dstf = sbt("dstf", [P, EP + 1])
            prev_i = sbt("prev_i", [P, 1], i32)
            keep = sbt("keep", [P, EP])
            dirv = sbt("dirv", [P, EP * 3])
            sq = sbt("sq", [P, EP * 3])
            s2 = sbt("s2", [P, EP])
            rn = sbt("rn", [P, EP])
            samp_b = sbt("samp_b", [P, NSB])
            node_i = sbt("node_i", [P, NP], i32)
            nodef = sbt("nodef", [P, NP])
            NF = 4
            junk = sbt("junk", [P, NF * SB], mybir.dt.bfloat16)
            cnt = sbt("cnt", [P, NP])
            blk_i = sbt("blk_i", [P, NP], i32)
            fine = sbt("fine", [P, NP])
            blkbuf = sbt("blkbuf", [P, NF * SB])
            w2s = sbt("w2s", [HID, 7 * 128])
            zeros = sbt("zeros", [P, 3200])
            w2x = sbt("w2x", [HID, NOUT * KF])
            w2d = sbt("w2d", [HID, NOUT * 4 * KF])
            w_hi = sbt("w_hi", [128, NOUT * HID], f32r)
            w1x = sbt("w1x", [128, 3 * 128])
            w1_hi = sbt("w1_hi", [128, 3 * 128], f32r)
            wr = sbt("wr", [HID, 128])
            head_row = sbt("head_row", [P, P])
            diag = sbt("diag", [P, P])
            part_i = sbt("part_i", [P, 1], i32)
            partf = sbt("partf", [P, 1])
            endh = sbt("endh", [P, 1])
            idx1 = sbt("idx1", [P, 1], i32)
            t1 = sbt("t1", [P, 4])
            tn = sbt("tn", [P, 4 * NP])

            with nc.Block() as block:
                @block.sync
                def _(sp):
                    sp.dma_start(dst_i[:, :], edges(dst, 1)).then_inc(S("a_dst"), 16)
                    sp.wait_ge(S("a_prev0"), 1)
                    sp.dma_start(prev_i[1:P, :], dst.rearrange("(p c) -> p c", c=EP)[0:P - 1, EP - 1:EP], allow_slow_non_contiguous=True).then_inc(S("a_prev"), 16)
                    sp.dma_start(dirv[:, :], vec.rearrange("(p c) f -> p (c f)", c=EP)).then_inc(S("a_vec"), 16)
                    sp.dma_start(xn[:, :], x.rearrange("(p k) f -> p (k f)", k=NP)).then_inc(S("a_x"), 16)
                    sp.dma_start(w2s[:, :], W2).then_inc(S("a_w"), 16)
                    sp.dma_start(attn_b[:, :], attn.rearrange("(a f) -> a f", a=1).broadcast_to([P, 2 * DIM])).then_inc(S("a_w"), 16)
                    sp.wait_ge(S("a_wh0"), 1)
                    for i in range(4):
                        row = KF * i + QF - 2 * KF
                        for half in range(2):
                            sp.dma_start(w1x[row:row + NEMB, half * 128:(half + 1) * 128].rearrange("k (w j) -> k w j", j=HJ),
                                         W1[:, half * HJ:(half + 1) * HJ].rearrange("k (w j) -> k w j", w=1).broadcast_to([NEMB, 2 * MO, HJ])).then_inc(S("a_w1"), 16)
                        sp.dma_start(w1x[row:row + NEMB, 256:384].rearrange("k (w j) -> k w j", j=HID),
                                     W1.rearrange("k (w j) -> k w j", w=1).broadcast_to([NEMB, MO, HID])).then_inc(S("a_w1"), 16)
                    sp.wait_ge(S("a_dstf"), 1)
                    sp.dma_start(dstf_d.rearrange("a b -> (a b)").rearrange("(p c) -> p c", c=EP), dstf[:, 1:]).then_inc(S("a_dstd"), 16)
                    sp.wait_ge(S("a_dstd"), 16)
                    sp.dma_start(samp_d.rearrange("(a b) -> a b", b=1), dstf_d[:, 0:1], allow_slow_non_contiguous=True).then_inc(S("a_samp"), 16)
                    sp.wait_ge(S("a_samp"), 16)
                    sp.dma_start(samp_b[:, :], samp_d.rearrange("(a b) -> a b", a=1).broadcast_to([P, NSB])).then_inc(S("a_sampb"), 16)
                    sp.wait_ge(S("a_zero"), 1)
                    for i in range(EP * DIM // 3200):
                        sp.dma_start(xd_d.rearrange("(p c) f -> p (c f)", c=EP)[:, i * 3200:(i + 1) * 3200], zeros[:, :]).then_inc(S("a_xd0"), 16)
                    sp.dma_start(sd_d.rearrange("(p c) a -> p (c a)", c=EP), zeros[:, 0:EP]).then_inc(S("a_xd0"), 16)
                    sp.dma_start(y0_d[E:E + PAD, :].rearrange("(a b) f -> a (b f)", a=64), zeros[0:64, 0:4 * DIM]).then_inc(S("a_pad"), 16)
                    sp.dma_start(y1_d[E:E + PAD, :].rearrange("(a b) f -> a (b f)", a=64), zeros[0:64, 0:4 * R1]).then_inc(S("a_pad"), 16)
                    sp.dma_start(end_d[0:1, :], zeros[0:1, 0:1]).then_inc(S("a_end"), 16)
                    sp.wait_ge(S("a_endf"), 1)
                    sp.dma_start(end_d[1:N + 1, :].rearrange("(p k) a -> p (k a)", k=NP), endf[:, :]).then_inc(S("a_end"), 16)
                    sp.wait_ge(S("a_end"), 32)
                    sp.dma_start(startf[:, :], end_d[0:N, :].rearrange("(p k) a -> p (k a)", k=NP)).then_inc(S("a_start"), 16)
                    sp.wait_ge(S("a_keep"), 1)
                    sp.dma_start(keep_d.rearrange("(p c) -> p c", c=EP), keep[:, :]).then_inc(S("a_out"), 16)
                    sp.wait_ge(S("a_dir"), 1)
                    sp.dma_start(dir_d.rearrange("(p c) f -> p (c f)", c=EP), dirv[:, :]).then_inc(S("a_out"), 16)
                    sp.wait_ge(S("a_out"), 32)
                    sp.wait_ge(S("a_pad"), 32)

                @block.gpsimd
                def _(pool):
                    nc.gpsimd.memset(prev_i[:, :], -1).then_inc(S("a_prev0"), 1)
                    nc.gpsimd.memset(ones[:, :], 1.0).then_inc(S("a_ones"), 1)
                    nc.gpsimd.memset(ident[:, :], 0.0).then_inc(S("a_id"), 1)
                    pool.wait_ge(S("a_id"), 1)
                    nc.gpsimd.affine_select(out=ident[:, :], in_=ident[:, :], compare_op=ALU.not_equal, fill=1.0, base=0,
                                            pattern=[[-1, 128]], channel_multiplier=1).then_inc(S("a_id"), 1)
                    nc.gpsimd.iota(node_i[:, :], [[1, NP]], base=0, channel_multiplier=NP).then_inc(S("a_iota"), 1)
                    nc.gpsimd.iota(part_i[:, :], [[0, 1]], base=0, channel_multiplier=1).then_inc(S("a_iota"), 1)
                    nc.gpsimd.memset(red[:, :], 0.0).then_inc(S("a_red"), 1)
                    pool.wait_ge(S("a_red"), 1)
                    nc.gpsimd.memset(w1x[:, :], 0.0).then_inc(S("a_wh0"), 1)
                    for b, (o0, nw, nj) in enumerate(((0, 2 * MO, HJ), (3 * MO, 2 * MO, HJ), (2 * MO, MO, HID), (5 * MO, MO, HID))):
                        blk = red[:, b * NOUT + o0:b * NOUT + o0 + nw]
                        nc.gpsimd.memset(blk, 1.0).then_inc(S("a_red"), 1)
                        pool.wait_ge(S("a_red"), 3 * b + 2)
                        nc.gpsimd.affine_select(out=blk, in_=blk, compare_op=ALU.is_ge, fill=0.0, base=0,
                                                pattern=[[-nj, nw]], channel_multiplier=1).then_inc(S("a_red"), 1)
                        pool.wait_ge(S("a_red"), 3 * b + 3)
                        nc.gpsimd.affine_select(out=blk, in_=blk, compare_op=ALU.is_ge, fill=0.0, base=nj - 1,
                                                pattern=[[nj, nw]], channel_multiplier=-1).then_inc(S("a_red"), 1)
                    pool.wait_ge(S("a_head"), 1)
                    pool.wait_ge(S("a_blk"), 1)
                    for k in range(NP):
                        if k >= NF:
                            pool.wait_ge(S("a_fine"), k - NF + 1)
                        nc.gpsimd.indirect_dma_start(out=blkbuf[:, (k % NF) * SB:(k % NF + 1) * SB], out_offset=None, in_=dstf_d,
                                                     in_offset=bass.IndirectOffsetOnAxis(blk_i[:, k:k + 1], 0)).then_inc(S(f"a_fg{k % NF}"), 16)
                    pool.wait_ge(S("a_idx"), 1)
                    pool.wait_ge(S("a_x"), 16)
                    pool.wait_ge(S("a_xd0"), 16 * (EP * DIM // 3200 + 1))
                    for k in range(NP):
                        nc.gpsimd.indirect_dma_start(out=xd_d, out_offset=bass.IndirectOffsetOnAxis(first_i[:, k:k + 1], 0),
                                                     in_=xn[:, k * DIM:(k + 1) * DIM], in_offset=None,
                                                     bounds_check=E - 1, oob_is_err=False).then_inc(S("a_xd"), 16)
                    pool.wait_ge(S("a_idx1"), 1)
                    nc.gpsimd.indirect_dma_start(out=endh[:, :], out_offset=None, in_=end_d,
                                                 in_offset=bass.IndirectOffsetOnAxis(idx1[:, :], 0)).then_inc(S("a_endh"), 16)
                    nc.gpsimd.indirect_dma_start(out=hx_keep[:, :], out_offset=None, in_=x,
                                                 in_offset=bass.IndirectOffsetOnAxis(head_i[:, :], 0)).then_inc(S("a_hx"), 16)
                    pool.wait_ge(S("a_xd"), 16 * NP)
                    pool.wait_ge(S("a_hx"), 16)
                    pool.wait_ge(S("a_link0"), 2)
                    nc.gpsimd.affine_select(out=link[:, :], in_=link[:, :], compare_op=ALU.is_gt, fill=0.0, base=0,
                                            pattern=[[1, P]], channel_multiplier=-1).then_inc(S("a_link"), 1)
                    pool.wait_ge(S("a_link"), 1)

                @block.vector
                def _(dve):
                    n = [0]

                    def step(ins):
                        n[0] += 1
                        ins.then_inc(S("a_dve"), 1)
                        dve.wait_ge(S("a_dve"), n[0])

                    V = nc.vector
                    V.memset(zeros[:, :], 0.0).then_inc(S("a_zero"), 1)
                    dve.wait_ge(S("a_dst"), 16)
                    V.tensor_copy(dstf[:, 1:], dst_i[:, :]).then_inc(S("a_dstf"), 1)
                    dve.wait_ge(S("a_prev"), 16)
                    step(V.tensor_copy(dstf[:, 0:1], prev_i[:, :]))
                    dve.wait_ge(S("a_dstf"), 1)
                    V.tensor_tensor(keep[:, :], dstf[:, 1:], dstf[:, 0:EP], ALU.is_equal).then_inc(S("a_keep"), 1)
                    V.tensor_copy(headf[:, :], dstf[:, 1:2])
                    V.tensor_copy(tailf[:, :], dstf[:, EP:EP + 1])
                    V.tensor_copy(head_i[:, :], dst_i[:, 0:1])
                    step(V.tensor_scalar(idx1[:, :], dstf[:, 1:2], 1.0, None, ALU.add))
                    V.memset(w2x[:, :], 0.0).then_inc(S("a_head"), 1)
                    dve.wait_ge(S("a_iota"), 2)
                    V.tensor_copy(partf[:, :], part_i[:, :])
                    step(V.tensor_copy(nodef[:, :], node_i[:, :]))
                    dve.wait_ge(S("a_sampb"), 16)
                    for k in range(NP):
                        if k >= NF:
                            dve.wait_ge(S("a_coarse"), k - NF + 1)
                        V.tensor_scalar(junk[:, (k % NF) * SB:(k % NF) * SB + NSB], samp_b[:, :], nodef[:, k:k + 1], None, ALU.is_le, ALU.add,
                                        accum_out=cnt[:, k:k + 1]).then_inc(S("a_coarse"), 1)
                    dve.wait_ge(S("a_coarse"), NP)
                    step(V.tensor_scalar(tn[:, 0:NP], cnt[:, :], -1.0, 0.0, ALU.add, ALU.max))
                    V.tensor_copy(blk_i[:, :], tn[:, 0:NP]).then_inc(S("a_blk"), 1)
                    for k in range(NP):
                        dve.wait_ge(S(f"a_fg{k % NF}"), 16 * (k // NF + 1))
                        if k >= NF:
                            dve.wait_ge(S("a_fine"), k - NF + 1)
                        V.tensor_scalar(junk[:, (k % NF) * SB:(k % NF + 1) * SB], blkbuf[:, (k % NF) * SB:(k % NF + 1) * SB], nodef[:, k:k + 1], None,
                                        ALU.is_le, ALU.add, accum_out=fine[:, k:k + 1]).then_inc(S("a_fine"), 1)
                    dve.wait_ge(S("a_fine"), NP)
                    V.scalar_tensor_tensor(endf[:, :], tn[:, 0:NP], float(SB), fine[:, :], ALU.mult, ALU.add).then_inc(S("a_endf"), 1)
                    dve.wait_ge(S("a_endf"), 1)
                    dve.wait_ge(S("a_start"), 16)
                    step(V.tensor_tensor(empty[:, :], endf[:, :], startf[:, :], ALU.is_equal))
                    V.scalar_tensor_tensor(first_i[:, :], empty[:, :], float(E), startf[:, :], ALU.mult, ALU.add).then_inc(S("a_idx"), 1)
                    step(V.tensor_scalar(tn[:, 0:NP], endf[:, :], -1.0, float(ZROW + 1), ALU.mult, ALU.add))
                    step(V.tensor_tensor(tn[:, NP:2 * NP], tn[:, 0:NP], empty[:, :], ALU.mult))
                    step(V.scalar_tensor_tensor(last_i[:, :], endf[:, :], -1.0, tn[:, NP:2 * NP], ALU.add, ALU.add))
                    V.tensor_scalar(t1[:, 3:4], headf[:, :], 0.0, None, ALU.add).then_inc(S("a_idx1"), 1)

                    dve.wait_ge(S("a_w"), 32)
                    dve.wait_ge(S("a_head"), 1)
                    w2v = w2s[:, :].rearrange("j (i u w) -> j i w u", i=7, w=MO)
                    w2o = w2x[:, :].rearrange("j (o w f) -> j o w f", o=6, f=KF)
                    wrv = wr[:, :].rearrange("j (w u) -> j w u", w=MO)
                    step(V.tensor_scalar(wrv, w2v[:, 6], -KV * C121 / 3.0, None, ALU.mult))
                    step(V.scalar_tensor_tensor(wrv, w2v[:, 5], KV * INV3, wrv, ALU.mult, ALU.add))
                    for o, f0, i, k in ((0, 0, 0, KS), (0, 16, 1, KS * INV3 * 3.0 ** 0.5), (1, 0, 2, KS),
                                        (1, 16, 3, KS * INV3 * 3.0 ** 0.5), (4, 0, 4, KV * INV3 * 3.0 ** 0.5), (4, 16, 6, KV * C121)):
                        V.tensor_scalar(w2o[:, o, :, f0:f0 + 16], w2v[:, i], k, None, ALU.mult).then_inc(S("a_w2x"), 1)
                    for o, f0 in ((2, 0), (3, 16), (5, 0)):
                        V.tensor_copy(w2o[:, o, :, f0:f0 + 16], wrv).then_inc(S("a_w2x"), 1)
                    dve.wait_ge(S("a_w2x"), 9)
                    V.tensor_copy(w2d[:, :].rearrange("j (o a f) -> j o a f", a=4, f=KF),
                                  w2x[:, :].rearrange("j (o a f) -> j o a f", a=1, f=KF).broadcast_to([HID, NOUT, 4, KF])).then_inc(S("a_w2d"), 1)
                    dve.wait_ge(S("a_vec"), 16)
                    step(V.tensor_tensor(sq[:, :], dirv[:, :], dirv[:, :], ALU.mult))
                    V.tensor_reduce(s2[:, :], sq[:, :].rearrange("p (c a) -> p c a", a=3), AX.X, ALU.add).then_inc(S("a_s2"), 1)
                    dve.wait_ge(S("a_sqrt"), 1)
                    step(V.reciprocal(rn[:, :], s2[:, :]))
                    V.tensor_tensor(dirv[:, :].rearrange("p (c a) -> p c a", a=3), dirv[:, :].rearrange("p (c a) -> p c a", a=3),
                                    rn[:, :].rearrange("p (c a) -> p c a", a=1).broadcast_to([P, EP, 3]), ALU.mult).then_inc(S("a_dir"), 1)
                    dve.wait_ge(S("a_wt"), 1)
                    wp = G_ps[0][:, 0:NOUT * HID]
                    step(V.tensor_copy(w_hi[:, :], wp))
                    dve.wait_ge(S("a_w1"), 16 * 12)
                    step(V.tensor_copy(w1_hi[:, :], w1x[:, :]))
                    for q0 in (0, 64):
                        rows = slice(q0, q0 + 64)
                        for pair in range(2):
                            o = wst[rows, pair * 256:(pair + 1) * 256].rearrange("p (a w j) -> p a w j", a=2, j=HJ)
                            hi = w_hi[rows, pair * 256:(pair + 1) * 256].rearrange("p (w a j) -> p a w j", a=2, j=HJ)
                            if q0 == 0:
                                V.tensor_copy(o, hi)
                            else:
                                V.tensor_tensor(o, wp[rows, pair * 256:(pair + 1) * 256].rearrange("p (w a j) -> p a w j", a=2, j=HJ), hi.bitcast(f32), ALU.subtract)
                        if q0 == 0:
                            V.tensor_copy(wst[rows, 512:768], w_hi[rows, 512:768])
                            V.tensor_copy(wh[rows, :], w1_hi[rows, :])
                        else:
                            V.tensor_tensor(wst[rows, 512:768], wp[rows, 512:768], w_hi[rows, 512:768].bitcast(f32), ALU.subtract)
                            step(V.tensor_tensor(wh[rows, :], w1x[rows, :], w1_hi[rows, :].bitcast(f32), ALU.subtract))
                    step(V.tensor_scalar(diag[:, :], ident[0:P, 0:P], headf[:, :], None, ALU.mult))
                    V.memset(t1[:, 0:1], 0.0).then_inc(S("a_diag"), 1)
                    dve.wait_ge(S("a_hrow"), 1)
                    V.tensor_scalar(link[:, :], R_ps[0:P, 0:P], tailf[:, :], None, ALU.is_equal).then_inc(S("a_link0"), 2)
                    dve.wait_ge(S("a_linkT"), 1)
                    V.tensor_copy(linkT[:, :], Y_ps[0:P, 0:P])
                    dve.wait_ge(S("a_endh"), 16)
                    step(V.tensor_scalar(t1[:, 0:1], partf[:, :], float(EP), float(EP), ALU.mult, ALU.add))
                    step(V.tensor_tensor(t1[:, 1:2], endh[:, :], t1[:, 0:1], ALU.is_le))
                    step(V.tensor_scalar(t1[:, 2:3], partf[:, :], float(E + 1), None, ALU.add))
                    step(V.tensor_tensor(t1[:, 0:1], endh[:, :], t1[:, 2:3], ALU.subtract))
                    step(V.tensor_tensor(t1[:, 0:1], t1[:, 0:1], t1[:, 1:2], ALU.mult))
                    step(V.scalar_tensor_tensor(fix_i[:, :], t1[:, 2:3], -1.0, t1[:, 0:1], ALU.add, ALU.add))

                @block.scalar
                def _(act):
                    act.wait_ge(S("a_s2"), 1)
                    nc.scalar.activation(s2[:, :], s2[:, :], ACT.Sqrt).then_inc(S("a_sqrt"), 1)

                @block.tensor
                def _(pe):
                    pe.wait_ge(S("a_id"), 2)
                    pe.wait_ge(S("a_w2d"), 1)
                    for o in range(NOUT):
                        last = nc.tensor.transpose(G_ps[0][:, o * HID:(o + 1) * HID],
                                                   w2d[:, o * 4 * KF:(o + 1) * 4 * KF], ident[0:HID, 0:HID])
                    last.then_inc(S("a_wt"), 1)
                    pe.wait_ge(S("a_ones"), 1)
                    pe.wait_ge(S("a_diag"), 1)
                    nc.tensor.matmul(R_ps[0:P, 0:P], ones[0:P, 0:P], diag[:, :], start=True, stop=True).then_inc(S("a_hrow"), 1)
                    pe.wait_ge(S("a_link"), 1)
                    nc.tensor.transpose(Y_ps[0:P, 0:P], link[:, :], ident[0:P, 0:P]).then_inc(S("a_linkT"), 1)

        with ExitStack() as st:
            def sbt(name, shape, dt=f32):
                return st.enter_context(nc.sbuf_tensor(name, shape, dt))

            def two(name, w, dt=f32):
                return [sbt(f"{name}_{h}", [P, w], dt) for h in range(2)]

            idx = two("idx", C, i32)
            gx = two("gx", C * DIM)
            xv = two("xv", C * DIM)
            em = two("em", C * NEMB)
            dr = two("dr", C * 3)
            kp = two("kp", C)
            drp = two("drp", C * 3)
            kpp = two("kpp", C)
            nmp = two("nmp", C)
            F = two("F", C * FW)
            PCG = 2
            PCW = PCG * GT
            HL = [sbt(f"HL{h}", [P, PCW * 4 * FW], f32r) for h in range(2)]
            O = two("O", C * DIM)
            Z = two("Z", C * DIM)
            tmp = sbt("tmp", [P, C * 48])
            FT = [sbt(f"FT{k}", [128, NT * GW], f32r) for k in range(2)]
            hid = [sbt(f"hid{k}", [128, 3 * GW]) for k in range(2)]
            psg = sbt("psg", [128, 2 * GW])
            pxy = sbt("pxy", [128, 2 * GW])
            ppz = [sbt(f"ppz{k}", [128, 2 * GW]) for k in range(2)]
            sums2 = [sbt(f"sums{k}", [128, 2 * GW]) for k in range(2)]
            rt = [sbt(f"rt{k}", [NOUT, GW]) for k in range(2)]
            W2G = 2 * GT
            th = sbt("th", [P, W2G * 16])
            pa = sbt("pa", [P, W2G * 24])
            pb = sbt("pb", [P, W2G * 24])
            pg = sbt("pg", [P, W2G * MO])

            Fv = [a[:, :].rearrange("p (c f) -> p c f", f=FW) for a in F]
            HLv = [a[:, :].rearrange("p (ct r s f) -> p ct r s f", r=2, s=2, f=KF) for a in HL]

            def col(f):
                if f < 8:
                    return 8 + f
                u, a = divmod(f - 8, 3)
                return 32 + 16 * a + 8 + u

            def some(n):
                return not isinstance(n, int) or n > 0

            NPC = 4
            PCF = DIM // NPC
            SP = GC // PCG
            AHEAD = 3
            NG = PAIRS * G2
            NCH = 2 * PAIRS

            with nc.Block() as block:
                @block.sync
                def _(sp):
                    def hold(s, n):
                        sp.wait_ge(s, n)
                        sp.sem_inc(S("go_sp"), 1)

                    def load(ch, h, t):
                        if not isinstance(ch, int) or ch > 1:
                            hold(S("b_fa"), ch * 3 - 3)
                        sp.dma_start(idx[h][:, :], edges(src, 1)[:, bass.ds(ch * C, C)]).then_inc(S(f"b_idx{h}"), 16)
                        sp.dma_start(em[h][:, :], emb.rearrange("(p c) f -> p (c f)", c=EP)[:, bass.ds(ch * C * NEMB, C * NEMB)]).then_inc(S(f"b_ld{h}"), 16)
                        if not isinstance(ch, int) or ch > 1:
                            hold(S("b_d"), ch * 3 - 3)
                        sp.dma_start(xv[h][:, :], xd_d.rearrange("(p c) f -> p (c f)", c=EP)[:, bass.ds(ch * C * DIM, C * DIM)]).then_inc(S(f"b_ld{h}"), 16)
                        sp.dma_start(dr[h][:, :], dir_d.rearrange("(p c) f -> p (c f)", c=EP)[:, bass.ds(ch * C * 3, C * 3)]).then_inc(S(f"b_ld{h}"), 16)
                        sp.dma_start(kp[h][:, :], edges(keep_d, 1)[:, bass.ds(ch * C, C)]).then_inc(S(f"b_ld{h}"), 16)

                    def load_post(ch, h):
                        sp.dma_start(drp[h][:, :], dir_d.rearrange("(p c) f -> p (c f)", c=EP)[:, bass.ds(ch * C * 3, C * 3)]).then_inc(S(f"b_lp{h}"), 16)
                        sp.dma_start(kpp[h][:, :], edges(keep_d, 1)[:, bass.ds(ch * C, C)]).then_inc(S(f"b_lp{h}"), 16)
                        sp.dma_start(nmp[h][:, :], edges(weight, 1)[:, bass.ds(ch * C, C)]).then_inc(S(f"b_lp{h}"), 16)

                    def store(ch, h, t):
                        hold(S(f"b_z{h}"), t * NPC + NPC)
                        sp.dma_start(y0_d[0:E, :].rearrange("(p c) f -> p (c f)", c=EP)[:, bass.ds(ch * C * DIM, C * DIM)], Z[h][:, :]).then_inc(S(f"b_st{h}"), 16)
                        hold(S(f"b_st{h}"), t * 16 + 16)

                    def turn(t, first=False, last=False):
                        for h in range(2):
                            if not last:
                                load(t * 2 + h + 2, h, t + 1)
                            if not (first and h == 0):
                                store(t * 2 + h - 1, 1 - h, t - 1 + h)
                                if not (last and h == 1):
                                    load_post(t * 2 + h + 1, 1 - h)

                    for h in range(2):
                        load(h, h, 0)
                        load_post(h, h)
                    turn(0, first=True)
                    with sp.Fori(1, PAIRS - 1) as t:
                        turn(t)
                    turn(PAIRS - 1, last=True)
                    store(2 * PAIRS - 1, 1, PAIRS - 1)

                @block.gpsimd
                def _(pool):
                    with pool.Fori(0, PAIRS) as t:
                        for h in range(2):
                            pool.wait_ge(S(f"b_idx{h}"), t * 16 + 16)
                            pool.sem_inc(S("go_pool"), 1)
                            for c in range(C):
                                nc.gpsimd.indirect_dma_start(out=gx[h][:, c * DIM:(c + 1) * DIM], out_offset=None, in_=x,
                                                             in_offset=bass.IndirectOffsetOnAxis(idx[h][:, c:c + 1], 0)).then_inc(S(f"b_gx{h}"), 16)

                @block.scalar
                def _(act):
                    A = nc.scalar
                    HSCALE = (2.0 / NEMB) ** 0.5

                    def copy_rows(i, ch, h, t):
                        g = gx[h][:, :].rearrange("p (c f) -> p c f", f=DIM)
                        if i == 0:
                            act.wait_ge(S(f"b_gx{h}"), t * 16 * C + 16 * C)
                            if not isinstance(ch, int) or ch > 1:
                                act.wait_ge(S("b_lo"), ch * SP - SP)
                            A.activation(Fv[h][:, :, 0:8], g[:, :, 0:8], ACT.Copy).then_inc(S("b_fa"), 1)
                        if i == 1:
                            A.activation(Fv[h][:, :, 32:80].rearrange("p c (a u) -> p c a u", a=3)[:, :, :, 0:8],
                                         g[:, :, 8:32].rearrange("p c (u a) -> p c a u", a=3), ACT.Copy).then_inc(S("b_fa"), 1)
                        if i == 2:
                            act.wait_ge(S(f"b_ld{h}"), t * 64 + 64)
                            A.activation(Fv[h][:, :, QF:FD], em[h][:, :].rearrange("p (c f) -> p c f", f=NEMB), ACT.Copy).then_inc(S("b_fa"), 1)

                    def high(pc, q, ch, h):
                        if q == 0:
                            act.wait_ge(S("b_d"), ch * 3 + 3)
                            act.wait_ge(S("b_fa"), ch * 3 + 3)
                        if not isinstance(pc, int) or pc > 1:
                            act.wait_ge(S("b_T"), (pc * PCG - PCG) * NT)
                        A.activation(HLv[(h * SP + q) % 2][:, :, :, 0, :],
                                     F[h][:, q * PCW * FW:(q + 1) * PCW * FW].rearrange("p (ct r f) -> p ct r f", r=1, f=KF).broadcast_to([P, PCW * NT, 2, KF]),
                                     ACT.Copy).then_inc(S("b_hi"), 1)

                    def low_again(pc, q, h):
                        act.wait_ge(S("b_lo"), pc + 1)
                        v = HLv[(h * SP + q) % 2]
                        A.activation(v[:, :, 1, 1, :], v[:, :, 0, 1, :].bitcast(f32), ACT.Copy).then_inc(S("b_lo2"), 1)

                    def out_of_T(n, k, i):
                        act.wait_ge(S("b_T"), n * NT + i + 1)
                        if i == 0 and (not isinstance(n, int) or n > 1):
                            act.wait_ge(S("b_G"), n * 3 - 3)
                        A.activation(FT[k][:, i * GW:(i + 1) * GW], T_ps[:, 0:GW], ACT.Copy).then_inc(S("b_FT"), 1)

                    def relu(n, k, i):
                        act.wait_ge(S("b_H"), n * 3 + i + 1)
                        if i == 0 and (not isinstance(n, int) or n > 1):
                            act.wait_ge(S("b_mul"), n * 3 - 3)
                        A.activation(hid[k][:, i * GW:(i + 1) * GW], H_ps[:, 0:GW], ACT.Relu, scale=HSCALE).then_inc(S("b_hid"), 1)

                    def out_of_R(n, k):
                        act.wait_ge(S("b_R"), n + 1)
                        if not isinstance(n, int) or n > 1:
                            act.wait_ge(S("b_Y"), n - 1)
                        A.activation(rt[k][:, :], R_ps[0:NOUT, 0:GW], ACT.Copy).then_inc(S("b_rt"), 1)

                    def tanh(m):
                        act.wait_ge(S("b_Y"), m * 2 + 2)
                        if some(m):
                            act.wait_ge(S("b_gs"), m * 2)
                        A.activation(th[:, :].rearrange("p (c f) -> p c f", f=16),
                                     Y_ps[0:P, 0:W2G * NOUT].rearrange("p (c f) -> p c f", f=NOUT)[:, :, 0:16], ACT.Tanh).then_inc(S("b_th"), 1)

                    def turn(t, first=False, last=False):
                        for g in range(G2):
                            n, k, gc, h = t * G2 + g, g % 2, g % GC, g // GC
                            more = not (last and g == G2 - 1)
                            if g % 2 == 0 and not (first and g < 4):
                                tanh(t * GC + (g - 4) // 2)
                            if more:
                                out_of_T(n + 1, 1 - k, 0)
                                out_of_T(n + 1, 1 - k, 1)
                                out_of_T(n + 1, 1 - k, 2)
                            split = (g + AHEAD) // PCG
                            sh, sq = split // SP % 2, split % SP
                            if g % 2 == 1 and not (last and g + AHEAD >= G2):
                                high(t * 2 * SP + split, sq, t * 2 + split // SP, sh)
                            if more:
                                relu(n + 1, 1 - k, 0)
                                relu(n + 1, 1 - k, 1)
                            if g % 2 == 0 and not (last and g - 1 + AHEAD >= G2) and not (first and g == 0):
                                low_again(t * 2 * SP + split, sq, sh)
                            if more:
                                relu(n + 1, 1 - k, 2)
                            if not (first and g == 0):
                                out_of_R(n - 1, 1 - k)
                            if not (last and h == 1) and gc < 3:
                                copy_rows(gc, t * 2 + h + 1, 1 - h, t + h)

                    act.wait_ge(S("b_init"), 5)
                    for i in range(3):
                        copy_rows(i, 0, 0, 0)
                    for i in range(2):
                        high(i, i, 0, 0)
                        low_again(i, i, 0)
                    for i in range(NT):
                        out_of_T(0, 0, i)
                    for i in range(3):
                        relu(0, 0, i)
                    turn(0, first=True)
                    with act.Fori(1, PAIRS - 1) as t:
                        turn(t)
                    turn(PAIRS - 1, last=True)
                    tanh(NG // 2 - 2)
                    out_of_R(NG - 1, 1)
                    tanh(NG // 2 - 1)

                @block.tensor
                def _(pe):
                    Tn = nc.tensor

                    def transposes(n, g, pc, i):
                        if i == 0 and g % PCG == 0:
                            pe.wait_ge(S("b_lo2"), pc + 1)
                        if some(n) or i > 0:
                            pe.wait_ge(S("b_FT"), n * NT + i)
                        for c in range(GT):
                            col0 = ((g % PCG * GT + c) * NT + i) * 128
                            last = Tn.transpose(T_ps[:, c * P:(c + 1) * P], HL[g // PCG % 2][:, col0:col0 + 128].bitcast(f32), ident[0:P, 0:P])
                        last.then_inc(S("b_T"), 1)

                    def hidden(n, k, i):
                        pe.wait_ge(S("b_FT"), n * NT + NT)
                        if some(n) or i > 0:
                            pe.wait_ge(S("b_hid"), n * 3 + i)
                        Tn.matmul(H_ps[:, 0:GW], wh[:, i * 128:(i + 1) * 128], FT[k][:, 2 * GW:3 * GW], start=True, stop=True).then_inc(S("b_H"), 1)

                    def product(n, k, i):
                        if not isinstance(n, int) or 3 * n + i > 1:
                            pe.wait_ge(S("b_mul"), n * 3 + i - 1)
                        q = G_ps[(k * 3 + i) % 2]
                        for j in range(2):
                            tile = (0, 1, 2 * j)[i]
                            last = Tn.matmul(q[:, j * 512:j * 512 + GW], wst[:, (2 * i + j) * 128:(2 * i + j + 1) * 128],
                                             FT[k][:, tile * GW:(tile + 1) * GW], start=True, stop=True)
                        last.then_inc(S("b_G"), 1)

                    def reduce(n, k, i):
                        if i == 0:
                            pe.wait_ge(S("b_add"), n * 2 + 1)
                            if some(n):
                                pe.wait_ge(S("b_rt"), n)
                        if i == 1:
                            pe.wait_ge(S("b_add"), n * 2 + 2)
                        if i == 2:
                            pe.wait_ge(S("b_mul"), n * 3 + 3)
                        a = sums2[k] if i < 2 else ppz[k]
                        j = i % 2
                        last = Tn.matmul(R_ps[0:NOUT, 0:GW], red[:, i * NOUT:(i + 1) * NOUT], a[:, j * GW:(j + 1) * GW], start=(i == 0), stop=(i == 3))
                        if i == 3:
                            last.then_inc(S("b_R"), 1)

                    def back(n, k):
                        pe.wait_ge(S("b_rt"), n + 1)
                        if k == 0 and some(n):
                            pe.wait_ge(S("b_yr"), n)
                        pe.sem_inc(S("go_pe"), 1)
                        for c in range(GT):
                            last = Tn.transpose(Y_ps[0:P, (k * GT + c) * NOUT:(k * GT + c + 1) * NOUT], rt[k][:, c * P:(c + 1) * P], ident[0:NOUT, 0:NOUT])
                        last.then_inc(S("b_Y"), 1)

                    def turn(t, first=False, last=False):
                        for g in range(G2):
                            n, k = t * G2 + g, g % 2
                            before = not (first and g == 0)
                            more = not (last and g == G2 - 1)
                            g1, pc1 = (g + 1) % G2, t * 2 * SP + (g + 1) // PCG
                            product(n, k, 0)
                            if more:
                                transposes(n + 1, g1, pc1, 0)
                            if before:
                                reduce(n - 1, 1 - k, 0)
                            if more:
                                transposes(n + 1, g1, pc1, 1)
                            product(n, k, 1)
                            if before:
                                reduce(n - 1, 1 - k, 1)
                            if more:
                                transposes(n + 1, g1, pc1, 2)
                            if before:
                                reduce(n - 1, 1 - k, 2)
                            if more:
                                hidden(n + 1, 1 - k, 0)
                            product(n, k, 2)
                            if more:
                                hidden(n + 1, 1 - k, 1)
                            if before:
                                reduce(n - 1, 1 - k, 3)
                            if more:
                                hidden(n + 1, 1 - k, 2)
                            if not (first and g < 2):
                                back(n - 2, k)

                    for i in range(NT):
                        transposes(0, 0, 0, i)
                    for i in range(3):
                        hidden(0, 0, i)
                    turn(0, first=True)
                    with pe.Fori(1, PAIRS - 1) as t:
                        turn(t)
                    turn(PAIRS - 1, last=True)
                    back(NG - 2, 0)
                    for i in range(4):
                        reduce(NG - 1, 1, i)
                    back(NG - 1, 1)

                @block.vector
                def _(dve):
                    V = nc.vector

                    def fill(i, ch, h, t):
                        if i == 0:
                            dve.wait_ge(S(f"b_ld{h}"), t * 64 + 64)
                            if not isinstance(ch, int) or ch > 1:
                                dve.wait_ge(S("b_lo"), ch * SP - SP)
                                dve.wait_ge(S("b_hi"), ch * SP - SP)
                            if some(ch):
                                dve.wait_ge(S("b_fs"), ch * NPC)
                        xvv = xv[h][:, :].rearrange("p (c f) -> p c f", f=DIM)
                        for f in range(i * PCF, (i + 1) * PCF):
                            last = V.tensor_tensor_scan(out=Fv[h][:, :, col(f)], data0=kp[h][:, :], data1=xvv[:, :, f],
                                                        initial=Fv[1 - h][:, C - 1, col(f):col(f) + 1], op0=ALU.mult, op1=ALU.add)
                        last.then_inc(S("b_fs"), 1)

                    tv = tmp[:, :].rearrange("p (c a u) -> p c a u", a=3, u=16)

                    def along(i, ch, h, t):
                        if i == 0:
                            dve.wait_ge(S("b_fs"), ch * NPC + NPC)
                            dve.wait_ge(S("b_fa"), ch * 3 + 2)
                            V.tensor_tensor(tv, Fv[h][:, :, 32:80].rearrange("p c (a u) -> p c a u", a=3),
                                            dr[h][:, :].rearrange("p (c a u) -> p c a u", a=3, u=1).broadcast_to([P, C, 3, 16]), ALU.mult).then_inc(S("b_d"), 1)
                        else:
                            dve.wait_ge(S("b_d"), ch * 3 + i)
                            first = tv[:, :, 0] if i == 1 else Fv[h][:, :, 16:32]
                            V.tensor_tensor(Fv[h][:, :, 16:32], first, tv[:, :, i], ALU.add).then_inc(S("b_d"), 1)

                    def low(pc, q, h):
                        dve.wait_ge(S("b_hi"), pc + 1)
                        v = HLv[(h * SP + q) % 2]
                        V.tensor_tensor(v[:, :, 0, 1, :], F[h][:, q * PCW * FW:(q + 1) * PCW * FW].rearrange("p (ct f) -> p ct f", f=KF),
                                        v[:, :, 0, 0, :].bitcast(f32), ALU.subtract).then_inc(S("b_lo"), 1)

                    def multiply(n, k, i):
                        dve.wait_ge(S("b_hid"), n * 3 + (2, 2, 3)[i])
                        dve.wait_ge(S("b_G"), n * 3 + i + 1)
                        if i < 2:
                            if some(n):
                                dve.wait_ge(S("b_add"), n * 2 - 1 + i)
                            o = (psg, pxy)[i]
                            hv = hid[k][:, 0:2 * GW].rearrange("p (a e) -> p a e", a=2)
                        else:
                            if not isinstance(n, int) or n > 1:
                                dve.wait_ge(S("b_R"), n - 1)
                            o = ppz[k]
                            hv = hid[k][:, 2 * GW:3 * GW].rearrange("p (a e) -> p a e", a=1).broadcast_to([128, 2, GW])
                        gv = G_ps[(k * 3 + i) % 2][:, :].rearrange("p (a e) -> p a e", a=2)[:, :, 0:GW]
                        V.tensor_tensor(o[:, :].rearrange("p (a e) -> p a e", a=2), gv, hv, ALU.mult).then_inc(S("b_mul"), 1)

                    def add(n, k, i):
                        dve.wait_ge(S("b_mul"), n * 3 + i + 1)
                        if i == 0 and (not isinstance(n, int) or n > 1):
                            dve.wait_ge(S("b_R"), n - 1)
                        q = (psg, pxy)[i]
                        V.tensor_tensor(sums2[k][:, i * GW:(i + 1) * GW], q[:, 0:GW], q[:, GW:2 * GW], ALU.add).then_inc(S("b_add"), 1)

                    yv = Y_ps[0:P, 0:W2G * NOUT].rearrange("p (c f) -> p c f", f=NOUT)
                    thv = th[:, :].rearrange("p (c f) -> p c f", f=16)
                    pav = pa[:, :].rearrange("p (c w a) -> p c w a", w=MO, a=3)
                    pbv = pb[:, :].rearrange("p (c w a) -> p c w a", w=MO, a=3)
                    pgv = pg[:, :].rearrange("p (c w) -> p c w", w=MO)

                    def post(i, m, h, q, t):
                        c0 = q * W2G
                        nrm = nmp[h][:, c0:c0 + W2G].rearrange("p (c w) -> p c w", w=1).broadcast_to([P, W2G, MO])
                        ov = O[h][:, :].rearrange("p (c f) -> p c f", f=DIM)[:, c0:c0 + W2G, :]
                        if i == 0:
                            if q == 0:
                                dve.wait_ge(S(f"b_lp{h}"), t * 48 + 48)
                            dve.wait_ge(S("b_Y"), m * 2 + 2)
                            dve.wait_ge(S("b_th"), m + 1)
                            if some(m):
                                dve.wait_ge(S("b_o"), m)
                            V.tensor_tensor(pav, yv[:, :, 16:24].rearrange("p c (w a) -> p c w a", a=1).broadcast_to([P, W2G, MO, 3]),
                                            drp[h][:, c0 * 3:(c0 + W2G) * 3].rearrange("p (c w a) -> p c w a", w=1, a=3).broadcast_to([P, W2G, MO, 3]),
                                            ALU.mult).then_inc(S("b_pa"), 1)
                            V.scalar_tensor_tensor(pgv, thv[:, :, 8:16], TG, nrm, ALU.mult, ALU.mult).then_inc(S("b_gs"), 1)
                            V.scalar_tensor_tensor(ov[:, :, 0:8], thv[:, :, 0:8], TG, nrm, ALU.mult, ALU.mult).then_inc(S("b_gs"), 1)
                        if i == 1:
                            dve.wait_ge(S("b_pa"), m + 1)
                            V.tensor_tensor(pbv, pav, yv[:, :, 24:48].rearrange("p c (a w) -> p c w a", a=3), ALU.add).then_inc(S("b_yr"), 2)
                        if i == 2:
                            dve.wait_ge(S("b_yr"), m * 2 + 2)
                            dve.wait_ge(S("b_gs"), m * 2 + 2)
                            V.tensor_tensor(ov[:, :, 8:32].rearrange("p c (w a) -> p c w a", a=3), pbv,
                                            pgv.rearrange("p c (w a) -> p c w a", a=1).broadcast_to([P, W2G, MO, 3]), ALU.mult).then_inc(S("b_o"), 1)

                    def sums(i, ch, h, t):
                        if i == 0:
                            dve.wait_ge(S("b_o"), ch * (GC // 2) + GC // 2)
                            dve.wait_ge(S(f"b_z{1 - h}"), (t + h) * NPC)
                        for f in range(i * PCF, (i + 1) * PCF):
                            ov = O[h][:, :].rearrange("p (c f) -> p c f", f=DIM)[:, :, f]
                            zv = Z[h][:, :].rearrange("p (c f) -> p c f", f=DIM)[:, :, f]
                            last = V.tensor_tensor_scan(out=zv, data0=kpp[h][:, :], data1=ov,
                                                        initial=Z[1 - h][:, (C - 1) * DIM + f:(C - 1) * DIM + f + 1], op0=ALU.mult, op1=ALU.add)
                        last.then_inc(S(f"b_z{h}"), 1)

                    def turn(t, first=False, last=False):
                        for g in range(G2):
                            n, k, gc, h = t * G2 + g, g % 2, g % GC, g // GC
                            feat = not (last and h == 1)
                            nxt = (t * 2 + h + 1, 1 - h, t + h)
                            prv = (t * 2 + h - 1, 1 - h, t - 1 + h)
                            with_post = g % 2 == 0 and not (first and g < 4)
                            pm = t * GC + (g - 4) // 2
                            pq = (g - 4) // 2 % GC
                            ph, pt = pq // (GC // 2), t - 1 if g < 4 else t
                            pq %= GC // 2
                            multiply(n, k, 0)
                            if with_post:
                                post(0, pm, ph, pq, pt)
                            multiply(n, k, 1)
                            add(n, k, 0)
                            if with_post:
                                post(1, pm, ph, pq, pt)
                            multiply(n, k, 2)
                            if with_post:
                                post(2, pm, ph, pq, pt)
                            add(n, k, 1)
                            if feat:
                                if gc < 4:
                                    fill(gc, *nxt)
                                elif gc == 4:
                                    along(0, *nxt)
                                elif gc == 5:
                                    along(1, *nxt)
                                    along(2, *nxt)
                            if g % 2 == 1 and not (last and g + AHEAD >= G2):
                                split = (g + AHEAD) // PCG
                                low(t * 2 * SP + split, split % SP, split // SP % 2)
                            if not (first and h == 0):
                                for i in {3: (0,), 6: (1, 2), 9: (3,)}.get(gc, ()):
                                    sums(i, *prv)

                    hv = hx_keep[:, :]
                    V.tensor_copy(Fv[1][:, C - 1, 8:16], hv[:, 0:8]).then_inc(S("b_init"), 1)
                    V.tensor_copy(Fv[1][:, C - 1, 32:80].rearrange("p (a u) -> p a u", a=3)[:, :, 8:16],
                                  hv[:, 8:32].rearrange("p (u a) -> p a u", a=3)).then_inc(S("b_init"), 1)
                    for h in range(2):
                        V.tensor_scalar(Fv[h][:, :, FD:FW], ident[0:P, 0:1].rearrange("p (a b) -> p a b", a=1).broadcast_to([P, C, FW - FD]),
                                        0.0, None, ALU.mult).then_inc(S("b_init"), 1)
                    V.memset(Z[1][:, :], 0.0).then_inc(S("b_init"), 1)
                    dve.wait_ge(S("b_init"), 5)
                    for i in range(NPC):
                        fill(i, 0, 0, 0)
                    for i in range(3):
                        along(i, 0, 0, 0)
                    for i in range(2):
                        low(i, i, 0)
                    turn(0, first=True)
                    with dve.Fori(1, PAIRS - 1) as t:
                        turn(t)
                    turn(PAIRS - 1, last=True)
                    for m in (NG // 2 - 2, NG // 2 - 1):
                        for i in range(3):
                            post(i, m, 1, m % (GC // 2), PAIRS - 1)
                    for i in range(NPC):
                        sums(i, NCH - 1, 1, PAIRS - 1)
                    dve.wait_ge(S("b_z1"), PAIRS * NPC)
                    V.tensor_copy(hx_keep[:, :], Z[1][:, (C - 1) * DIM:C * DIM]).then_inc(S("b_tail"), 1)
                    dve.wait_ge(S("b_tail"), 1)

        def layer_norm(dve, step, v, out_v, sq_t, st, key):
            V = nc.vector
            vv = v.rearrange("p (k f) -> p k f", f=DIM)
            mean, var, rs = st[:, 0:NP], st[:, NP:2 * NP], st[:, 2 * NP:3 * NP]
            bc = lambda a: a.rearrange("p (k f) -> p k f", f=1).broadcast_to([P, NP, DIM])
            step(V.tensor_reduce(mean, vv, AX.X, ALU.add))
            step(V.tensor_scalar(mean, mean, 1.0 / DIM, None, ALU.mult))
            step(V.tensor_tensor(vv, vv, bc(mean), ALU.subtract))
            step(V.tensor_tensor(sq_t, v, v, ALU.mult))
            step(V.tensor_reduce(var, sq_t.rearrange("p (k f) -> p k f", f=DIM), AX.X, ALU.add))
            V.tensor_scalar(var, var, 1.0 / DIM, EPS, ALU.mult, ALU.add).then_inc(S(key + "_var"), 1)
            dve.wait_ge(S(key + "_std"), 1)
            step(V.reciprocal(rs, rs))
            step(V.tensor_tensor(out_v, vv, bc(rs), ALU.mult))

        with ExitStack() as st:
            def sbt(name, shape, dt=f32):
                return st.enter_context(nc.sbuf_tensor(name, shape, dt))

            fixr = sbt("fixr", [P, DIM])
            ng = sbt("ng", [P, NP * DIM])
            sqb = sbt("sqb", [P, NP * DIM])
            stt = sbt("stt", [P, 3 * NP])
            x1e = sbt("x1e", [P, NP * (DIM + 1)])
            sd = sbt("sd", [P, NP])

            with nc.Block() as block:
                @block.tensor
                def _(pe):
                    nc.tensor.matmul(R_ps[0:P, 0:DIM], link[:, :], hx_keep[:, :], start=True, stop=True).then_inc(S("c_carry"), 1)

                @block.gpsimd
                def _(pool):
                    nc.gpsimd.indirect_dma_start(out=fixr[:, :], out_offset=None, in_=y0_d,
                                                 in_offset=bass.IndirectOffsetOnAxis(fix_i[:, :], 0)).then_inc(S("c_fixr"), 16)
                    pool.wait_ge(S("c_fix"), 1)
                    nc.gpsimd.indirect_dma_start(out=y0_d, out_offset=bass.IndirectOffsetOnAxis(fix_i[:, :], 0),
                                                 in_=fixr[:, :], in_offset=None).then_inc(S("c_fixw"), 16)
                    pool.wait_ge(S("c_fixw"), 16)
                    for k in range(NP):
                        nc.gpsimd.indirect_dma_start(out=ng[:, k * DIM:(k + 1) * DIM], out_offset=None, in_=y0_d,
                                                     in_offset=bass.IndirectOffsetOnAxis(last_i[:, k:k + 1], 0)).then_inc(S("c_ng"), 16)
                    pool.wait_ge(S("c_sd"), 1)
                    for k in range(NP):
                        nc.gpsimd.indirect_dma_start(out=sd_d, out_offset=bass.IndirectOffsetOnAxis(first_i[:, k:k + 1], 0),
                                                     in_=sd[:, k:k + 1], in_offset=None,
                                                     bounds_check=E - 1, oob_is_err=False).then_inc(S("c_sdw"), 16)
                    pool.wait_ge(S("c_sdt"), 16)
                    nc.gpsimd.indirect_dma_start(out=hsd[:, :], out_offset=None, in_=sdt_d,
                                                 in_offset=bass.IndirectOffsetOnAxis(head_i[:, :], 0)).then_inc(S("c_hsd"), 16)
                    pool.wait_ge(S("c_sdw"), 16 * NP)
                    pool.wait_ge(S("c_hsd"), 16)

                @block.vector
                def _(dve):
                    n = [0]

                    def step(ins):
                        n[0] += 1
                        ins.then_inc(S("c_dve"), 1)
                        dve.wait_ge(S("c_dve"), n[0])

                    V = nc.vector
                    dve.wait_ge(S("c_carry"), 1)
                    dve.wait_ge(S("c_fixr"), 16)
                    V.tensor_tensor(fixr[:, :], R_ps[0:P, 0:DIM], fixr[:, :], ALU.add).then_inc(S("c_fix"), 1)
                    dve.wait_ge(S("c_ng"), 16 * NP)
                    step(V.tensor_tensor(ng[:, :], ng[:, :], xn[:, :], ALU.add))
                    layer_norm(dve, step, ng[:, :], xn[:, :].rearrange("p (k f) -> p k f", f=DIM), sqb[:, :], stt, "c")
                    xv3 = xn[:, :].rearrange("p (k f) -> p k f", f=DIM)
                    x1v = x1e[:, :].rearrange("p (k f) -> p k f", f=DIM + 1)
                    V.tensor_copy(x1v[:, :, 0:DIM], xv3)
                    bc = lambda a: a.rearrange("p (k f) -> p k f", k=1).broadcast_to([P, NP, DIM])
                    sq3 = sqb[:, :].rearrange("p (k f) -> p k f", f=DIM)
                    step(V.tensor_tensor(sq3, xv3, bc(attn_b[:, DIM:2 * DIM]), ALU.mult))
                    V.tensor_reduce(sd[:, :], sq3, AX.X, ALU.add).then_inc(S("c_sd"), 1)
                    dve.wait_ge(S("c_sd"), 1)
                    step(V.tensor_tensor(sq3, xv3, bc(attn_b[:, 0:DIM]), ALU.mult))
                    V.tensor_reduce(x1v[:, :, DIM:DIM + 1], sq3, AX.X, ALU.add).then_inc(S("c_x1e"), 1)

                @block.scalar
                def _(act):
                    act.wait_ge(S("c_var"), 1)
                    nc.scalar.activation(stt[:, 2 * NP:3 * NP], stt[:, NP:2 * NP], ACT.Sqrt).then_inc(S("c_std"), 1)

                @block.sync
                def _(sp):
                    sp.wait_ge(S("c_sd"), 1)
                    sp.dma_start(sdt_d.rearrange("(p k) a -> p (k a)", k=NP), sd[:, :]).then_inc(S("c_sdt"), 16)
                    sp.wait_ge(S("c_x1e"), 1)
                    sp.dma_start(tab_d.rearrange("(p k) f -> p (k f)", k=NP), x1e[:, :]).then_inc(S("c_tab"), 16)
                    sp.wait_ge(S("c_tab"), 16)
                    sp.wait_ge(S("c_sdt"), 16)

        with ExitStack() as st:
            def sbt(name, shape, dt=f32):
                return st.enter_context(nc.sbuf_tensor(name, shape, dt))

            def two(name, w, dt=f32):
                return [sbt(f"{name}_{h}", [P, w], dt) for h in range(2)]

            T1 = DIM + 1
            idx = two("idxb", C, i32)
            gx = two("gxb", C * T1)
            sdr = two("sdr", C)
            kp = two("kpb", C)
            rst = sbt("rst", [P, C])
            sdf = two("sdf", C)
            ee = sbt("ee", [P, C])
            lk = sbt("lk", [P, C])
            mx = two("mx", C + 1)
            ex = sbt("ex", [P, 2 * C])
            dec = sbt("dec", [P, C])
            wx = sbt("wx", [P, C * DIM])
            Z = two("Zb", C * R1)

            with nc.Block() as block:
                @block.sync
                def _(sp):
                    def load(ch, h, t):
                        sp.wait_ge(S(f"d_gx{h}"), t * 16 * C)
                        sp.sem_inc(S("go_sp"), 1)
                        sp.wait_ge(S(f"d_wx{h}"), t)
                        sp.sem_inc(S("go_sp"), 1)
                        sp.dma_start(idx[h][:, :], edges(src, 1)[:, bass.ds(ch * C, C)]).then_inc(S(f"d_idx{h}"), 16)
                        sp.wait_ge(S(f"d_z{h}"), t)
                        sp.sem_inc(S("go_sp"), 1)
                        sp.wait_ge(S(f"d_st{h}"), t * 16)
                        sp.sem_inc(S("go_sp"), 1)
                        sp.dma_start(sdr[h][:, :], sd_d.rearrange("(p c) a -> p (c a)", c=EP)[:, bass.ds(ch * C, C)]).then_inc(S(f"d_ld{h}"), 16)
                        sp.dma_start(kp[h][:, :], edges(keep_d, 1)[:, bass.ds(ch * C, C)]).then_inc(S(f"d_ld{h}"), 16)

                    def store(ch, h, t):
                        sp.wait_ge(S(f"d_z{h}"), t + 1)
                        sp.wait_ge(S(f"d_zm{h}"), t + 1)
                        sp.dma_start(y1_d[0:E, :].rearrange("(p c) f -> p (c f)", c=EP)[:, bass.ds(ch * C * R1, C * R1)], Z[h][:, :]).then_inc(S(f"d_st{h}"), 16)

                    load(0, 0, 0)
                    load(1, 1, 0)
                    with sp.Fori(0, PAIRS - 1) as t:
                        for h in range(2):
                            store(t * 2 + h, h, t)
                            load(t * 2 + h + 2, h, t + 1)
                    for h in range(2):
                        store(2 * PAIRS - 2 + h, h, PAIRS - 1)
                    for h in range(2):
                        sp.wait_ge(S(f"d_st{h}"), 16 * PAIRS)

                @block.gpsimd
                def _(pool):
                    with pool.Fori(0, PAIRS) as t:
                        for h in range(2):
                            pool.wait_ge(S(f"d_idx{h}"), t * 16 + 16)
                            pool.sem_inc(S("go_pool"), 1)
                            for c in range(C):
                                nc.gpsimd.indirect_dma_start(out=gx[h][:, c * T1:(c + 1) * T1], out_offset=None, in_=tab_d,
                                                             in_offset=bass.IndirectOffsetOnAxis(idx[h][:, c:c + 1], 0)).then_inc(S(f"d_gx{h}"), 16)

                @block.scalar
                def _(act):
                    def chunk(h, t):
                        act.wait_ge(S("d_pre"), t * 2 + h + 1)
                        nc.scalar.activation(ex[:, :], ex[:, :], ACT.Exp).then_inc(S("d_exp"), 1)
                        nc.scalar.activation(Z[h][:, :].rearrange("p (c f) -> p c f", f=R1)[:, :, DIM + 1],
                                             mx[h][:, 1:C + 1], ACT.Copy).then_inc(S(f"d_zm{h}"), 1)

                    with act.Fori(0, PAIRS) as t:
                        for h in range(2):
                            chunk(h, t)

                @block.vector
                def _(dve):
                    V = nc.vector
                    STEPS = 6

                    def chunk(h, t):
                        n = [0]

                        def step(ins):
                            n[0] += 1
                            ins.then_inc(S("d_dve"), 1)
                            dve.wait_ge(S("d_dve"), t * 2 * STEPS + h * STEPS + n[0])

                        g = gx[h][:, :].rearrange("p (c f) -> p c f", f=T1)
                        dve.wait_ge(S(f"d_ld{h}"), t * 32 + 32)
                        V.tensor_scalar(rst[:, :], kp[h][:, :], -1.0, BIG, ALU.add, ALU.mult)
                        V.tensor_copy(mx[h][:, 0:1], mx[1 - h][:, C:C + 1])
                        step(V.tensor_tensor_scan(out=sdf[h][:, :], data0=kp[h][:, :], data1=sdr[h][:, :],
                                                  initial=sdf[1 - h][:, C - 1:C], op0=ALU.mult, op1=ALU.add))
                        dve.wait_ge(S(f"d_gx{h}"), t * 16 * C + 16 * C)
                        step(V.tensor_tensor(lk[:, :], sdf[h][:, :], g[:, :, DIM], ALU.add))
                        step(V.scalar_tensor_tensor(ee[:, :], lk[:, :], 0.01, lk[:, :], ALU.mult, ALU.max))
                        step(V.tensor_tensor_scan(out=mx[h][:, 1:C + 1], data0=rst[:, :], data1=ee[:, :],
                                                  initial=mx[1 - h][:, C:C + 1], op0=ALU.add, op1=ALU.max))
                        V.tensor_tensor(ex[:, 0:C], ee[:, :], mx[h][:, 1:C + 1], ALU.subtract)
                        step(V.tensor_tensor(ex[:, C:2 * C], mx[h][:, 0:C], mx[h][:, 1:C + 1], ALU.subtract))
                        V.memset(one[:, :], 0.0).then_inc(S("d_pre"), 1)
                        dve.wait_ge(S("d_exp"), t * 2 + h + 1)
                        V.scalar_tensor_tensor(dec[:, :], ex[:, C:2 * C], 1.0, kp[h][:, :], ALU.min, ALU.mult)
                        step(V.tensor_tensor(wx[:, :].rearrange("p (c f) -> p c f", f=DIM), g[:, :, 0:DIM],
                                             ex[:, 0:C].rearrange("p (c f) -> p c f", f=1).broadcast_to([P, C, DIM]), ALU.mult))
                        V.memset(one[:, :], 0.0).then_inc(S(f"d_wx{h}"), 1)
                        assert n[0] == STEPS
                        zv = Z[h][:, :].rearrange("p (c f) -> p c f", f=R1)
                        zp = Z[1 - h][:, :].rearrange("p (c f) -> p c f", f=R1)
                        V.tensor_tensor_scan(out=zv[:, :, DIM], data0=dec[:, :], data1=ex[:, 0:C], initial=zp[:, C - 1, DIM:DIM + 1],
                                             op0=ALU.mult, op1=ALU.add)
                        for f in range(DIM):
                            last = V.tensor_tensor_scan(out=zv[:, :, f], data0=dec[:, :],
                                                        data1=wx[:, :].rearrange("p (c f) -> p c f", f=DIM)[:, :, f],
                                                        initial=zp[:, C - 1, f:f + 1], op0=ALU.mult, op1=ALU.add)
                        last.then_inc(S(f"d_z{h}"), 1)
                        dve.wait_ge(S(f"d_z{h}"), t + 1)

                    one = sbt("one_d", [P, 1])
                    V.tensor_copy(sdf[1][:, C - 1:C], hsd[:, :]).then_inc(S("d_init"), 1)
                    V.memset(mx[1][:, C:C + 1], -BIG).then_inc(S("d_init"), 1)
                    V.memset(Z[1][:, :], 0.0).then_inc(S("d_init"), 1)
                    dve.wait_ge(S("d_init"), 3)
                    with dve.Fori(0, PAIRS) as t:
                        for h in range(2):
                            chunk(h, t)
                    dve.wait_ge(S("d_zm1"), PAIRS)
                    V.tensor_copy(tail1[:, :], Z[1][:, (C - 1) * R1:C * R1]).then_inc(S("d_tail"), 1)
                    dve.wait_ge(S("d_tail"), 1)

        with ExitStack() as st:
            def sbt(name, shape, dt=f32):
                return st.enter_context(nc.sbuf_tensor(name, shape, dt))

            fixr = sbt("fixr1", [P, R1])
            dm = sbt("dm", [P, P])
            am = sbt("am", [P, P])
            cw = sbt("cw", [P, P])
            sm = sbt("sm", [P, 8])
            ng = sbt("ng1", [P, NP * R1])
            hh = sbt("hh", [P, NP * DIM])
            sqb = sbt("sqb1", [P, NP * DIM])
            stt = sbt("stt1", [P, 3 * NP])

            with nc.Block() as block:
                @block.tensor
                def _(pe):
                    pe.wait_ge(S("e_dm"), 1)
                    nc.tensor.matmul(R_ps[0:P, 0:P], ones[0:P, 0:P], dm[:, :], start=True, stop=True).then_inc(S("e_mrow"), 1)
                    pe.wait_ge(S("e_dm"), 2)
                    nc.tensor.matmul(Y_ps[0:P, 0:P], ones[0:P, 0:P], dm[:, :], start=True, stop=True).then_inc(S("e_mrow"), 1)
                    pe.wait_ge(S("e_cw"), 1)
                    nc.tensor.matmul(T_ps[0:P, 0:DIM + 1], cw[:, :], tail1[:, 0:DIM + 1], start=True, stop=True).then_inc(S("e_carry"), 1)

                @block.gpsimd
                def _(pool):
                    nc.gpsimd.indirect_dma_start(out=fixr[:, :], out_offset=None, in_=y1_d,
                                                 in_offset=bass.IndirectOffsetOnAxis(fix_i[:, :], 0)).then_inc(S("e_fixr"), 16)
                    pool.wait_ge(S("e_fix"), 1)
                    nc.gpsimd.indirect_dma_start(out=y1_d, out_offset=bass.IndirectOffsetOnAxis(fix_i[:, :], 0),
                                                 in_=fixr[:, :], in_offset=None).then_inc(S("e_fixw"), 16)
                    pool.wait_ge(S("e_fixw"), 16)
                    for k in range(NP):
                        nc.gpsimd.indirect_dma_start(out=ng[:, k * R1:(k + 1) * R1], out_offset=None, in_=y1_d,
                                                     in_offset=bass.IndirectOffsetOnAxis(last_i[:, k:k + 1], 0)).then_inc(S("e_ng"), 16)

                @block.vector
                def _(dve):
                    n = [0]

                    def step(ins):
                        n[0] += 1
                        ins.then_inc(S("e_dve"), 1)
                        dve.wait_ge(S("e_dve"), n[0])

                    V = nc.vector
                    mt = tail1[:, DIM + 1:DIM + 2]
                    V.tensor_scalar(dm[:, :], ident[0:P, 0:P], mt, None, ALU.mult).then_inc(S("e_dm"), 1)
                    step(V.tensor_scalar(am[:, :], linkT[:, :], -1.0, BIG, ALU.add, ALU.mult))
                    dve.wait_ge(S("e_mrow"), 1)
                    step(V.tensor_tensor(cw[:, :], R_ps[0:P, 0:P], linkT[:, :], ALU.mult))
                    step(V.tensor_tensor(cw[:, :], cw[:, :], am[:, :], ALU.add))
                    step(V.tensor_reduce(sm[:, 0:1], cw[:, :], AX.X, ALU.max))
                    dve.wait_ge(S("e_fixr"), 16)
                    step(V.tensor_tensor(sm[:, 1:2], sm[:, 0:1], fixr[:, DIM + 1:DIM + 2], ALU.max))
                    V.tensor_scalar(dm[:, :], ident[0:P, 0:P], sm[:, 1:2], None, ALU.mult).then_inc(S("e_dm"), 1)
                    dve.wait_ge(S("e_mrow"), 2)
                    step(V.tensor_scalar(am[:, :], Y_ps[0:P, 0:P], mt, 0.0, ALU.subtract, ALU.max))
                    V.tensor_tensor(sm[:, 2:3], fixr[:, DIM + 1:DIM + 2], sm[:, 1:2], ALU.subtract).then_inc(S("e_am"), 1)
                    dve.wait_ge(S("e_exp"), 2)
                    V.tensor_tensor(cw[:, :], am[:, :], link[:, :], ALU.mult).then_inc(S("e_cw"), 1)
                    dve.wait_ge(S("e_carry"), 1)
                    V.scalar_tensor_tensor(fixr[:, 0:DIM + 1], fixr[:, 0:DIM + 1], sm[:, 3:4], T_ps[0:P, 0:DIM + 1],
                                           ALU.mult, ALU.add).then_inc(S("e_fix"), 1)
                    dve.wait_ge(S("e_ng"), 16 * NP)
                    ngv = ng[:, :].rearrange("p (k f) -> p k f", f=R1)
                    hv = hh[:, :].rearrange("p (k f) -> p k f", f=DIM)
                    step(V.tensor_tensor(stt[:, 0:NP].rearrange("p (k f) -> p k f", f=1), ngv[:, :, DIM:DIM + 1],
                                         empty[:, :].rearrange("p (k f) -> p k f", f=1), ALU.add))
                    step(V.reciprocal(stt[:, NP:2 * NP], stt[:, 0:NP]))
                    step(V.tensor_tensor(hv, ngv[:, :, 0:DIM], stt[:, NP:2 * NP].rearrange("p (k f) -> p k f", f=1).broadcast_to([P, NP, DIM]), ALU.mult))
                    step(V.tensor_tensor(hh[:, :], hh[:, :], xn[:, :], ALU.add))
                    layer_norm(dve, step, hh[:, :], xn[:, :].rearrange("p (k f) -> p k f", f=DIM), sqb[:, :], stt, "e")
                    V.memset(sm[:, 4:5], 0.0).then_inc(S("e_done"), 1)

                @block.scalar
                def _(act):
                    act.wait_ge(S("e_am"), 1)
                    nc.scalar.activation(am[:, :], am[:, :], ACT.Exp, scale=-1.0).then_inc(S("e_exp"), 1)
                    nc.scalar.activation(sm[:, 3:4], sm[:, 2:3], ACT.Exp).then_inc(S("e_exp"), 1)
                    act.wait_ge(S("e_var"), 1)
                    nc.scalar.activation(stt[:, 2 * NP:3 * NP], stt[:, NP:2 * NP], ACT.Sqrt).then_inc(S("e_std"), 1)

                @block.sync
                def _(sp):
                    sp.wait_ge(S("e_done"), 1)
                    sp.dma_start(out.rearrange("(p k) f -> p (k f)", k=NP), xn[:, :]).then_inc(S("e_out"), 16)
                    sp.wait_ge(S("e_out"), 16)


_INS = ["x", "src", "dst", "edge_attr_10", "edge_attr_3", "edge_weight", "L0_gnn_W1", "L0_gnn_W2", "L1_gnn_attn_w"]


def kernel(**inputs):
    import numpy as _np
    import concourse.bacc as _bacc
    from concourse import mybir as _mybir
    from concourse.bass_utils import run_bass_kernel_spmd as _run

    nc = _bacc.Bacc("TRN2", target_bir_lowering=False, num_devices=1)
    arrays, args = {}, []
    for name in _INS:
        a = _np.ascontiguousarray(inputs[name])
        arrays[f"in_{name}"] = a
        args.append(nc.dram_tensor(f"in_{name}", a.shape, _mybir.dt.from_np(a.dtype), kind="ExternalInput").ap())
    shape = inputs["x"].shape
    args.append(nc.dram_tensor("out_0", shape, _mybir.dt.float32, kind="ExternalOutput").ap())
    gnn_resnorm_kernel(nc, *args)
    r = _run(nc, [arrays], core_ids=[0])
    return r.results[0]["out_0"]
```

```python
import concourse.bass as bass
from concourse import mybir
from contextlib import ExitStack


def gnn_resnorm_kernel(nc, x, src, dst, emb, vec, weight, W1, W2, attn, out):
    f32 = mybir.dt.float32
    f32r = mybir.dt.float32r
    i32 = mybir.dt.int32
    ALU = mybir.AluOpType
    ACT = mybir.ActivationFunctionType
    AX = mybir.AxisListType

    N, DIM = x.shape
    E = src.shape[0]
    NEMB, HID = W1.shape
    P = 125
    EP = E // P
    NP = N // P
    assert P * EP == E and P * NP == N
    C = 40
    PAIRS = EP // (2 * C)
    GT = 4
    GW = GT * P
    GC = C // GT
    G2 = 2 * GC
    MO = 8
    NOUT = 6 * MO
    KF = 32
    NT = 3
    QF = 80
    FD = QF + NEMB
    FW = NT * KF
    HJ = HID // 2
    SB = 400
    ZEARLY = 12
    EARLY = 60
    NSB = E // SB
    ZROW = E + 200
    PAD = 256
    R1 = DIM + 2
    BIG = 3.0e38
    EPS = 1e-5
    TG = 1.593
    PW_S, PW_V, INV3 = 0.17677669529663687, 0.25, 0.5773502691896258
    KS = PW_S / HID ** 0.5
    KV = PW_V / HID ** 0.5
    C121 = 1.5 ** 0.5

    def edges(ap, width):
        return ap.rearrange("(p c) f -> p c f", c=EP) if width > 1 else ap.rearrange("(p c) -> p c", c=EP)

    ctx = ExitStack()
    with ctx:
        def sb(name, shape, dt=f32):
            return ctx.enter_context(nc.sbuf_tensor(name, shape, dt))

        def sem(name):
            return ctx.enter_context(nc.semaphore(name))

        def dram(name, shape, dt=f32):
            return nc.dram_tensor(name, shape, dt, kind="Internal").ap()

        dstf_d = dram("dstf_d", (NSB, SB))
        samp_d = dram("samp_d", (NSB,), i32)
        end_d = dram("end_d", (N + 1, 1))
        xd_d = dram("xd_d", (E, DIM))
        sd_d = dram("sd_d", (E, 1))
        dir_d = dram("dir_d", (E, 3))
        keep_d = dram("keep_d", (E,))
        y0_d = dram("y0_d", (E + PAD, DIM))
        y1_d = dram("y1_d", (E + PAD, R1))
        tab_d = dram("tab_d", (N, DIM + 1))
        sdt_d = dram("sdt_d", (N, 1))

        ident = sb("ident", [128, 128])
        ones = sb("ones", [128, 128])
        wst = sb("wst", [128, 8 * 128], f32r)
        wh = sb("wh", [128, 2 * 128], f32r)
        red = sb("red", [128, 3 * NOUT])
        attn_b = sb("attn_b", [P, 2 * DIM])

        xn = sb("xn", [P, NP * DIM])
        endf = sb("endf", [P, NP])
        startf = sb("startf", [P, NP])
        empty = sb("empty", [P, NP])
        first_i = sb("first_i", [P, NP], i32)
        last_i = sb("last_i", [P, NP], i32)
        head_i = sb("head_i", [P, 1], i32)
        fix_i = sb("fix_i", [P, 1], i32)
        headf = sb("headf", [P, 1])
        tailf = sb("tailf", [P, 1])
        hx_keep = sb("hx_keep", [P, DIM])
        tail1 = sb("tail1", [P, R1])
        hsd = sb("hsd", [P, 1])
        link = sb("link", [P, P])
        linkT = sb("linkT", [P, P])

        G_ps = [ctx.enter_context(nc.psum_tensor(f"G_ps{i}", [128, 1024], f32)) for i in range(2)]
        T_ps = ctx.enter_context(nc.psum_tensor("T_ps", [128, 512], f32))
        H_ps = ctx.enter_context(nc.psum_tensor("H_ps", [128, 512], f32))
        R_ps = ctx.enter_context(nc.psum_tensor("R_ps", [128, 512], f32))
        Y_ps = ctx.enter_context(nc.psum_tensor("Y_ps", [128, 512], f32))

        idx = [sb(f"idx_{h}", [P, C], i32) for h in range(2)]
        gx = [sb(f"gx_{h}", [P, C * DIM]) for h in range(2)]

        all_sems = {}

        def S(name):
            if name not in all_sems:
                all_sems[name] = sem(name)
            return all_sems[name]

        with ExitStack() as st:
            def sbt(name, shape, dt=f32):
                return st.enter_context(nc.sbuf_tensor(name, shape, dt))

            dst_i = sbt("dst_i", [P, EP], i32)
            dstf = sbt("dstf", [P, EP + 1])
            prev_i = sbt("prev_i", [P, 1], i32)
            keep = sbt("keep", [P, EP])
            dirv = sbt("dirv", [P, EP * 3])
            sq = sbt("sq", [P, EP * 3])
            s2 = sbt("s2", [P, EP])
            rn = sbt("rn", [P, EP])
            samp_b = sbt("samp_b", [P, NSB])
            samp_i = sbt("samp_i", [P, NSB], i32)
            node_i = sbt("node_i", [P, NP], i32)
            nodef = sbt("nodef", [P, NP])
            NF = 8
            JW = max(SB, NSB)
            junk = sbt("junk", [P, NF * JW], mybir.dt.bfloat16)
            cnt = sbt("cnt", [P, NP])
            blk_i = sbt("blk_i", [P, NP], i32)
            fine = sbt("fine", [P, NP])
            blkbuf = sbt("blkbuf", [P, NF * SB])
            w2s = sbt("w2s", [HID, 7 * 128])
            zeros = sbt("zeros", [P, 3200])
            w2x = sbt("w2x", [HID, NOUT * KF])
            w2d = sbt("w2d", [HID, NOUT * 4 * KF])
            w_hi = sbt("w_hi", [128, NOUT * HID], f32r)
            w1x = sbt("w1x", [128, 2 * 128])
            w1_hi = sbt("w1_hi", [128, 2 * 128], f32r)
            wr = sbt("wr", [HID, 128])
            head_row = sbt("head_row", [P, P])
            diag = sbt("diag", [P, P])
            part_i = sbt("part_i", [P, 1], i32)
            partf = sbt("partf", [P, 1])
            endh = sbt("endh", [P, 1])
            idx1 = sbt("idx1", [P, 1], i32)
            t1 = sbt("t1", [P, 4])
            tn = sbt("tn", [P, 4 * NP])

            with nc.Block() as block:
                @block.sync
                def _(sp):
                    sp.dma_start(dst_i[:, :], edges(dst, 1)).then_inc(S("a_dst"), 16)
                    sp.dma_start(samp_d.rearrange("(a b) -> a b", b=1), dst.rearrange("(a b) -> a b", b=SB)[:, 0:1], allow_slow_non_contiguous=True).then_inc(S("a_samp"), 16)
                    sp.wait_ge(S("a_samp"), 16)
                    sp.dma_start(samp_i[:, :], samp_d.rearrange("(a b) -> a b", a=1).broadcast_to([P, NSB])).then_inc(S("a_sampb"), 16)
                    sp.wait_ge(S("a_prev0"), 1)
                    sp.dma_start(prev_i[1:P, :], dst.rearrange("(p c) -> p c", c=EP)[0:P - 1, EP - 1:EP], allow_slow_non_contiguous=True).then_inc(S("a_prev"), 16)
                    for h in range(2):
                        sp.dma_start(idx[h][:, :], edges(src, 1)[:, h * C:(h + 1) * C]).then_inc(S(f"b_idx{h}"), 16)
                    sp.dma_start(dirv[:, :], vec.rearrange("(p c) f -> p (c f)", c=EP)).then_inc(S("a_vec"), 16)
                    sp.dma_start(xn[:, :], x.rearrange("(p k) f -> p (k f)", k=NP)).then_inc(S("a_x"), 16)
                    sp.dma_start(w2s[:, :], W2).then_inc(S("a_w"), 16)
                    sp.dma_start(attn_b[:, :], attn.rearrange("(a f) -> a f", a=1).broadcast_to([P, 2 * DIM])).then_inc(S("a_w"), 16)
                    sp.wait_ge(S("a_wh0"), 1)
                    for i in range(4):
                        row = KF * i + QF - 2 * KF
                        for half in range(2):
                            sp.dma_start(w1x[row:row + NEMB, half * 128:(half + 1) * 128].rearrange("k (w j) -> k w j", j=HJ),
                                         W1[:, half * HJ:(half + 1) * HJ].rearrange("k (w j) -> k w j", w=1).broadcast_to([NEMB, 2 * MO, HJ])).then_inc(S("a_w1"), 16)
                    sp.wait_ge(S("a_dstf"), 1)
                    sp.dma_start(dstf_d.rearrange("a b -> (a b)").rearrange("(p c) -> p c", c=EP), dstf[:, 1:]).then_inc(S("a_dstd"), 16)
                    sp.wait_ge(S("a_zero"), 1)
                    for i in range(EP * DIM // 3200):
                        if i >= ZEARLY:
                            sp.wait_ge(S("a_fine"), 12 * (i - ZEARLY) + 8)
                        sp.dma_start(xd_d.rearrange("(p c) f -> p (c f)", c=EP)[:, i * 3200:(i + 1) * 3200], zeros[:, :]).then_inc(S("a_xd0"), 16)
                    sp.dma_start(sd_d.rearrange("(p c) a -> p (c a)", c=EP), zeros[:, 0:EP]).then_inc(S("a_pad"), 16)
                    sp.dma_start(y0_d[E:E + PAD, :].rearrange("(a b) f -> a (b f)", a=64), zeros[0:64, 0:4 * DIM]).then_inc(S("a_pad"), 16)
                    sp.dma_start(y1_d[E:E + PAD, :].rearrange("(a b) f -> a (b f)", a=64), zeros[0:64, 0:4 * R1]).then_inc(S("a_pad"), 16)
                    sp.dma_start(end_d[0:1, :], zeros[0:1, 0:1]).then_inc(S("a_end"), 16)
                    sp.wait_ge(S("a_endf"), 1)
                    sp.dma_start(end_d[1:N + 1, :].rearrange("(p k) a -> p (k a)", k=NP), endf[:, :]).then_inc(S("a_end"), 16)
                    sp.wait_ge(S("a_end"), 32)
                    sp.dma_start(startf[:, :], end_d[0:N, :].rearrange("(p k) a -> p (k a)", k=NP)).then_inc(S("a_start"), 16)
                    sp.wait_ge(S("a_keep"), 1)
                    sp.dma_start(keep_d.rearrange("(p c) -> p c", c=EP), keep[:, :]).then_inc(S("a_out"), 16)
                    sp.wait_ge(S("a_dir"), 1)
                    sp.dma_start(dir_d.rearrange("(p c) f -> p (c f)", c=EP), dirv[:, :]).then_inc(S("a_out"), 16)
                    sp.wait_ge(S("a_out"), 32)
                    sp.wait_ge(S("a_pad"), 48)

                @block.gpsimd
                def _(pool):
                    nc.gpsimd.memset(prev_i[:, :], -1).then_inc(S("a_prev0"), 1)
                    nc.gpsimd.memset(ones[:, :], 1.0).then_inc(S("a_ones"), 1)
                    nc.gpsimd.memset(ident[:, :], 0.0).then_inc(S("a_id"), 1)
                    pool.wait_ge(S("a_id"), 1)
                    nc.gpsimd.affine_select(out=ident[:, :], in_=ident[:, :], compare_op=ALU.not_equal, fill=1.0, base=0,
                                            pattern=[[-1, 128]], channel_multiplier=1).then_inc(S("a_id"), 1)
                    nc.gpsimd.iota(node_i[:, :], [[1, NP]], base=0, channel_multiplier=NP).then_inc(S("a_iota"), 1)
                    nc.gpsimd.iota(part_i[:, :], [[0, 1]], base=0, channel_multiplier=1).then_inc(S("a_iota"), 1)
                    nc.gpsimd.memset(red[:, :], 0.0).then_inc(S("a_red"), 1)
                    pool.wait_ge(S("a_red"), 1)
                    nc.gpsimd.memset(w1x[:, :], 0.0).then_inc(S("a_wh0"), 1)
                    for i, (b, o0, nw, r0) in enumerate(((0, 0, 2 * MO, 0), (1, 3 * MO, 2 * MO, 0), (2, 2 * MO, MO, 0), (2, 5 * MO, MO, 64))):
                        blk = red[:, b * NOUT + o0:b * NOUT + o0 + nw]
                        nc.gpsimd.memset(blk, 1.0).then_inc(S("a_red"), 1)
                        pool.wait_ge(S("a_red"), 3 * i + 2)
                        nc.gpsimd.affine_select(out=blk, in_=blk, compare_op=ALU.is_ge, fill=0.0, base=-r0,
                                                pattern=[[-HJ, nw]], channel_multiplier=1).then_inc(S("a_red"), 1)
                        pool.wait_ge(S("a_red"), 3 * i + 3)
                        nc.gpsimd.affine_select(out=blk, in_=blk, compare_op=ALU.is_ge, fill=0.0, base=r0 + HJ - 1,
                                                pattern=[[HJ, nw]], channel_multiplier=-1).then_inc(S("a_red"), 1)
                    pool.wait_ge(S("a_head"), 1)

                    def early(i):
                        h, c = divmod(i, C)
                        if c == 0:
                            pool.wait_ge(S(f"b_idx{h}"), 16)
                        nc.gpsimd.indirect_dma_start(out=gx[h][:, c * DIM:(c + 1) * DIM], out_offset=None, in_=x,
                                                     in_offset=bass.IndirectOffsetOnAxis(idx[h][:, c:c + 1], 0)).then_inc(S(f"b_gx{h}"), 16)

                    for i in range(EARLY):
                        early(i)
                    pool.wait_ge(S("a_dstd"), 16)
                    pool.wait_ge(S("a_blk"), 1)
                    for k in range(NP):
                        if k >= NF:
                            pool.wait_ge(S("a_fine"), k - NF + 1)
                        nc.gpsimd.indirect_dma_start(out=blkbuf[:, (k % NF) * SB:(k % NF + 1) * SB], out_offset=None, in_=dstf_d,
                                                     in_offset=bass.IndirectOffsetOnAxis(blk_i[:, k:k + 1], 0)).then_inc(S(f"a_fg{k % NF}"), 16)
                    pool.wait_ge(S("a_start"), 16)
                    nc.gpsimd.indirect_dma_start(out=endh[:, :], out_offset=None, in_=end_d,
                                                 in_offset=bass.IndirectOffsetOnAxis(idx1[:, :], 0)).then_inc(S("a_endh"), 16)
                    nc.gpsimd.indirect_dma_start(out=hx_keep[:, :], out_offset=None, in_=x,
                                                 in_offset=bass.IndirectOffsetOnAxis(head_i[:, :], 0)).then_inc(S("a_hx"), 16)
                    pool.wait_ge(S("a_link0"), 2)
                    nc.gpsimd.affine_select(out=link[:, :], in_=link[:, :], compare_op=ALU.is_gt, fill=0.0, base=0,
                                            pattern=[[1, P]], channel_multiplier=-1).then_inc(S("a_link"), 1)
                    pool.wait_ge(S("a_idx"), 1)
                    pool.wait_ge(S("a_x"), 16)
                    pool.wait_ge(S("a_xd0"), 16 * (EP * DIM // 3200))
                    for k in range(NP):
                        nc.gpsimd.indirect_dma_start(out=xd_d, out_offset=bass.IndirectOffsetOnAxis(first_i[:, k:k + 1], 0),
                                                     in_=xn[:, k * DIM:(k + 1) * DIM], in_offset=None,
                                                     bounds_check=E - 1, oob_is_err=False).then_inc(S("a_xd"), 16)
                    pool.wait_ge(S("a_xd"), 16 * NP)
                    pool.wait_ge(S("a_hx"), 16)
                    pool.wait_ge(S("a_link"), 1)

                @block.vector
                def _(dve):
                    n = [0]

                    def step(ins):
                        n[0] += 1
                        ins.then_inc(S("a_dve"), 1)
                        dve.wait_ge(S("a_dve"), n[0])

                    V = nc.vector
                    V.memset(zeros[:, :], 0.0).then_inc(S("a_zero"), 1)
                    dve.wait_ge(S("a_dst"), 16)
                    V.tensor_copy(dstf[:, 1:], dst_i[:, :]).then_inc(S("a_dstf"), 1)
                    dve.wait_ge(S("a_prev"), 16)
                    step(V.tensor_copy(dstf[:, 0:1], prev_i[:, :]))
                    dve.wait_ge(S("a_dstf"), 1)
                    V.tensor_tensor(keep[:, :], dstf[:, 1:], dstf[:, 0:EP], ALU.is_equal).then_inc(S("a_keep"), 1)
                    V.tensor_copy(headf[:, :], dstf[:, 1:2])
                    V.tensor_copy(tailf[:, :], dstf[:, EP:EP + 1])
                    V.tensor_copy(head_i[:, :], dst_i[:, 0:1])
                    step(V.tensor_scalar(idx1[:, :], dstf[:, 1:2], 1.0, None, ALU.add))
                    V.memset(w2x[:, :], 0.0).then_inc(S("a_head"), 1)
                    dve.wait_ge(S("a_iota"), 2)
                    V.tensor_copy(partf[:, :], part_i[:, :])
                    step(V.tensor_copy(nodef[:, :], node_i[:, :]))
                    dve.wait_ge(S("a_id"), 2)
                    step(V.tensor_scalar(diag[:, :], ident[0:P, 0:P], headf[:, :], None, ALU.mult))
                    V.memset(t1[:, 0:1], 0.0).then_inc(S("a_diag"), 1)
                    dve.wait_ge(S("a_hrow"), 1)
                    V.tensor_scalar(link[:, :], R_ps[0:P, 0:P], tailf[:, :], None, ALU.is_equal).then_inc(S("a_link0"), 2)
                    dve.wait_ge(S("a_sampb"), 16)
                    step(V.tensor_copy(samp_b[:, :], samp_i[:, :]))
                    for k in range(NP):
                        if k >= NF:
                            dve.wait_ge(S("a_coarse"), k - NF + 1)
                        V.tensor_scalar(junk[:, (k % NF) * JW:(k % NF) * JW + NSB], samp_b[:, :], nodef[:, k:k + 1], None, ALU.is_le, ALU.add,
                                        accum_out=cnt[:, k:k + 1]).then_inc(S("a_coarse"), 1)
                    dve.wait_ge(S("a_coarse"), NP)
                    step(V.tensor_scalar(tn[:, 0:NP], cnt[:, :], -1.0, 0.0, ALU.add, ALU.max))
                    V.tensor_copy(blk_i[:, :], tn[:, 0:NP]).then_inc(S("a_blk"), 1)
                    for k in range(NP):
                        dve.wait_ge(S(f"a_fg{k % NF}"), 16 * (k // NF + 1))
                        if k >= NF:
                            dve.wait_ge(S("a_fine"), k - NF + 1)
                        V.tensor_scalar(junk[:, (k % NF) * JW:(k % NF) * JW + SB], blkbuf[:, (k % NF) * SB:(k % NF + 1) * SB], nodef[:, k:k + 1], None,
                                        ALU.is_le, ALU.add, accum_out=fine[:, k:k + 1]).then_inc(S("a_fine"), 1)
                    dve.wait_ge(S("a_fine"), NP)
                    V.scalar_tensor_tensor(endf[:, :], tn[:, 0:NP], float(SB), fine[:, :], ALU.mult, ALU.add).then_inc(S("a_endf"), 1)
                    dve.wait_ge(S("a_endf"), 1)
                    dve.wait_ge(S("a_start"), 16)
                    step(V.tensor_tensor(empty[:, :], endf[:, :], startf[:, :], ALU.is_equal))
                    V.scalar_tensor_tensor(first_i[:, :], empty[:, :], float(E), startf[:, :], ALU.mult, ALU.add).then_inc(S("a_idx"), 1)
                    step(V.tensor_scalar(tn[:, 0:NP], endf[:, :], -1.0, float(ZROW + 1), ALU.mult, ALU.add))
                    step(V.tensor_tensor(tn[:, NP:2 * NP], tn[:, 0:NP], empty[:, :], ALU.mult))
                    step(V.scalar_tensor_tensor(last_i[:, :], endf[:, :], -1.0, tn[:, NP:2 * NP], ALU.add, ALU.add))

                    dve.wait_ge(S("a_w"), 32)
                    dve.wait_ge(S("a_head"), 1)
                    w2v = w2s[:, :].rearrange("j (i u w) -> j i w u", i=7, w=MO)
                    w2o = w2x[:, :].rearrange("j (o w f) -> j o w f", o=6, f=KF)
                    wrv = wr[:, :].rearrange("j (w u) -> j w u", w=MO)
                    step(V.tensor_scalar(wrv, w2v[:, 6], -KV * C121 / 3.0, None, ALU.mult))
                    step(V.scalar_tensor_tensor(wrv, w2v[:, 5], KV * INV3, wrv, ALU.mult, ALU.add))
                    for o, f0, i, k in ((0, 0, 0, KS), (0, 16, 1, KS * INV3 * 3.0 ** 0.5), (1, 0, 2, KS),
                                        (1, 16, 3, KS * INV3 * 3.0 ** 0.5), (4, 0, 4, KV * INV3 * 3.0 ** 0.5), (4, 16, 6, KV * C121)):
                        V.tensor_scalar(w2o[:, o, :, f0:f0 + 16], w2v[:, i], k, None, ALU.mult).then_inc(S("a_w2x"), 1)
                    for o, f0 in ((2, 0), (3, 16), (5, 0)):
                        V.tensor_copy(w2o[:, o, :, f0:f0 + 16], wrv).then_inc(S("a_w2x"), 1)
                    dve.wait_ge(S("a_w2x"), 9)
                    V.tensor_copy(w2d[:, :].rearrange("j (o a f) -> j o a f", a=4, f=KF),
                                  w2x[:, :].rearrange("j (o a f) -> j o a f", a=1, f=KF).broadcast_to([HID, NOUT, 4, KF])).then_inc(S("a_w2d"), 1)
                    dve.wait_ge(S("a_vec"), 16)
                    step(V.tensor_tensor(sq[:, :], dirv[:, :], dirv[:, :], ALU.mult))
                    V.tensor_reduce(s2[:, :], sq[:, :].rearrange("p (c a) -> p c a", a=3), AX.X, ALU.add).then_inc(S("a_s2"), 1)
                    dve.wait_ge(S("a_sqrt"), 1)
                    step(V.reciprocal(rn[:, :], s2[:, :]))
                    V.tensor_tensor(dirv[:, :].rearrange("p (c a) -> p c a", a=3), dirv[:, :].rearrange("p (c a) -> p c a", a=3),
                                    rn[:, :].rearrange("p (c a) -> p c a", a=1).broadcast_to([P, EP, 3]), ALU.mult).then_inc(S("a_dir"), 1)
                    dve.wait_ge(S("a_wt"), 1)
                    wp = G_ps[0][:, 0:NOUT * HID]
                    step(V.tensor_copy(w_hi[:, :], wp))
                    dve.wait_ge(S("a_w1"), 16 * 8)
                    step(V.tensor_copy(w1_hi[:, :], w1x[:, :]))
                    step(V.tensor_scalar(wst[:, 512:1024].rearrange("p (a f) -> p a f", a=4),
                                         ident[:, :].rearrange("p (a f) -> p a f", a=1).broadcast_to([128, 4, 128]), 0.0, None, ALU.mult))
                    for q0 in (0, 64):
                        rows = slice(q0, q0 + 64)
                        halves = lambda a, c0, w: a[rows, c0:c0 + w].rearrange("p (w a j) -> p a w j", a=2, j=HJ)
                        for c0, w, o in ((0, 256, wst[rows, 0:256].rearrange("p (a w j) -> p a w j", a=2, j=HJ)),
                                         (256, 256, wst[rows, 256:512].rearrange("p (a w j) -> p a w j", a=2, j=HJ)),
                                         (512, 128, wst[rows, 512:1024].rearrange("p (a b w j) -> p a b w j", a=2, b=4, j=HJ)[:, :, 0]),
                                         (640, 128, wst[rows, 512:1024].rearrange("p (a b w j) -> p a b w j", a=2, b=4, j=HJ)[:, :, 3])):
                            if q0 == 0:
                                V.tensor_copy(o, halves(w_hi, c0, w))
                            else:
                                V.tensor_tensor(o, halves(wp, c0, w), halves(w_hi, c0, w).bitcast(f32), ALU.subtract)
                        if q0 == 0:
                            V.tensor_copy(wh[rows, :], w1_hi[rows, :])
                        else:
                            step(V.tensor_tensor(wh[rows, :], w1x[rows, :], w1_hi[rows, :].bitcast(f32), ALU.subtract))
                    dve.wait_ge(S("a_linkT"), 1)
                    V.tensor_copy(linkT[:, :], Y_ps[0:P, 0:P])
                    dve.wait_ge(S("a_endh"), 16)
                    step(V.tensor_scalar(t1[:, 0:1], partf[:, :], float(EP), float(EP), ALU.mult, ALU.add))
                    step(V.tensor_tensor(t1[:, 1:2], endh[:, :], t1[:, 0:1], ALU.is_le))
                    step(V.tensor_scalar(t1[:, 2:3], partf[:, :], float(E + 1), None, ALU.add))
                    step(V.tensor_tensor(t1[:, 0:1], endh[:, :], t1[:, 2:3], ALU.subtract))
                    step(V.tensor_tensor(t1[:, 0:1], t1[:, 0:1], t1[:, 1:2], ALU.mult))
                    step(V.scalar_tensor_tensor(fix_i[:, :], t1[:, 2:3], -1.0, t1[:, 0:1], ALU.add, ALU.add))

                @block.scalar
                def _(act):
                    act.wait_ge(S("a_s2"), 1)
                    nc.scalar.activation(s2[:, :], s2[:, :], ACT.Sqrt).then_inc(S("a_sqrt"), 1)

                @block.tensor
                def _(pe):
                    pe.wait_ge(S("a_id"), 2)
                    pe.wait_ge(S("a_ones"), 1)
                    pe.wait_ge(S("a_diag"), 1)
                    nc.tensor.matmul(R_ps[0:P, 0:P], ones[0:P, 0:P], diag[:, :], start=True, stop=True).then_inc(S("a_hrow"), 1)
                    pe.wait_ge(S("a_w2d"), 1)
                    for o in range(NOUT):
                        last = nc.tensor.transpose(G_ps[0][:, o * HID:(o + 1) * HID],
                                                   w2d[:, o * 4 * KF:(o + 1) * 4 * KF], ident[0:HID, 0:HID])
                    last.then_inc(S("a_wt"), 1)
                    pe.wait_ge(S("a_link"), 1)
                    nc.tensor.transpose(Y_ps[0:P, 0:P], link[:, :], ident[0:P, 0:P]).then_inc(S("a_linkT"), 1)

        with ExitStack() as st:
            def sbt(name, shape, dt=f32):
                return st.enter_context(nc.sbuf_tensor(name, shape, dt))

            def two(name, w, dt=f32):
                return [sbt(f"{name}_{h}", [P, w], dt) for h in range(2)]

            C1 = C + 1
            xv = two("xv", C * DIM)
            xt = sbt("xt", [P, DIM * C1])
            em = two("em", C * NEMB)
            dr = two("dr", C * 3)
            kp = two("kp", 8 * C1)
            drp = two("drp", C * 3)
            kpp = two("kpp", 8 * C1)
            nmp = two("nmp", C)
            F = two("F", C1 * FW)
            PCG = 2
            PCW = PCG * GT
            HL = [sbt(f"HL{h}", [P, PCW * 4 * FW], f32r) for h in range(2)]
            O = two("O", C1 * DIM)
            Z = two("Z", C1 * DIM)
            zr = sbt("zr", [P, C * DIM])
            tmp = sbt("tmp", [P, C * 48])
            FT = [sbt(f"FT{k}", [128, NT * GW], f32r) for k in range(2)]
            hid = [sbt(f"hid{k}", [128, 2 * GW]) for k in range(2)]
            prod_t = sbt("prod", [128, 3 * 2 * GW])
            prod = [prod_t[:, i * 2 * GW:(i + 1) * 2 * GW] for i in range(3)]
            sums2 = [sbt(f"sums{k}", [128, 3 * GW]) for k in range(2)]
            rt = [sbt(f"rt{k}", [NOUT, GW]) for k in range(2)]
            W2G = 2 * GT
            th = sbt("th", [P, W2G * 16])
            pa = sbt("pa", [P, W2G * 24])
            pb = sbt("pb", [P, W2G * 24])
            pg = sbt("pg", [P, W2G * MO])

            Fv = [a[:, :].rearrange("p (f c) -> p c f", c=C1)[:, 1:] for a in F]
            HLp = [a[:, :].rearrange("p (c t r s f) -> p c t r s f", t=NT, r=2, s=2, f=KF) for a in HL]
            HLv = [a[:, :].rearrange("p (ct r s f) -> p ct r s f", r=2, s=2, f=KF) for a in HL]

            tv = tmp[:, :].rearrange("p (c a u) -> p c a u", a=3, u=16)

            pav = pa[:, :].rearrange("p (c w a) -> p c w a", w=MO, a=3)
            pbv = pb[:, :].rearrange("p (c w a) -> p c w a", w=MO, a=3)
            pgv = pg[:, :].rearrange("p (c w) -> p c w", w=MO)

            def some(n):
                return not isinstance(n, int) or n > 0

            NPC = 4
            PCF = DIM // NPC
            assert PCF == MO
            SP = GC // PCG
            AHEAD = 4
            NG = PAIRS * G2
            NCH = 2 * PAIRS

            with nc.Block() as block:
                @block.sync
                def _(sp):
                    def hold(s, n):
                        sp.wait_ge(s, n)
                        sp.sem_inc(S("go_sp"), 1)

                    def load(ch, h, t):
                        if not isinstance(ch, int) or ch > 1:
                            hold(S("b_fa"), ch * 3 - 3)
                            sp.dma_start(idx[h][:, :], edges(src, 1)[:, bass.ds(ch * C, C)]).then_inc(S(f"b_idx{h}"), 16)
                        sp.dma_start(em[h][:, :], emb.rearrange("(p c) f -> p (c f)", c=EP)[:, bass.ds(ch * C * NEMB, C * NEMB)]).then_inc(S(f"b_ld{h}"), 16)
                        if not isinstance(ch, int) or ch > 1:
                            hold(S("b_d"), ch * 3 - 3)
                        sp.dma_start(xv[h][:, :], xd_d.rearrange("(p c) f -> p (c f)", c=EP)[:, bass.ds(ch * C * DIM, C * DIM)]).then_inc(S(f"b_ld{h}"), 16)
                        sp.dma_start(dr[h][:, :], dir_d.rearrange("(p c) f -> p (c f)", c=EP)[:, bass.ds(ch * C * 3, C * 3)]).then_inc(S(f"b_ld{h}"), 16)
                        sp.dma_start(kp[h][:, :].rearrange("p (a c) -> p a c", c=C1)[:, :, 1:],
                                     edges(keep_d, 1)[:, bass.ds(ch * C, C)].rearrange("p (a c) -> p a c", a=1).broadcast_to([P, 8, C])).then_inc(S(f"b_ld{h}"), 16)

                    def load_post(ch, h):
                        sp.dma_start(drp[h][:, :], dir_d.rearrange("(p c) f -> p (c f)", c=EP)[:, bass.ds(ch * C * 3, C * 3)]).then_inc(S(f"b_lp{h}"), 16)
                        sp.dma_start(kpp[h][:, :].rearrange("p (a c) -> p a c", c=C1)[:, :, 1:],
                                     edges(keep_d, 1)[:, bass.ds(ch * C, C)].rearrange("p (a c) -> p a c", a=1).broadcast_to([P, 8, C])).then_inc(S(f"b_lp{h}"), 16)
                        sp.dma_start(nmp[h][:, :], edges(weight, 1)[:, bass.ds(ch * C, C)]).then_inc(S(f"b_lp{h}"), 16)

                    def store(ch, h, t):
                        hold(S("b_zr"), ch + 1)
                        sp.dma_start(y0_d[0:E, :].rearrange("(p c) f -> p (c f)", c=EP)[:, bass.ds(ch * C * DIM, C * DIM)], zr[:, :]).then_inc(S("b_st"), 16)

                    def turn(t, first=False, last=False):
                        for h in range(2):
                            if not last:
                                load(t * 2 + h + 2, h, t + 1)
                            if not first:
                                hold(S(f"b_z{h}"), t * NPC)
                                load_post(t * 2 + h, h)
                                store(t * 2 + h - 2, h, t - 1)

                    for h in range(2):
                        load(h, h, 0)
                        load_post(h, h)
                    turn(0, first=True)
                    with sp.Fori(1, PAIRS - 1) as t:
                        turn(t)
                    turn(PAIRS - 1, last=True)
                    for h in range(2):
                        store(2 * PAIRS - 2 + h, h, PAIRS - 1)
                    sp.wait_ge(S("b_st"), 16 * NCH)

                @block.gpsimd
                def _(pool):
                    def gather(c0, n, h, t):
                        if c0 == 0:
                            pool.wait_ge(S(f"b_idx{h}"), t * 16 + 16)
                            pool.sem_inc(S("go_pool"), 1)
                        for c in range(c0, c0 + n):
                            nc.gpsimd.indirect_dma_start(out=gx[h][:, c * DIM:(c + 1) * DIM], out_offset=None, in_=x,
                                                         in_offset=bass.IndirectOffsetOnAxis(idx[h][:, c:c + 1], 0)).then_inc(S(f"b_gx{h}"), 16)

                    def add(n, k):
                        pool.wait_ge(S("b_mul"), n * 3 + 1)
                        if not isinstance(n, int) or n > 1:
                            pool.wait_ge(S("b_R"), n - 1)
                        nc.gpsimd.tensor_tensor(sums2[k][:, 0:GW], prod[0][:, 0:GW], prod[0][:, GW:2 * GW], ALU.add).then_inc(S("b_addp"), 1)

                    def along(ch, h):
                        for i in (1, 2):
                            pool.wait_ge(S("b_d"), ch * 3 + i)
                            first = tv[:, :, 0] if i == 1 else Fv[h][:, :, 16:32]
                            nc.gpsimd.tensor_tensor(Fv[h][:, :, 16:32], first, tv[:, :, i], ALU.add).then_inc(S("b_d"), 1)

                    def gates(m, h, q):
                        pool.wait_ge(S("b_yr"), m * 2 + 2)
                        pool.wait_ge(S("b_gs"), m * 2 + 2)
                        c0 = q * W2G
                        ov = O[h][:, :].rearrange("p (f c) -> p c f", c=C1)[:, 1 + c0:1 + c0 + W2G, :]
                        nc.gpsimd.tensor_tensor(ov[:, :, 8:32].rearrange("p c (w a) -> p c w a", a=3), pbv,
                                                pgv.rearrange("p c (w a) -> p c w a", a=1).broadcast_to([P, W2G, MO, 3]), ALU.mult).then_inc(S("b_o"), 1)

                    def turn(t, first=False, last=False):
                        for g in range(G2):
                            add(t * G2 + g, g % 2)
                            if g % GC == 5 and not (last and g > GC):
                                along(t * 2 + g // GC + 1, 1 - g // GC)
                            if not last:
                                gather(g % GC * GT, GT, g // GC, t + 1)
                            if g % 2 == 0 and not (first and g < 4):
                                pq = (g - 4) // 2 % GC
                                gates(t * GC + (g - 4) // 2, pq // (GC // 2), pq % (GC // 2))

                    along(0, 0)
                    gather(EARLY - C, 2 * C - EARLY, 1, 0)
                    turn(0, first=True)
                    with pool.Fori(1, PAIRS - 1) as t:
                        turn(t)
                    turn(PAIRS - 1, last=True)
                    for m in (NG // 2 - 2, NG // 2 - 1):
                        gates(m, 1, m % (GC // 2))

                @block.scalar
                def _(act):
                    A = nc.scalar
                    HSCALE = (2.0 / NEMB) ** 0.5

                    def spread(ch, h, t):
                        act.wait_ge(S(f"b_ld{h}"), t * 64 + 64)
                        if some(ch):
                            act.wait_ge(S("b_fs"), ch * NPC)
                        xvv = xv[h][:, :].rearrange("p (c f) -> p f c", f=DIM)
                        xtv = xt[:, :].rearrange("p (f c) -> p f c", c=C1)[:, :, 1:]
                        A.activation(xtv[:, 0:8], xvv[:, 0:8], ACT.Copy).then_inc(S("b_sp"), 1)
                        A.activation(xtv[:, 8:DIM].rearrange("p (a u) c -> p a u c", a=3), xvv[:, 8:DIM].rearrange("p (u a) c -> p a u c", a=3), ACT.Copy).then_inc(S("b_sp"), 1)

                    def gather_sums(ch, h, t):
                        act.wait_ge(S(f"b_z{h}"), t * NPC + NPC)
                        if some(ch):
                            act.wait_ge(S("b_st"), ch * 16)
                        A.activation(zr[:, :].rearrange("p (c f) -> p c f", f=DIM), Z[h][:, :].rearrange("p (f c) -> p c f", c=C1)[:, 1:], ACT.Copy).then_inc(S("b_zr"), 1)

                    def copy_rows(i, ch, h, t):
                        g = gx[h][:, :].rearrange("p (c f) -> p c f", f=DIM)
                        if i == 0:
                            act.wait_ge(S(f"b_gx{h}"), t * 16 * C + 16 * C)
                            if not isinstance(ch, int) or ch > 1:
                                act.wait_ge(S("b_lo"), ch * SP - SP)
                            A.activation(Fv[h][:, :, 0:8], g[:, :, 0:8], ACT.Copy).then_inc(S("b_fa"), 1)
                        if i == 1:
                            A.activation(Fv[h][:, :, 32:80].rearrange("p c (a u) -> p c a u", a=3)[:, :, :, 0:8],
                                         g[:, :, 8:32].rearrange("p c (u a) -> p c a u", a=3), ACT.Copy).then_inc(S("b_fa"), 1)
                        if i == 2:
                            act.wait_ge(S(f"b_ld{h}"), t * 64 + 64)
                            A.activation(Fv[h][:, :, QF:FD], em[h][:, :].rearrange("p (c f) -> p c f", f=NEMB), ACT.Copy).then_inc(S("b_fa"), 1)

                    def high(pc, q, ch, h, r):
                        if q == 0 and r == 0:
                            act.wait_ge(S("b_d"), ch * 3 + 3)
                            act.wait_ge(S("b_fa"), ch * 3 + 3)
                        if r == 0 and (not isinstance(pc, int) or pc > 1):
                            act.wait_ge(S("b_T"), (pc * PCG - PCG) * NT)
                        A.activation(HLp[(h * SP + q) % 2][:, :, :, r, 0, :], Fv[h][:, q * PCW:(q + 1) * PCW].rearrange("p c (t f) -> p c t f", f=KF),
                                     ACT.Copy).then_inc(S("b_hi"), 1)

                    def low_again(pc, q, h):
                        act.wait_ge(S("b_lo"), pc + 1)
                        v = HLv[(h * SP + q) % 2]
                        A.activation(v[:, :, 1, 1, :], v[:, :, 0, 1, :].bitcast(f32), ACT.Copy).then_inc(S("b_lo2"), 1)

                    def out_of_T(n, k, i):
                        act.wait_ge(S("b_T"), n * NT + i + 1)
                        if i == 0 and (not isinstance(n, int) or n > 1):
                            act.wait_ge(S("b_G"), n * 3 - 3)
                        A.activation(FT[k][:, i * GW:(i + 1) * GW], T_ps[:, 0:GW], ACT.Copy).then_inc(S("b_FT"), 1)

                    def relu(n, k, i):
                        act.wait_ge(S("b_H"), n * 2 + i + 1)
                        if i == 0 and (not isinstance(n, int) or n > 1):
                            act.wait_ge(S("b_mul"), n * 3 - 3)
                        A.activation(hid[k][:, i * GW:(i + 1) * GW], H_ps[:, 0:GW], ACT.Relu, scale=HSCALE).then_inc(S("b_hid"), 1)

                    def out_of_R(n, k):
                        act.wait_ge(S("b_R"), n + 1)
                        if not isinstance(n, int) or n > 1:
                            act.wait_ge(S("b_Y"), n - 1)
                        A.activation(rt[k][:, :], R_ps[0:NOUT, 0:GW], ACT.Copy).then_inc(S("b_rt"), 1)

                    def tanh(m):
                        act.wait_ge(S("b_Y"), m * 2 + 2)
                        if some(m):
                            act.wait_ge(S("b_gs"), m * 2)
                        A.activation(th[:, :].rearrange("p (c f) -> p c f", f=16),
                                     Y_ps[0:P, 0:W2G * NOUT].rearrange("p (c f) -> p c f", f=NOUT)[:, :, 0:16], ACT.Tanh).then_inc(S("b_th"), 1)

                    def turn(t, first=False, last=False):
                        for g in range(G2):
                            n, k, gc, h = t * G2 + g, g % 2, g % GC, g // GC
                            more1 = not (last and g == G2 - 1)
                            more2 = not (last and g >= G2 - 2)
                            if g % 2 == 0 and not (first and g < 4):
                                tanh(t * GC + (g - 4) // 2)
                            pt = (g + AHEAD) // PCG
                            split, sh, sq = t * 2 * SP + pt, pt // SP % 2, pt % SP
                            if more1:
                                relu(n + 1, 1 - k, 0)
                            if g % 2 == 0 and not (last and g + AHEAD >= G2):
                                high(split, sq, t * 2 + pt // SP, sh, 0)
                            if more2:
                                out_of_T(n + 2, k, 0)
                            if g % 2 == 0 and not (last and g + AHEAD >= G2):
                                high(split, sq, t * 2 + pt // SP, sh, 1)
                            if more1:
                                relu(n + 1, 1 - k, 1)
                            if more2:
                                out_of_T(n + 2, k, 1)
                            if g % 2 == 1 and not (last and g - 1 + AHEAD >= G2):
                                low_again(split, sq, sh)
                            if more2:
                                out_of_T(n + 2, k, 2)
                            if not (first and g == 0):
                                out_of_R(n - 1, 1 - k)
                            if gc == 0:
                                if not (last and h == 1):
                                    spread(t * 2 + h + 1, 1 - h, t + h)
                                if not first:
                                    gather_sums(t * 2 + h - 2, h, t - 1)
                            if not (last and h == 1) and 0 < gc < 4:
                                copy_rows(gc - 1, t * 2 + h + 1, 1 - h, t + h)

                    act.wait_ge(S("b_init"), 9)
                    spread(0, 0, 0)
                    for i in range(3):
                        copy_rows(i, 0, 0, 0)
                    for i in range(2):
                        high(i, i, 0, 0, 0)
                        high(i, i, 0, 0, 1)
                        low_again(i, i, 0)
                    for n in range(2):
                        for i in range(NT):
                            out_of_T(n, n, i)
                    for i in range(2):
                        relu(0, 0, i)
                    turn(0, first=True)
                    with act.Fori(1, PAIRS - 1) as t:
                        turn(t)
                    turn(PAIRS - 1, last=True)
                    tanh(NG // 2 - 2)
                    out_of_R(NG - 1, 1)
                    tanh(NG // 2 - 1)
                    for h in range(2):
                        gather_sums(NCH - 2 + h, h, PAIRS - 1)

                @block.tensor
                def _(pe):
                    Tn = nc.tensor

                    def transposes(n, g, pc, i):
                        if i == 0 and g % PCG == 0:
                            pe.wait_ge(S("b_lo2"), pc + 1)
                        if some(n) or i > 0:
                            pe.wait_ge(S("b_FT"), n * NT + i)
                        for c in range(GT):
                            col0 = ((g % PCG * GT + c) * NT + i) * 128
                            last = Tn.transpose(T_ps[:, c * P:(c + 1) * P], HL[g // PCG % 2][:, col0:col0 + 128].bitcast(f32), ident[0:P, 0:P])
                        last.then_inc(S("b_T"), 1)

                    def hidden(n, k, i):
                        pe.wait_ge(S("b_FT"), n * NT + NT)
                        if some(n) or i > 0:
                            pe.wait_ge(S("b_hid"), n * 2 + i)
                        Tn.matmul(H_ps[:, 0:GW], wh[:, i * 128:(i + 1) * 128], FT[k][:, 2 * GW:3 * GW], start=True, stop=True).then_inc(S("b_H"), 1)

                    def product(n, k, i):
                        pe.wait_ge(S("b_FT"), n * NT + (1, 2, 3)[i])
                        if not isinstance(n, int) or 3 * n + i > 1:
                            pe.wait_ge(S("b_mul"), n * 3 + i - 1)
                        q = G_ps[(k * 3 + i) % 2]
                        for j in range(2):
                            w0, g0 = (2 * i + j) * 128, j * 512
                            if i < 2:
                                last = Tn.matmul(q[:, g0:g0 + GW], wst[:, w0:w0 + 128], FT[k][:, i * GW:(i + 1) * GW], start=True, stop=True)
                            else:
                                w0 = (4 + 2 * j) * 128
                                Tn.matmul(q[:, g0:g0 + GW], wst[:, w0:w0 + 128], FT[k][:, 0:GW], start=True, stop=False)
                                last = Tn.matmul(q[:, g0:g0 + GW], wst[:, w0 + 128:w0 + 256], FT[k][:, 2 * GW:3 * GW], start=False, stop=True)
                        last.then_inc(S("b_G"), 1)

                    def reduce(n, k, i):
                        if i == 0:
                            pe.wait_ge(S("b_addp"), n + 1)
                            if some(n):
                                pe.wait_ge(S("b_rt"), n)
                        else:
                            pe.wait_ge(S("b_add"), n + 1)
                        last = Tn.matmul(R_ps[0:NOUT, 0:GW], red[:, i * NOUT:(i + 1) * NOUT], sums2[k][:, i * GW:(i + 1) * GW], start=(i == 0), stop=(i == 2))
                        if i == 2:
                            last.then_inc(S("b_R"), 1)

                    def back(n, k):
                        pe.wait_ge(S("b_rt"), n + 1)
                        if k == 0 and some(n):
                            pe.wait_ge(S("b_yr"), n)
                        pe.sem_inc(S("go_pe"), 1)
                        for c in range(GT):
                            last = Tn.transpose(Y_ps[0:P, (k * GT + c) * NOUT:(k * GT + c + 1) * NOUT], rt[k][:, c * P:(c + 1) * P], ident[0:NOUT, 0:NOUT])
                        last.then_inc(S("b_Y"), 1)

                    def turn(t, first=False, last=False):
                        for g in range(G2):
                            n, k = t * G2 + g, g % 2
                            before = not (first and g == 0)
                            more1 = not (last and g == G2 - 1)
                            more2 = not (last and g >= G2 - 2)
                            g2, pc2 = (g + 2) % G2, t * 2 * SP + (g + 2) // PCG
                            if more1:
                                hidden(n + 1, 1 - k, 0)
                            if more2:
                                transposes(n + 2, g2, pc2, 0)
                            product(n, k, 2)
                            if before:
                                reduce(n - 1, 1 - k, 0)
                            if more1:
                                hidden(n + 1, 1 - k, 1)
                            if more2:
                                transposes(n + 2, g2, pc2, 1)
                            if before:
                                reduce(n - 1, 1 - k, 1)
                            if more1:
                                product(n + 1, 1 - k, 0)
                            if more2:
                                transposes(n + 2, g2, pc2, 2)
                            if before:
                                reduce(n - 1, 1 - k, 2)
                            if more1:
                                product(n + 1, 1 - k, 1)
                            if not (first and g < 2):
                                back(n - 2, k)

                    for n in range(2):
                        for i in range(NT):
                            transposes(n, n, 0, i)
                    for i in range(2):
                        hidden(0, 0, i)
                    for i in range(2):
                        product(0, 0, i)
                    turn(0, first=True)
                    with pe.Fori(1, PAIRS - 1) as t:
                        turn(t)
                    turn(PAIRS - 1, last=True)
                    back(NG - 2, 0)
                    for i in range(3):
                        reduce(NG - 1, 1, i)
                    back(NG - 1, 1)

                @block.vector
                def _(dve):
                    V = nc.vector

                    def carry_x(ch, h):
                        if some(ch):
                            dve.wait_ge(S("b_fs"), ch * NPC)
                        a = xt[:, :].rearrange("p (f c) -> p f c", c=C1)[:, :, 0]
                        V.tensor_copy(a[:, 0:8], Fv[1 - h][:, C - 1, 8:16]).then_inc(S("b_cx"), 1)
                        V.tensor_copy(a[:, 8:DIM].rearrange("p (a u) -> p a u", a=3),
                                      Fv[1 - h][:, C - 1, 32:80].rearrange("p (a u) -> p a u", a=3)[:, :, 8:16]).then_inc(S("b_cx"), 1)

                    def fill(i, ch, h, t):
                        if i == 0:
                            dve.wait_ge(S(f"b_ld{h}"), t * 64 + 64)
                            dve.wait_ge(S("b_sp"), ch * 2 + 2)
                            dve.wait_ge(S("b_cx"), ch * 2 + 2)
                            if not isinstance(ch, int) or ch > 1:
                                dve.wait_ge(S("b_lo"), ch * SP - SP)
                                dve.wait_ge(S("b_hi"), ch * 2 * SP - 2 * SP)
                        f0 = 8 if i == 0 else 32 + 16 * (i - 1) + 8
                        V.tensor_tensor_scan(out=F[h][:, f0 * C1:(f0 + 8) * C1], data0=kp[h][:, :], data1=xt[:, i * 8 * C1:(i + 1) * 8 * C1],
                                             initial=0.0, op0=ALU.mult, op1=ALU.add).then_inc(S("b_fs"), 1)

                    def along(ch, h):
                        dve.wait_ge(S("b_fs"), ch * NPC + NPC)
                        dve.wait_ge(S("b_fa"), ch * 3 + 2)
                        if some(ch):
                            dve.wait_ge(S("b_d"), ch * 3)
                        V.tensor_tensor(tv, Fv[h][:, :, 32:80].rearrange("p c (a u) -> p c a u", a=3),
                                        dr[h][:, :].rearrange("p (c a u) -> p c a u", a=3, u=1).broadcast_to([P, C, 3, 16]), ALU.mult).then_inc(S("b_d"), 1)

                    def low(pc, q, h):
                        dve.wait_ge(S("b_hi"), pc * 2 + 2)
                        v = HLp[(h * SP + q) % 2]
                        V.tensor_tensor(v[:, :, :, 0, 1, :], Fv[h][:, q * PCW:(q + 1) * PCW].rearrange("p c (t f) -> p c t f", f=KF),
                                        v[:, :, :, 0, 0, :].bitcast(f32), ALU.subtract).then_inc(S("b_lo"), 1)

                    def multiply(n, k, i):
                        if i == 0:
                            dve.wait_ge(S("b_hid"), n * 2 + 2)
                        dve.wait_ge(S("b_G"), n * 3 + i + 1)
                        if some(n):
                            if i == 0:
                                dve.wait_ge(S("b_addp"), n)
                            else:
                                dve.wait_ge(S("b_add"), n)
                        gv = G_ps[(k * 3 + i) % 2][:, :].rearrange("p (a e) -> p a e", a=2)[:, :, 0:GW]
                        V.tensor_tensor(prod[i][:, :].rearrange("p (a e) -> p a e", a=2), gv, hid[k][:, :].rearrange("p (a e) -> p a e", a=2), ALU.mult).then_inc(S("b_mul"), 1)

                    def add(n, k):
                        dve.wait_ge(S("b_mul"), n * 3 + 3)
                        if not isinstance(n, int) or n > 1:
                            dve.wait_ge(S("b_R"), n - 1)
                        q = prod_t[:, 2 * GW:].rearrange("p (i a e) -> p i a e", i=2, a=2)
                        V.tensor_tensor(sums2[k][:, GW:3 * GW].rearrange("p (i e) -> p i e", i=2), q[:, :, 0], q[:, :, 1], ALU.add).then_inc(S("b_add"), 1)

                    yv = Y_ps[0:P, 0:W2G * NOUT].rearrange("p (c f) -> p c f", f=NOUT)
                    thv = th[:, :].rearrange("p (c f) -> p c f", f=16)

                    def post(i, m, h, q, t):
                        c0 = q * W2G
                        nrm = nmp[h][:, c0:c0 + W2G].rearrange("p (c w) -> p c w", w=1).broadcast_to([P, W2G, MO])
                        ov = O[h][:, :].rearrange("p (f c) -> p c f", c=C1)[:, 1 + c0:1 + c0 + W2G, :]
                        if i == 0:
                            if q == 0:
                                dve.wait_ge(S(f"b_lp{h}"), t * 48 + 48)
                            dve.wait_ge(S("b_Y"), m * 2 + 2)
                            dve.wait_ge(S("b_th"), m + 1)
                            if some(m):
                                dve.wait_ge(S("b_o"), m)
                            V.tensor_tensor(pav, yv[:, :, 16:24].rearrange("p c (w a) -> p c w a", a=1).broadcast_to([P, W2G, MO, 3]),
                                            drp[h][:, c0 * 3:(c0 + W2G) * 3].rearrange("p (c w a) -> p c w a", w=1, a=3).broadcast_to([P, W2G, MO, 3]),
                                            ALU.mult).then_inc(S("b_pa"), 1)
                            V.scalar_tensor_tensor(pgv, thv[:, :, 8:16], TG, nrm, ALU.mult, ALU.mult).then_inc(S("b_gs"), 1)
                            V.scalar_tensor_tensor(ov[:, :, 0:8], thv[:, :, 0:8], TG, nrm, ALU.mult, ALU.mult).then_inc(S("b_gs"), 1)
                        if i == 1:
                            dve.wait_ge(S("b_pa"), m + 1)
                            V.tensor_tensor(pbv, pav, yv[:, :, 24:48].rearrange("p c (a w) -> p c w a", a=3), ALU.add).then_inc(S("b_yr"), 2)

                    def carry_sums(ch, h, t):
                        if not isinstance(t, int) or t + h > 0:
                            dve.wait_ge(S(f"b_z{1 - h}"), (t + h) * NPC)
                        V.tensor_copy(O[h][:, :].rearrange("p (f c) -> p f c", c=C1)[:, :, 0], Z[1 - h][:, :].rearrange("p (f c) -> p f c", c=C1)[:, :, C]).then_inc(S("b_cs"), 1)

                    def sums(i, ch, h, t):
                        if i == 0:
                            dve.wait_ge(S("b_cs"), ch + 1)
                            dve.wait_ge(S("b_o"), ch * (GC // 2) + GC // 2)
                            if not isinstance(ch, int) or ch > 1:
                                dve.wait_ge(S("b_zr"), ch - 1)
                        part = slice(i * PCF * C1, (i + 1) * PCF * C1)
                        V.tensor_tensor_scan(out=Z[h][:, part], data0=kpp[h][:, :], data1=O[h][:, part],
                                             initial=0.0, op0=ALU.mult, op1=ALU.add).then_inc(S(f"b_z{h}"), 1)

                    def turn(t, first=False, last=False):
                        for g in range(G2):
                            n, k, gc, h = t * G2 + g, g % 2, g % GC, g // GC
                            feat = not (last and h == 1)
                            nxt = (t * 2 + h + 1, 1 - h, t + h)
                            prv = (t * 2 + h - 1, 1 - h, t - 1 + h)
                            with_post = g % 2 == 0 and not (first and g < 4)
                            pm = t * GC + (g - 4) // 2
                            pq = (g - 4) // 2 % GC
                            ph, pt = pq // (GC // 2), t - 1 if g < 4 else t
                            pq %= GC // 2
                            multiply(n, k, 0)
                            multiply(n, k, 1)
                            if with_post:
                                post(0, pm, ph, pq, pt)
                            multiply(n, k, 2)
                            if with_post:
                                post(1, pm, ph, pq, pt)
                            add(n, k)
                            if feat:
                                if gc == 0:
                                    carry_x(nxt[0], nxt[1])
                                elif gc in (1, 3):
                                    fill(gc - 1, *nxt)
                                    fill(gc, *nxt)
                                elif gc == 4:
                                    along(nxt[0], nxt[1])
                            if g % 2 == 0 and not (last and g + AHEAD >= G2):
                                split = (g + AHEAD) // PCG
                                low(t * 2 * SP + split, split % SP, split // SP % 2)
                            if not (first and h == 0):
                                if gc == 2:
                                    carry_sums(*prv)
                                if gc in (7, 9):
                                    sums(gc - 7, *prv)
                                    sums(gc - 6, *prv)

                    hv = hx_keep[:, :]
                    V.tensor_copy(Fv[1][:, C - 1, 8:16], hv[:, 0:8]).then_inc(S("b_init"), 1)
                    V.tensor_copy(Fv[1][:, C - 1, 32:80].rearrange("p (a u) -> p a u", a=3)[:, :, 8:16],
                                  hv[:, 8:32].rearrange("p (u a) -> p a u", a=3)).then_inc(S("b_init"), 1)
                    for h in range(2):
                        V.memset(kp[h][:, :].rearrange("p (a c) -> p a c", c=C1)[:, :, 0:1], 0.0).then_inc(S("b_init"), 1)
                        V.memset(kpp[h][:, :].rearrange("p (a c) -> p a c", c=C1)[:, :, 0:1], 0.0).then_inc(S("b_init"), 1)
                        V.memset(F[h][:, FD * C1:FW * C1], 0.0).then_inc(S("b_init"), 1)
                    V.memset(Z[1][:, :], 0.0).then_inc(S("b_init"), 1)
                    dve.wait_ge(S("b_init"), 9)
                    carry_x(0, 0)
                    for i in range(NPC):
                        fill(i, 0, 0, 0)
                    along(0, 0)
                    for i in range(2):
                        low(i, i, 0)
                    turn(0, first=True)
                    with dve.Fori(1, PAIRS - 1) as t:
                        turn(t)
                    turn(PAIRS - 1, last=True)
                    for m in (NG // 2 - 2, NG // 2 - 1):
                        for i in range(2):
                            post(i, m, 1, m % (GC // 2), PAIRS - 1)
                    carry_sums(NCH - 1, 1, PAIRS - 1)
                    for i in range(NPC):
                        sums(i, NCH - 1, 1, PAIRS - 1)
                    dve.wait_ge(S("b_z1"), PAIRS * NPC)
                    V.tensor_copy(hx_keep[:, :], Z[1][:, :].rearrange("p (f c) -> p f c", c=C1)[:, :, C]).then_inc(S("b_tail"), 1)
                    dve.wait_ge(S("b_tail"), 1)

        NPIECE = 4
        KP = NP // NPIECE
        assert KP * NPIECE == NP

        def piece_of(ap, i, width):
            return ap[:, i * KP * width:(i + 1) * KP * width].rearrange("p (k f) -> p k f", f=width)

        def layer_norm(dve, step, i, v, out_v, sq_t, st, key):
            V = nc.vector
            vv, oo, sq = piece_of(v, i, DIM), piece_of(out_v, i, DIM), piece_of(sq_t, i, DIM)
            mean, var, rs = [st[:, j * NP + i * KP:j * NP + (i + 1) * KP] for j in range(3)]
            bc = lambda a: a.rearrange("p (k f) -> p k f", f=1).broadcast_to([P, KP, DIM])
            step(V.tensor_reduce(mean, vv, AX.X, ALU.add))
            step(V.tensor_scalar(mean, mean, 1.0 / DIM, None, ALU.mult))
            step(V.tensor_tensor(vv, vv, bc(mean), ALU.subtract))
            step(V.tensor_tensor(sq, vv, vv, ALU.mult))
            step(V.tensor_reduce(var, sq, AX.X, ALU.add))
            V.tensor_scalar(var, var, 1.0 / DIM, EPS, ALU.mult, ALU.add).then_inc(S(key + "_var"), 1)
            dve.wait_ge(S(key + "_std"), i + 1)
            step(V.reciprocal(rs, rs))
            step(V.tensor_tensor(oo, vv, bc(rs), ALU.mult))

        with ExitStack() as st:
            def sbt(name, shape, dt=f32):
                return st.enter_context(nc.sbuf_tensor(name, shape, dt))

            fixr = sbt("fixr", [P, DIM])
            ng = sbt("ng", [P, NP * DIM])
            sqb = sbt("sqb", [P, NP * DIM])
            stt = sbt("stt", [P, 3 * NP])
            x1e = sbt("x1e", [P, NP * (DIM + 1)])
            sd = sbt("sd", [P, NP])

            with nc.Block() as block:
                @block.tensor
                def _(pe):
                    nc.tensor.matmul(R_ps[0:P, 0:DIM], link[:, :], hx_keep[:, :], start=True, stop=True).then_inc(S("c_carry"), 1)

                @block.gpsimd
                def _(pool):
                    nc.gpsimd.indirect_dma_start(out=fixr[:, :], out_offset=None, in_=y0_d,
                                                 in_offset=bass.IndirectOffsetOnAxis(fix_i[:, :], 0)).then_inc(S("c_fixr"), 16)
                    pool.wait_ge(S("c_fix"), 1)
                    nc.gpsimd.indirect_dma_start(out=y0_d, out_offset=bass.IndirectOffsetOnAxis(fix_i[:, :], 0),
                                                 in_=fixr[:, :], in_offset=None).then_inc(S("c_fixw"), 16)
                    pool.wait_ge(S("c_fixw"), 16)
                    for k in range(NP):
                        nc.gpsimd.indirect_dma_start(out=ng[:, k * DIM:(k + 1) * DIM], out_offset=None, in_=y0_d,
                                                     in_offset=bass.IndirectOffsetOnAxis(last_i[:, k:k + 1], 0)).then_inc(S(f"c_ng{k // KP}"), 16)
                    for k in range(NP):
                        if k % KP == 0:
                            pool.wait_ge(S("c_sd"), k // KP + 1)
                        nc.gpsimd.indirect_dma_start(out=sd_d, out_offset=bass.IndirectOffsetOnAxis(first_i[:, k:k + 1], 0),
                                                     in_=sd[:, k:k + 1], in_offset=None,
                                                     bounds_check=E - 1, oob_is_err=False).then_inc(S("c_sdw"), 16)
                    pool.wait_ge(S("c_sdt"), 16)
                    nc.gpsimd.indirect_dma_start(out=hsd[:, :], out_offset=None, in_=sdt_d,
                                                 in_offset=bass.IndirectOffsetOnAxis(head_i[:, :], 0)).then_inc(S("c_hsd"), 16)
                    pool.wait_ge(S("c_sdw"), 16 * NP)
                    pool.wait_ge(S("c_hsd"), 16)

                @block.vector
                def _(dve):
                    n = [0]

                    def step(ins):
                        n[0] += 1
                        ins.then_inc(S("c_dve"), 1)
                        dve.wait_ge(S("c_dve"), n[0])

                    V = nc.vector
                    dve.wait_ge(S("c_carry"), 1)
                    dve.wait_ge(S("c_fixr"), 16)
                    V.tensor_tensor(fixr[:, :], R_ps[0:P, 0:DIM], fixr[:, :], ALU.add).then_inc(S("c_fix"), 1)
                    for i in range(NPIECE):
                        dve.wait_ge(S(f"c_ng{i}"), 16 * KP)
                        step(V.tensor_tensor(piece_of(ng, i, DIM), piece_of(ng, i, DIM), piece_of(xn, i, DIM), ALU.add))
                        layer_norm(dve, step, i, ng, xn, sqb, stt, "c")
                        x1, x1v, sq = piece_of(xn, i, DIM), piece_of(x1e, i, DIM + 1), piece_of(sqb, i, DIM)
                        bc = lambda a: a.rearrange("p (k f) -> p k f", k=1).broadcast_to([P, KP, DIM])
                        V.tensor_copy(x1v[:, :, 0:DIM], x1)
                        step(V.tensor_tensor(sq, x1, bc(attn_b[:, DIM:2 * DIM]), ALU.mult))
                        V.tensor_reduce(sd[:, i * KP:(i + 1) * KP], sq, AX.X, ALU.add).then_inc(S("c_sd"), 1)
                        dve.wait_ge(S("c_sd"), i + 1)
                        step(V.tensor_tensor(sq, x1, bc(attn_b[:, 0:DIM]), ALU.mult))
                        V.tensor_reduce(x1v[:, :, DIM:DIM + 1], sq, AX.X, ALU.add).then_inc(S("c_x1e"), 1)

                @block.scalar
                def _(act):
                    for i in range(NPIECE):
                        act.wait_ge(S("c_var"), i + 1)
                        nc.scalar.activation(stt[:, 2 * NP + i * KP:2 * NP + (i + 1) * KP], stt[:, NP + i * KP:NP + (i + 1) * KP], ACT.Sqrt).then_inc(S("c_std"), 1)

                @block.sync
                def _(sp):
                    sp.wait_ge(S("c_sd"), NPIECE)
                    sp.dma_start(sdt_d.rearrange("(p k) a -> p (k a)", k=NP), sd[:, :]).then_inc(S("c_sdt"), 16)
                    sp.wait_ge(S("c_x1e"), NPIECE)
                    sp.dma_start(tab_d.rearrange("(p k) f -> p (k f)", k=NP), x1e[:, :]).then_inc(S("c_tab"), 16)
                    sp.wait_ge(S("c_tab"), 16)
                    sp.wait_ge(S("c_sdt"), 16)

        with ExitStack() as st:
            def sbt(name, shape, dt=f32):
                return st.enter_context(nc.sbuf_tensor(name, shape, dt))

            def two(name, w, dt=f32):
                return [sbt(f"{name}_{h}", [P, w], dt) for h in range(2)]

            T1 = DIM + 1
            idx = two("idxb", C, i32)
            gx = two("gxb", C * T1)
            sdr = two("sdr", C)
            kp = two("kpb", C)
            rst = sbt("rst", [P, C])
            sdf = two("sdf", C)
            ee = sbt("ee", [P, C])
            lk = sbt("lk", [P, C])
            mx = two("mx", C + 1)
            ex = sbt("ex", [P, 2 * C])
            dec = sbt("dec", [P, C])
            wx = sbt("wx", [P, C * DIM])
            Z = two("Zb", C * R1)

            with nc.Block() as block:
                @block.sync
                def _(sp):
                    def load(ch, h, t):
                        sp.wait_ge(S(f"d_gx{h}"), t * 16 * C)
                        sp.sem_inc(S("go_sp"), 1)
                        sp.wait_ge(S(f"d_wx{h}"), t)
                        sp.sem_inc(S("go_sp"), 1)
                        sp.dma_start(idx[h][:, :], edges(src, 1)[:, bass.ds(ch * C, C)]).then_inc(S(f"d_idx{h}"), 16)
                        sp.wait_ge(S(f"d_z{h}"), t)
                        sp.sem_inc(S("go_sp"), 1)
                        sp.wait_ge(S(f"d_st{h}"), t * 16)
                        sp.sem_inc(S("go_sp"), 1)
                        sp.dma_start(sdr[h][:, :], sd_d.rearrange("(p c) a -> p (c a)", c=EP)[:, bass.ds(ch * C, C)]).then_inc(S(f"d_ld{h}"), 16)
                        sp.dma_start(kp[h][:, :], edges(keep_d, 1)[:, bass.ds(ch * C, C)]).then_inc(S(f"d_ld{h}"), 16)

                    def store(ch, h, t):
                        sp.wait_ge(S(f"d_z{h}"), t + 1)
                        sp.wait_ge(S(f"d_zm{h}"), t + 1)
                        sp.dma_start(y1_d[0:E, :].rearrange("(p c) f -> p (c f)", c=EP)[:, bass.ds(ch * C * R1, C * R1)], Z[h][:, :]).then_inc(S(f"d_st{h}"), 16)

                    load(0, 0, 0)
                    load(1, 1, 0)
                    with sp.Fori(0, PAIRS - 1) as t:
                        for h in range(2):
                            store(t * 2 + h, h, t)
                            load(t * 2 + h + 2, h, t + 1)
                    for h in range(2):
                        store(2 * PAIRS - 2 + h, h, PAIRS - 1)
                    for h in range(2):
                        sp.wait_ge(S(f"d_st{h}"), 16 * PAIRS)

                @block.gpsimd
                def _(pool):
                    with pool.Fori(0, PAIRS) as t:
                        for h in range(2):
                            pool.wait_ge(S(f"d_idx{h}"), t * 16 + 16)
                            pool.sem_inc(S("go_pool"), 1)
                            for c in range(C):
                                nc.gpsimd.indirect_dma_start(out=gx[h][:, c * T1:(c + 1) * T1], out_offset=None, in_=tab_d,
                                                             in_offset=bass.IndirectOffsetOnAxis(idx[h][:, c:c + 1], 0)).then_inc(S(f"d_gx{h}"), 16)

                @block.scalar
                def _(act):
                    def chunk(h, t):
                        act.wait_ge(S("d_pre"), t * 2 + h + 1)
                        nc.scalar.activation(ex[:, :], ex[:, :], ACT.Exp).then_inc(S("d_exp"), 1)
                        nc.scalar.activation(Z[h][:, :].rearrange("p (c f) -> p c f", f=R1)[:, :, DIM + 1],
                                             mx[h][:, 1:C + 1], ACT.Copy).then_inc(S(f"d_zm{h}"), 1)

                    with act.Fori(0, PAIRS) as t:
                        for h in range(2):
                            chunk(h, t)

                @block.vector
                def _(dve):
                    V = nc.vector
                    STEPS = 6

                    def chunk(h, t):
                        n = [0]

                        def step(ins):
                            n[0] += 1
                            ins.then_inc(S("d_dve"), 1)
                            dve.wait_ge(S("d_dve"), t * 2 * STEPS + h * STEPS + n[0])

                        g = gx[h][:, :].rearrange("p (c f) -> p c f", f=T1)
                        dve.wait_ge(S(f"d_ld{h}"), t * 32 + 32)
                        V.tensor_scalar(rst[:, :], kp[h][:, :], -1.0, BIG, ALU.add, ALU.mult)
                        V.tensor_copy(mx[h][:, 0:1], mx[1 - h][:, C:C + 1])
                        step(V.tensor_tensor_scan(out=sdf[h][:, :], data0=kp[h][:, :], data1=sdr[h][:, :],
                                                  initial=sdf[1 - h][:, C - 1:C], op0=ALU.mult, op1=ALU.add))
                        dve.wait_ge(S(f"d_gx{h}"), t * 16 * C + 16 * C)
                        step(V.tensor_tensor(lk[:, :], sdf[h][:, :], g[:, :, DIM], ALU.add))
                        step(V.scalar_tensor_tensor(ee[:, :], lk[:, :], 0.01, lk[:, :], ALU.mult, ALU.max))
                        step(V.tensor_tensor_scan(out=mx[h][:, 1:C + 1], data0=rst[:, :], data1=ee[:, :],
                                                  initial=mx[1 - h][:, C:C + 1], op0=ALU.add, op1=ALU.max))
                        V.tensor_tensor(ex[:, 0:C], ee[:, :], mx[h][:, 1:C + 1], ALU.subtract)
                        step(V.tensor_tensor(ex[:, C:2 * C], mx[h][:, 0:C], mx[h][:, 1:C + 1], ALU.subtract))
                        V.memset(one[:, :], 0.0).then_inc(S("d_pre"), 1)
                        dve.wait_ge(S("d_exp"), t * 2 + h + 1)
                        V.scalar_tensor_tensor(dec[:, :], ex[:, C:2 * C], 1.0, kp[h][:, :], ALU.min, ALU.mult)
                        step(V.tensor_tensor(wx[:, :].rearrange("p (c f) -> p c f", f=DIM), g[:, :, 0:DIM],
                                             ex[:, 0:C].rearrange("p (c f) -> p c f", f=1).broadcast_to([P, C, DIM]), ALU.mult))
                        V.memset(one[:, :], 0.0).then_inc(S(f"d_wx{h}"), 1)
                        assert n[0] == STEPS
                        zv = Z[h][:, :].rearrange("p (c f) -> p c f", f=R1)
                        zp = Z[1 - h][:, :].rearrange("p (c f) -> p c f", f=R1)
                        V.tensor_tensor_scan(out=zv[:, :, DIM], data0=dec[:, :], data1=ex[:, 0:C], initial=zp[:, C - 1, DIM:DIM + 1],
                                             op0=ALU.mult, op1=ALU.add)
                        for f in range(DIM):
                            last = V.tensor_tensor_scan(out=zv[:, :, f], data0=dec[:, :],
                                                        data1=wx[:, :].rearrange("p (c f) -> p c f", f=DIM)[:, :, f],
                                                        initial=zp[:, C - 1, f:f + 1], op0=ALU.mult, op1=ALU.add)
                        last.then_inc(S(f"d_z{h}"), 1)
                        dve.wait_ge(S(f"d_z{h}"), t + 1)

                    one = sbt("one_d", [P, 1])
                    V.tensor_copy(sdf[1][:, C - 1:C], hsd[:, :]).then_inc(S("d_init"), 1)
                    V.memset(mx[1][:, C:C + 1], -BIG).then_inc(S("d_init"), 1)
                    V.memset(Z[1][:, :], 0.0).then_inc(S("d_init"), 1)
                    dve.wait_ge(S("d_init"), 3)
                    with dve.Fori(0, PAIRS) as t:
                        for h in range(2):
                            chunk(h, t)
                    dve.wait_ge(S("d_zm1"), PAIRS)
                    V.tensor_copy(tail1[:, :], Z[1][:, (C - 1) * R1:C * R1]).then_inc(S("d_tail"), 1)
                    dve.wait_ge(S("d_tail"), 1)

        with ExitStack() as st:
            def sbt(name, shape, dt=f32):
                return st.enter_context(nc.sbuf_tensor(name, shape, dt))

            fixr = sbt("fixr1", [P, R1])
            dm = sbt("dm", [P, P])
            am = sbt("am", [P, P])
            cw = sbt("cw", [P, P])
            sm = sbt("sm", [P, 8])
            ng = sbt("ng1", [P, NP * R1])
            hh = sbt("hh", [P, NP * DIM])
            sqb = sbt("sqb1", [P, NP * DIM])
            stt = sbt("stt1", [P, 3 * NP])

            with nc.Block() as block:
                @block.tensor
                def _(pe):
                    pe.wait_ge(S("e_dm"), 1)
                    nc.tensor.matmul(R_ps[0:P, 0:P], ones[0:P, 0:P], dm[:, :], start=True, stop=True).then_inc(S("e_mrow"), 1)
                    pe.wait_ge(S("e_dm"), 2)
                    nc.tensor.matmul(Y_ps[0:P, 0:P], ones[0:P, 0:P], dm[:, :], start=True, stop=True).then_inc(S("e_mrow"), 1)
                    pe.wait_ge(S("e_cw"), 1)
                    nc.tensor.matmul(T_ps[0:P, 0:DIM + 1], cw[:, :], tail1[:, 0:DIM + 1], start=True, stop=True).then_inc(S("e_carry"), 1)

                @block.gpsimd
                def _(pool):
                    nc.gpsimd.indirect_dma_start(out=fixr[:, :], out_offset=None, in_=y1_d,
                                                 in_offset=bass.IndirectOffsetOnAxis(fix_i[:, :], 0)).then_inc(S("e_fixr"), 16)
                    pool.wait_ge(S("e_fix"), 1)
                    nc.gpsimd.indirect_dma_start(out=y1_d, out_offset=bass.IndirectOffsetOnAxis(fix_i[:, :], 0),
                                                 in_=fixr[:, :], in_offset=None).then_inc(S("e_fixw"), 16)
                    pool.wait_ge(S("e_fixw"), 16)
                    for k in range(NP):
                        nc.gpsimd.indirect_dma_start(out=ng[:, k * R1:(k + 1) * R1], out_offset=None, in_=y1_d,
                                                     in_offset=bass.IndirectOffsetOnAxis(last_i[:, k:k + 1], 0)).then_inc(S(f"e_ng{k // KP}"), 16)

                @block.vector
                def _(dve):
                    n = [0]

                    def step(ins):
                        n[0] += 1
                        ins.then_inc(S("e_dve"), 1)
                        dve.wait_ge(S("e_dve"), n[0])

                    V = nc.vector
                    mt = tail1[:, DIM + 1:DIM + 2]
                    V.tensor_scalar(dm[:, :], ident[0:P, 0:P], mt, None, ALU.mult).then_inc(S("e_dm"), 1)
                    step(V.tensor_scalar(am[:, :], linkT[:, :], -1.0, BIG, ALU.add, ALU.mult))
                    dve.wait_ge(S("e_mrow"), 1)
                    step(V.tensor_tensor(cw[:, :], R_ps[0:P, 0:P], linkT[:, :], ALU.mult))
                    step(V.tensor_tensor(cw[:, :], cw[:, :], am[:, :], ALU.add))
                    step(V.tensor_reduce(sm[:, 0:1], cw[:, :], AX.X, ALU.max))
                    dve.wait_ge(S("e_fixr"), 16)
                    step(V.tensor_tensor(sm[:, 1:2], sm[:, 0:1], fixr[:, DIM + 1:DIM + 2], ALU.max))
                    V.tensor_scalar(dm[:, :], ident[0:P, 0:P], sm[:, 1:2], None, ALU.mult).then_inc(S("e_dm"), 1)
                    dve.wait_ge(S("e_mrow"), 2)
                    step(V.tensor_scalar(am[:, :], Y_ps[0:P, 0:P], mt, 0.0, ALU.subtract, ALU.max))
                    V.tensor_tensor(sm[:, 2:3], fixr[:, DIM + 1:DIM + 2], sm[:, 1:2], ALU.subtract).then_inc(S("e_am"), 1)
                    dve.wait_ge(S("e_exp"), 2)
                    V.tensor_tensor(cw[:, :], am[:, :], link[:, :], ALU.mult).then_inc(S("e_cw"), 1)
                    dve.wait_ge(S("e_carry"), 1)
                    V.scalar_tensor_tensor(fixr[:, 0:DIM + 1], fixr[:, 0:DIM + 1], sm[:, 3:4], T_ps[0:P, 0:DIM + 1],
                                           ALU.mult, ALU.add).then_inc(S("e_fix"), 1)
                    for i in range(NPIECE):
                        dve.wait_ge(S(f"e_ng{i}"), 16 * KP)
                        ngv, hv = piece_of(ng, i, R1), piece_of(hh, i, DIM)
                        total, inv = [stt[:, j * NP + i * KP:j * NP + (i + 1) * KP].rearrange("p (k f) -> p k f", f=1) for j in range(2)]
                        step(V.tensor_tensor(total, ngv[:, :, DIM:DIM + 1], piece_of(empty, i, 1), ALU.add))
                        step(V.reciprocal(inv, total))
                        step(V.tensor_tensor(hv, ngv[:, :, 0:DIM], inv.broadcast_to([P, KP, DIM]), ALU.mult))
                        step(V.tensor_tensor(hv, hv, piece_of(xn, i, DIM), ALU.add))
                        layer_norm(dve, step, i, hh, xn, sqb, stt, "e")
                        V.memset(sm[:, 4:5], 0.0).then_inc(S("e_done"), 1)

                @block.scalar
                def _(act):
                    act.wait_ge(S("e_am"), 1)
                    nc.scalar.activation(am[:, :], am[:, :], ACT.Exp, scale=-1.0).then_inc(S("e_exp"), 1)
                    nc.scalar.activation(sm[:, 3:4], sm[:, 2:3], ACT.Exp).then_inc(S("e_exp"), 1)
                    for i in range(NPIECE):
                        act.wait_ge(S("e_var"), i + 1)
                        nc.scalar.activation(stt[:, 2 * NP + i * KP:2 * NP + (i + 1) * KP], stt[:, NP + i * KP:NP + (i + 1) * KP], ACT.Sqrt).then_inc(S("e_std"), 1)

                @block.sync
                def _(sp):
                    for i in range(NPIECE):
                        sp.wait_ge(S("e_done"), i + 1)
                        part = slice(i * KP * DIM, (i + 1) * KP * DIM)
                        sp.dma_start(out.rearrange("(p k) f -> p (k f)", k=NP)[:, part], xn[:, part]).then_inc(S("e_out"), 16)
                    sp.wait_ge(S("e_out"), 16 * NPIECE)


_INS = ["x", "src", "dst", "edge_attr_10", "edge_attr_3", "edge_weight", "L0_gnn_W1", "L0_gnn_W2", "L1_gnn_attn_w"]


def kernel(**inputs):
    import numpy as _np
    import concourse.bacc as _bacc
    from concourse import mybir as _mybir
    from concourse.bass_utils import run_bass_kernel_spmd as _run

    nc = _bacc.Bacc("TRN2", target_bir_lowering=False, num_devices=1)
    arrays, args = {}, []
    for name in _INS:
        a = _np.ascontiguousarray(inputs[name])
        arrays[f"in_{name}"] = a
        args.append(nc.dram_tensor(f"in_{name}", a.shape, _mybir.dt.from_np(a.dtype), kind="ExternalInput").ap())
    shape = inputs["x"].shape
    args.append(nc.dram_tensor("out_0", shape, _mybir.dt.float32, kind="ExternalOutput").ap())
    gnn_resnorm_kernel(nc, *args)
    r = _run(nc, [arrays], core_ids=[0])
    return r.results[0]["out_0"]
```
